# Optimizing a Trainium2 kernel written in Bass

```python
import numpy as np
import jax
import jax.numpy as jnp

def _softmax(x, axis=-1):
    return jax.nn.softmax(x, axis=axis)

def _gelu(x):
    return jax.nn.gelu(x, approximate=True)

def _silu(x):
    return jax.nn.silu(x)

def _sigmoid(x):
    return jax.nn.sigmoid(x)

def _layernorm(x, axis=-1, eps=1e-05):
    m = jnp.mean(x, axis=axis, keepdims=True)
    v = jnp.var(x, axis=axis, keepdims=True)
    return (x - m) / jnp.sqrt(v + eps)

def _scatter_add(tgt, idx, src, axis=0):
    return tgt.at[idx].add(src)

def _segment_sum(src, seg, n):
    return jax.ops.segment_sum(src, seg, n)
kernel_name = 'mk_vit_tower_postln_d1_tok_img1024_r4_32d1c8'

def setup_inputs(seed: int=0):
    np.random.seed(seed)
    _w = jnp.asarray

    def _rec_inputs():
        import jax
        import jax.numpy as jnp
        _rk = jax.random.key(seed)
        x = -0.00016672 + 0.999947 * jax.random.normal(jax.random.fold_in(_rk, 1), (16, 3, 96, 96), jnp.float32)
        return x
    x = _rec_inputs()

    def _L0_tok_setup():
        import jax, jax.numpy as jnp
        import numpy as np
        PATCH = 16
        EPS = 1e-05

        def _patchify(img, p):
            B, C, H, W = img.shape
            h, w = (H // p, W // p)
            x = img.reshape(B, C, h, p, w, p)
            x = x.transpose(0, 2, 4, 1, 3, 5)
            return x.reshape(B, h, w, C * p * p)

        def _layernorm(x, gamma):
            mu = x.mean(axis=-1, keepdims=True)
            var = ((x - mu) ** 2).mean(axis=-1, keepdims=True)
            return (x - mu) * jax.lax.rsqrt(var + EPS) * gamma

        def _posemb_sincos_2d(h, w, dim, temperature=10000.0, dtype=jnp.float32):
            y, x = jnp.meshgrid(jnp.arange(h, dtype=dtype), jnp.arange(w, dtype=dtype), indexing='ij')
            omega = jnp.arange(dim // 4, dtype=dtype) / (dim // 4 - 1)
            omega = 1.0 / temperature ** omega
            y = y.reshape(-1)[:, None] * omega[None, :]
            x = x.reshape(-1)[:, None] * omega[None, :]
            return jnp.concatenate([jnp.sin(x), jnp.cos(x), jnp.sin(y), jnp.cos(y)], axis=1)
        key = jax.random.key(seed)
        k1, k2, k3, k4 = jax.random.split(key, 4)
        patch_dim = 3 * PATCH * PATCH
        dim = 256
        img = jax.random.normal(k1, (64, 3, 96, 96), dtype=jnp.float32)
        ln1_w = jax.random.uniform(k2, (patch_dim,), dtype=jnp.float32, minval=0.9, maxval=1.1)
        W = jax.random.normal(k3, (dim, patch_dim), dtype=jnp.float32) * 0.02
        ln2_w = jax.random.uniform(k4, (dim,), dtype=jnp.float32, minval=0.9, maxval=1.1)
        return {'img': img, 'ln1_w': ln1_w, 'W': W, 'ln2_w': ln2_w}
    _L0_tok_all = _L0_tok_setup()
    _L0_tok_in = {k: v for k, v in _L0_tok_all.items() if k in ('ln1_w', 'W', 'ln2_w')}
    del _L0_tok_all

    def _L0_attn_setup():
        import jax, jax.numpy as jnp
        import numpy as np
        import math
        NUM_HEADS = 8
        D_HEAD = 128
        DEPTH = 1
        LAMBDA_INIT = 0.8 - 0.6 * math.exp(-0.3 * DEPTH)
        EPS = 1e-05
        key = jax.random.key(seed)
        ks = jax.random.split(key, 10)
        B, N, D = (2, 512, 256)
        s = 0.02
        return {'X': jax.random.normal(ks[0], (B, N, D), jnp.float32), 'Wq': jax.random.normal(ks[1], (2 * D_HEAD * NUM_HEADS, D), jnp.float32) * s, 'Wk': jax.random.normal(ks[2], (2 * D_HEAD * NUM_HEADS, D), jnp.float32) * s, 'Wv': jax.random.normal(ks[3], (2 * D_HEAD * NUM_HEADS, D), jnp.float32) * s, 'Wo': jax.random.normal(ks[4], (D, 2 * D_HEAD * NUM_HEADS), jnp.float32) * s, 'lambda_q1': jax.random.normal(ks[5], (NUM_HEADS, D_HEAD), jnp.float32) * 0.1, 'lambda_k1': jax.random.normal(ks[6], (NUM_HEADS, D_HEAD), jnp.float32) * 0.1, 'lambda_q2': jax.random.normal(ks[7], (NUM_HEADS, D_HEAD), jnp.float32) * 0.1, 'lambda_k2': jax.random.normal(ks[8], (NUM_HEADS, D_HEAD), jnp.float32) * 0.1, 'rms_scale': jnp.ones((2 * D_HEAD,), jnp.float32)}
    _L0_attn_all = _L0_attn_setup()
    _L0_attn_in = {k: v for k, v in _L0_attn_all.items() if k in ('Wq', 'Wk', 'Wv', 'Wo', 'lambda_q1', 'lambda_k1', 'lambda_q2', 'lambda_k2', 'rms_scale')}
    del _L0_attn_all

    def _L0_ffn_setup():
        import jax, jax.numpy as jnp
        import numpy as np
        B, T, C = (4, 512, 256)
        E = 8
        K = 2
        H = 352
        HS = 352 * 2
        key = jax.random.key(seed)
        k = jax.random.split(key, 8)
        s = 0.02
        return {'x': jax.random.normal(k[0], (B, T, C), jnp.float32), 'Wg': jax.random.normal(k[1], (C, E), jnp.float32) * s, 'W1': jax.random.normal(k[2], (E, C, H), jnp.float32) * s, 'W2': jax.random.normal(k[3], (E, C, H), jnp.float32) * s, 'W3': jax.random.normal(k[4], (E, H, C), jnp.float32) * s, 'Ws1': jax.random.normal(k[5], (C, HS), jnp.float32) * s, 'Ws2': jax.random.normal(k[6], (C, HS), jnp.float32) * s, 'Ws3': jax.random.normal(k[7], (HS, C), jnp.float32) * s}
    _L0_ffn_all = _L0_ffn_setup()
    _L0_ffn_in = {k: v for k, v in _L0_ffn_all.items() if k in ('Wg', 'W1', 'W2', 'W3', 'Ws1', 'Ws2', 'Ws3')}
    del _L0_ffn_all
    return {'x': x, 'L0_tok_ln1_w': _L0_tok_in['ln1_w'], 'L0_tok_W': _L0_tok_in['W'], 'L0_tok_ln2_w': _L0_tok_in['ln2_w'], 'L0_attn_Wq': _L0_attn_in['Wq'], 'L0_attn_Wk': _L0_attn_in['Wk'], 'L0_attn_Wv': _L0_attn_in['Wv'], 'L0_attn_Wo': _L0_attn_in['Wo'], 'L0_attn_lambda_q1': _L0_attn_in['lambda_q1'], 'L0_attn_lambda_k1': _L0_attn_in['lambda_k1'], 'L0_attn_lambda_q2': _L0_attn_in['lambda_q2'], 'L0_attn_lambda_k2': _L0_attn_in['lambda_k2'], 'L0_attn_rms_scale': _L0_attn_in['rms_scale'], 'L0_ffn_Wg': _L0_ffn_in['Wg'], 'L0_ffn_W1': _L0_ffn_in['W1'], 'L0_ffn_W2': _L0_ffn_in['W2'], 'L0_ffn_W3': _L0_ffn_in['W3'], 'L0_ffn_Ws1': _L0_ffn_in['Ws1'], 'L0_ffn_Ws2': _L0_ffn_in['Ws2'], 'L0_ffn_Ws3': _L0_ffn_in['Ws3']}

def reference(x, L0_tok_ln1_w, L0_tok_W, L0_tok_ln2_w, L0_attn_Wq, L0_attn_Wk, L0_attn_Wv, L0_attn_Wo, L0_attn_lambda_q1, L0_attn_lambda_k1, L0_attn_lambda_q2, L0_attn_lambda_k2, L0_attn_rms_scale, L0_ffn_Wg, L0_ffn_W1, L0_ffn_W2, L0_ffn_W3, L0_ffn_Ws1, L0_ffn_Ws2, L0_ffn_Ws3):
    import jax
    import jax.numpy as jnp

    def _L0_tok_ref(img, ln1_w, W, ln2_w):
        import jax, jax.numpy as jnp
        import numpy as np
        PATCH = 16
        EPS = 1e-05

        def _patchify(img, p):
            B, C, H, W = img.shape
            h, w = (H // p, W // p)
            x = img.reshape(B, C, h, p, w, p)
            x = x.transpose(0, 2, 4, 1, 3, 5)
            return x.reshape(B, h, w, C * p * p)

        def _layernorm(x, gamma):
            mu = x.mean(axis=-1, keepdims=True)
            var = ((x - mu) ** 2).mean(axis=-1, keepdims=True)
            return (x - mu) * jax.lax.rsqrt(var + EPS) * gamma

        def _posemb_sincos_2d(h, w, dim, temperature=10000.0, dtype=jnp.float32):
            y, x = jnp.meshgrid(jnp.arange(h, dtype=dtype), jnp.arange(w, dtype=dtype), indexing='ij')
            omega = jnp.arange(dim // 4, dtype=dtype) / (dim // 4 - 1)
            omega = 1.0 / temperature ** omega
            y = y.reshape(-1)[:, None] * omega[None, :]
            x = x.reshape(-1)[:, None] * omega[None, :]
            return jnp.concatenate([jnp.sin(x), jnp.cos(x), jnp.sin(y), jnp.cos(y)], axis=1)
        patches = _patchify(img, PATCH)
        B, h, w, d = patches.shape
        x = patches.reshape(B, h * w, d)
        x = _layernorm(x, ln1_w)
        x = jnp.einsum('bnd,ed->bne', x, W)
        x = _layernorm(x, ln2_w)
        pe = _posemb_sincos_2d(h, w, x.shape[-1], dtype=x.dtype)
        return x + pe[None, :, :]

    def _L0_attn_ref(X, Wq, Wk, Wv, Wo, lambda_q1, lambda_k1, lambda_q2, lambda_k2, rms_scale):
        import jax, jax.numpy as jnp
        import numpy as np
        import math
        NUM_HEADS = 8
        D_HEAD = 128
        DEPTH = 1
        LAMBDA_INIT = 0.8 - 0.6 * math.exp(-0.3 * DEPTH)
        EPS = 1e-05
        B, N, D = X.shape
        H, dh = (NUM_HEADS, D_HEAD)

        def proj(W):
            y = jnp.einsum('bnd,ed->bne', X, W)
            return y.reshape(B, N, H, 2 * dh).transpose(0, 2, 1, 3)
        Q = proj(Wq)
        K = proj(Wk)
        V = proj(Wv)
        Q1, Q2 = (Q[..., :dh], Q[..., dh:])
        K1, K2 = (K[..., :dh], K[..., dh:])
        lam1 = jnp.exp(jnp.sum(lambda_q1 * lambda_k1, axis=-1))
        lam2 = jnp.exp(jnp.sum(lambda_q2 * lambda_k2, axis=-1))
        lam = (lam1 - lam2 + LAMBDA_INIT)[None, :, None, None]
        scaling = 1.0 / math.sqrt(dh)
        A1 = jnp.einsum('bhqd,bhkd->bhqk', Q1, K1) * scaling
        A2 = jnp.einsum('bhqd,bhkd->bhqk', Q2, K2) * scaling
        attn = jax.nn.softmax(A1, axis=-1) - lam * jax.nn.softmax(A2, axis=-1)
        O = jnp.einsum('bhqk,bhkd->bhqd', attn, V)
        rms = jnp.sqrt(jnp.mean(O * O, axis=-1, keepdims=True) + EPS)
        O = O / rms * rms_scale
        O = O * (1.0 - LAMBDA_INIT)
        O = O.transpose(0, 2, 1, 3).reshape(B, N, H * 2 * dh)
        return jnp.einsum('bne,de->bnd', O, Wo)

    def _L0_ffn_ref(x, Wg, W1, W2, W3, Ws1, Ws2, Ws3):
        import jax, jax.numpy as jnp
        import numpy as np
        B, T, C = (4, 512, 256)
        E = 8
        K = 2
        H = 352
        HS = 352 * 2
        b, t, c = x.shape
        xf = x.reshape(-1, c)
        n = xf.shape[0]
        router = xf @ Wg
        top_logits, idx = jax.lax.top_k(router, K)
        probs = jax.nn.softmax(top_logits.astype(jnp.float32), axis=-1).astype(x.dtype)
        w = jnp.zeros((n, E), x.dtype).at[jnp.arange(n)[:, None], idx].add(probs)
        h = jax.nn.silu(jnp.einsum('tc,ech->eth', xf, W1)) * jnp.einsum('tc,ech->eth', xf, W2)
        y = jnp.einsum('eth,ehc,te->tc', h, W3, w)
        y = y.reshape(b, t, c)
        hs = jax.nn.silu(xf @ Ws1) * (xf @ Ws2)
        y = y + (hs @ Ws3).reshape(b, t, c)
        return y
    h = _L0_tok_ref(x, L0_tok_ln1_w, L0_tok_W, L0_tok_ln2_w)
    h = _layernorm(h + _L0_attn_ref(h, L0_attn_Wq, L0_attn_Wk, L0_attn_Wv, L0_attn_Wo, L0_attn_lambda_q1, L0_attn_lambda_k1, L0_attn_lambda_q2, L0_attn_lambda_k2, L0_attn_rms_scale), axis=-1)
    h = _layernorm(h + _L0_ffn_ref(h, L0_ffn_Wg, L0_ffn_W1, L0_ffn_W2, L0_ffn_W3, L0_ffn_Ws1, L0_ffn_Ws2, L0_ffn_Ws3), axis=-1)
    return h

_drawn_inputs = setup_inputs


def setup_inputs(seed=0):
    import zlib

    import numpy as np

    out = dict(_drawn_inputs(seed))
    spreads = {'L0_attn_rms_scale': (1.0, 0.2)}
    factors = {'L0_attn_lambda_q1': 5.066,
     'L0_attn_lambda_k1': 8.0,
     'L0_attn_lambda_q2': 7.623,
     'L0_attn_lambda_k2': 8.0,
     'L0_ffn_Wg': 4.717,
     'L0_ffn_W1': 4.036,
     'L0_ffn_W2': 3.989,
     'L0_ffn_W3': 4.015,
     'L0_ffn_Ws1': 3.142,
     'L0_ffn_Ws2': 3.055,
     'L0_ffn_Ws3': 3.056}
    for name, (base, spread) in spreads.items():
        noise = np.random.default_rng([zlib.crc32(name.encode()), seed]).standard_normal(out[name].shape)
        drawn = base * np.exp(spread * noise) if base else spread * noise
        out[name] = jnp.asarray(drawn.astype(out[name].dtype))
    for name, factor in factors.items():
        out[name] = (out[name] * factor).astype(out[name].dtype)
    return out
```

```python
from contextlib import ExitStack

import concourse.bass as bass
from concourse import mybir

F32 = mybir.dt.float32
F32R = mybir.dt.float32r
U32 = mybir.dt.uint32
ACT = mybir.ActivationFunctionType
ALU = mybir.AluOpType
AX_X = mybir.AxisListType.X

P = 128
IMAGES = 16
IMG_TOK = 36
TOK = IMAGES * IMG_TOK
TILES = 5
TROWS = [min(P, TOK - P * t) for t in range(TILES)]
D = 256
DC = D // P
PATCH = 768
KC = PATCH // P
HEADS = 8
HALF = TOK // 2
GRP = 2 * IMG_TOK
GRPS = HALF // GRP
UNITS = 2 * HEADS
EXPERTS = 8
SHARED0 = 64
CHUNKS = 28
SHARED_CHUNKS = 6
EPS = 1e-5
LAMBDA_INIT = 0.8 - 0.6 * 0.7408182206817179
SCALE = 1.0 / 128 ** 0.5
OUT_C = 1.0 - LAMBDA_INIT


def build(nc, x, tokw, consts, pe_tab, g2, wqk, wv, wo, ident_d, masks, wg, s12, s3, w12, w3, out):
    ctx = ExitStack()
    with ctx:
        def sb(name, shape, dt=F32):
            return ctx.enter_context(nc.sbuf_tensor(name, shape, dt))

        def sem(name):
            return ctx.enter_context(nc.semaphore(name))

        region = sb("region", [P, TILES * PATCH])
        xr = region[:, :].rearrange("p (t f) -> p t f", t=TILES)
        xg_raw = region[0:GRP, 0:2 * GRPS * D].rearrange("p (g d) -> p g d", d=D)
        gates = region[:, 0:4 * TOK].rearrange("p (s n) -> p s n", s=4)
        split_region = sb("split_region", [P, 2 * KC * TOK], F32R)
        xT = [split_region[:, i * KC * TOK:(i + 1) * KC * TOK].rearrange("p (k n) -> p k n", k=KC) for i in range(2)]
        h2T = [split_region[:, i * DC * TOK:(i + 1) * DC * TOK].rearrange("p (k n) -> p k n", k=DC) for i in range(2)]
        base12 = 2 * DC * TOK
        w12s = [split_region[:, base12 + 1024 * i:base12 + 1024 * (i + 1)].rearrange("p (s w k m) -> p s w k m", s=2, w=2, k=DC)
                for i in range(2)]
        base3 = base12 + 2048
        w3s = [split_region[:, base3 + 512 * i:base3 + 512 * (i + 1)].rearrange("p (s n) -> p s n", s=2) for i in range(2)]
        tw = sb("tw", [P, KC, D])
        tws = [sb(f"tws{i}", [P, KC, D], F32R) for i in range(2)]
        cst = sb("cst", [P, KC + 2 + 4 * HEADS])
        gam1 = cst[:, 0:KC]
        rms = cst[:, KC:KC + 2]
        lam4 = cst[:, KC + 2:KC + 2 + 4 * HEADS].rearrange("p (i j h) -> p i j h", i=2, j=2)
        ident = sb("ident", [P, P])
        ones = sb("ones", [P, P])
        pet = sb("pet", [P, TILES, D])
        g2b = sb("g2b", [P, D])
        mask_raw = sb("mask_raw", [2, GRP + HALF])
        mask = sb("mask", [2, GRP + HALF], F32R)
        bns = sb("bns", [P, TILES, 2, 6])
        mv = sb("mv", [P, TILES, 2])
        rstd = sb("rstd", [P, TILES])
        mhalf = sb("mhalf", [P, TILES])
        h = sb("h", [P, TILES, D])
        hT = [sb(f"hT{i}", [P, DC, TOK], F32R) for i in range(2)]
        xg = [sb(f"xg{i}", [GRP, 2 * GRPS, D], F32R) for i in range(2)]
        lprod = sb("lprod", [P, 2 * HEADS])
        lexp = sb("lexp", [P, 2 * HEADS])
        nlam = sb("nlam", [P, HEADS])
        qk_raw = sb("qk_raw", [P, 2, 4 * D])
        v_raw = sb("v_raw", [P, 2, 2 * D])
        o_raw = sb("o_raw", [P, 2, 2 * D])
        qks = [sb(f"qks{i}", [P, 2, 4 * D], F32R) for i in range(2)]
        vs = [sb(f"vs{i}", [P, 2, 2 * D], F32R) for i in range(2)]
        os_ = [sb(f"os{i}", [P, 2, 2 * D], F32R) for i in range(2)]
        qkT = [sb(f"qkT{i}", [P, 4, HALF], F32R) for i in range(2)]
        prob = sb("prob", [GRP, 2 * GRPS, GRP])
        smax = sb("smax", [GRP, 2 * GRPS])
        ssum = sb("ssum", [GRP, 2 * GRPS])
        rsum = sb("rsum", [GRP, 2 * GRPS])
        attn = sb("attn", [GRP, GRPS, GRP])
        aT = [sb(f"aT{i}", [GRP, HALF], F32R) for i in range(2)]
        axT = [sb(f"axT{i}", [P, DC, HALF], F32R) for i in range(2)]
        oT = [sb(f"oT{i}", [P, 2, DC, TOK], F32R) for i in range(2)]
        sq = sb("sq", [P, DC, HALF])
        sqs = sb("sqs", [P, 2, TOK])
        ms = sb("ms", [P, TILES])
        rinv = sb("rinv", [P, TILES])
        wgr = sb("wgr", [P, DC, EXPERTS])
        wgs = [sb(f"wgs{i}", [P, DC, EXPERTS], F32R) for i in range(2)]
        logit = sb("logit", [P, TILES, EXPERTS])
        top = sb("top", [P, TILES, 8])
        topi = sb("topi", [P, TILES, 8], U32)
        topf = sb("topf", [P, TILES, 2])
        iota = sb("iota", [P, EXPERTS])
        prb = sb("prb", [P, TILES, 4])
        gate = sb("gate", [P, 2, TILES, EXPERTS])
        gateT = sb("gateT", [EXPERTS, TOK])
        r12 = sb("r12", [P, 2, 2, DC, P])
        r3 = sb("r3", [P, 2, D])
        ffn_rows = pet[:, :, :].rearrange("p t d -> p (t d)")
        sil = ffn_rows[:, 0:TOK].rearrange("p (s n) -> p s n", s=2)
        hraw = ffn_rows[:, TOK:2 * TOK].rearrange("p (s n) -> p s n", s=2)
        hh = [a[:, :, :].rearrange("p k d -> p (k d)")[:, 0:TOK].rearrange("p (s n) -> p s n", s=2) for a in tws]
        yT = tw[:, :, :].rearrange("p k d -> p (k d)")[:, 0:DC * TOK].rearrange("p (k n) -> p k n", k=DC)

        ps = ctx.enter_context(nc.psum_tensor("ps", [P, 8, 512], F32))

        h_dram = nc.dram_tensor("h_scratch", (TOK, D), F32, kind="Internal").ap()
        g_dram = nc.dram_tensor("gate_scratch", (EXPERTS * 11, TOK), F32, kind="Internal").ap()

        ld_const = sem("ld_const")
        ld_mask = sem("ld_mask")
        ld_tw = sem("ld_tw")
        h_stored = sem("h_stored")
        ld_xg = sem("ld_xg")
        g_stored = sem("g_stored")
        out_stored = sem("out_stored")
        mem_ready = sem("mem_ready")
        stat1 = sem("stat1")
        rstd_ready = sem("rstd_ready")
        xn_ready = sem("xn_ready")
        pe_t = sem("pe_t")
        act_t = sem("act_t")
        dve_t = sem("dve_t")
        pe_z = sem("pe_z")
        stat2 = sem("stat2")
        h_part = sem("h_part")
        h_ready = sem("h_ready")
        pe_ht = sem("pe_ht")
        act_ht = sem("act_ht")
        dve_ht = sem("dve_ht")
        tw_scaled = sem("tw_scaled")
        tw_hi = sem("tw_hi")
        tw_lo = sem("tw_lo")
        xg_hi = sem("xg_hi")
        xg_lo = sem("xg_lo")
        lam_prod = sem("lam_prod")
        pe_lam = sem("pe_lam")
        lam_exp = sem("lam_exp")
        lam_part = sem("lam_part")
        lam_ready = sem("lam_ready")
        mask_ready = sem("mask_ready")
        wg_split = sem("wg_split")
        pe_q = sem("pe_q")
        act_q = sem("act_q")
        dve_q = sem("dve_q")
        pe_s = sem("pe_s")
        dve_max = sem("dve_max")
        dve_sub = sem("dve_sub")
        act_exp = sem("act_exp")
        dve_sum = sem("dve_sum")
        dve_rec = sem("dve_rec")
        dve_r = sem("dve_r")
        pool_mul = sem("pool_mul")
        pool_attn = sem("pool_attn")
        pe_pt = sem("pe_pt")
        act_pt = sem("act_pt")
        dve_pt = sem("dve_pt")
        pe_ax = sem("pe_ax")
        act_ax = sem("act_ax")
        dve_ax = sem("dve_ax")
        pe_o = sem("pe_o")
        act_hi = sem("act_hi")
        act_o = sem("act_o")
        dve_o = sem("dve_o")
        pool_sq = sem("pool_sq")
        pe_stat = sem("pe_stat")
        dve_stat = sem("dve_stat")
        pool_rinv = sem("pool_rinv")
        pe_f = sem("pe_f")
        dve_f = sem("dve_f")
        hi_qk = sem("hi_qk")
        lo_qk = sem("lo_qk")
        hi_v = sem("hi_v")
        lo_v = sem("lo_v")
        hi_o = sem("hi_o")
        lo_o = sem("lo_o")
        stat3 = sem("stat3")
        stat3a = sem("stat3a")
        h2_ready = sem("h2_ready")
        pe_h2t = sem("pe_h2t")
        act_h2t = sem("act_h2t")
        dve_h2t = sem("dve_h2t")
        pe_route = sem("pe_route")
        dve_small = sem("dve_small")
        act_small = sem("act_small")
        gate_ready = sem("gate_ready")
        pe_gt = sem("pe_gt")
        gt_ready = sem("gt_ready")
        hi_12 = sem("hi_12")
        lo_12 = sem("lo_12")
        hi_3 = sem("hi_3")
        lo_3 = sem("lo_3")
        pe_up = sem("pe_up")
        act_sil = sem("act_sil")
        pool_gate = sem("pool_gate")
        dve_h = sem("dve_h")
        act_h = sem("act_h")
        dve_hl = sem("dve_hl")
        pe_dn = sem("pe_dn")
        y_ready = sem("y_ready")
        pe_yt = sem("pe_yt")
        y_tok = sem("y_tok")
        stat4 = sem("stat4")
        y_done = sem("y_done")
        iota_ready = sem("iota_ready")
        ld_x = [sem(f"ld_x{t}") for t in range(TILES)]
        ld_qk = [sem(f"ld_qk{i}") for i in range(2)]
        ld_v = [sem(f"ld_v{i}") for i in range(2)]
        ld_o = [sem(f"ld_o{i}") for i in range(2)]
        ld_12 = [sem(f"ld_12_{i}") for i in range(2)]
        ld_3 = [sem(f"ld_3_{i}") for i in range(2)]
        ld_g = [sem(f"ld_g{i}") for i in range(4)]
        block = ctx.enter_context(nc.Block())

        def tcols(t):
            return slice(P * t, P * t + TROWS[t])

        def up_rows(c):
            return SHARED0 if c == 0 else P

        @block.sync
        def _(sp):
            for t in range(TILES):
                sp.dma_start(xr[0:TROWS[t], t, :], x[P * t:P * t + TROWS[t], :]).then_inc(ld_x[t], 16)
                if t == 0:
                    sp.dma_start(ident[:], ident_d).then_inc(ld_const, 16)
                    sp.dma_start(cst[:], consts).then_inc(ld_const, 16)
                    sp.dma_start(tw[:], tokw).then_inc(ld_tw, 16)
            sp.dma_start(qk_raw[:, 0, :], wqk[0, :, :]).then_inc(ld_qk[0], 16)
            sp.dma_start(g2b[:], g2.broadcast_to([P, D])).then_inc(ld_const, 16)
            sp.dma_start(pet[:, 0:4, :], pe_tab[0:512, :].rearrange("(t p) d -> p t d", p=P)).then_inc(ld_const, 16)
            sp.dma_start(pet[0:64, 4, :], pe_tab[512:TOK, :]).then_inc(ld_const, 16)
            sp.dma_start(wgr[:], wg).then_inc(ld_const, 16)
            sp.dma_start(mask_raw[:], masks).then_inc(ld_mask, 16)
            sp.dma_start(qk_raw[:, 1, :], wqk[1, :, :]).then_inc(ld_qk[1], 16)
            for i in range(2):
                sp.dma_start(v_raw[:, i, :], wv[i, :, :]).then_inc(ld_v[i], 16)
                sp.dma_start(o_raw[:, i, :], wo[i, :, :]).then_inc(ld_o[i], 16)
            for t in range(TILES):
                sp.wait_ge(h_ready, t + 1)
                sp.dma_start(h_dram[P * t:P * t + TROWS[t], :], h[0:TROWS[t], t, :]).then_inc(h_stored, 16)
            sp.wait_ge(h_stored, 16 * TILES)
            sp.dma_start(xg_raw, h_dram.rearrange("(g p) d -> p g d", p=GRP)).then_inc(ld_xg, 16)
            sp.dma_start(r12[:, 0, :, :, 0:SHARED0], s12).then_inc(ld_12[0], 16)
            sp.dma_start(r3[0:SHARED0, 0, :], s3).then_inc(ld_3[0], 16)
            sp.dma_start(r12[:, 1, :, :, :], w12[0, :, :]).then_inc(ld_12[1], 16)
            sp.dma_start(r3[:, 1, :], w3[0, :, :]).then_inc(ld_3[1], 16)

            def head_pair(i):
                for r in range(2):
                    hd = 2 + 2 * i + r
                    sp.wait_ge(lo_qk, 2 * i + r + 1)
                    sp.dma_start(qk_raw[:, r, :], wqk[bass.ds(hd, 1), :, :].rearrange("a p n -> p (a n)")).then_inc(ld_qk[r], 16)
                    sp.wait_ge(lo_v, 2 * i + r + 1)
                    sp.dma_start(v_raw[:, r, :], wv[bass.ds(hd, 1), :, :].rearrange("a p n -> p (a n)")).then_inc(ld_v[r], 16)
                    sp.wait_ge(lo_o, 2 * i + r + 1)
                    sp.dma_start(o_raw[:, r, :], wo[bass.ds(hd, 1), :, :].rearrange("a p n -> p (a n)")).then_inc(ld_o[r], 16)

            with sp.Fori(0, HEADS // 2 - 1) as i:
                head_pair(i)
            sp.wait_ge(gt_ready, 1)
            sp.dma_start(g_dram.rearrange("(e k) n -> e k n", k=11),
                         gateT[:, :].unsqueeze(1).broadcast_to([EXPERTS, 11, TOK])).then_inc(g_stored, 16)

            def load_gate(i, r):
                for b in range(4):
                    sp.dma_start(gates[32 * b:32 * b + 32, r, :],
                                 g_dram[bass.ds(4 * i + b, 1), :].broadcast_to([32, TOK])).then_inc(ld_g[r], 16)

            def load_w(c, r):
                sp.wait_ge(lo_12, c - 1)
                sp.dma_start(r12[:, r, :, :, :], w12[bass.ds(c - 1, 1), :, :].rearrange("a p n -> p (a n)")).then_inc(ld_12[r], 16)
                sp.wait_ge(lo_3, c - 1)
                sp.dma_start(r3[:, r, :], w3[bass.ds(c - 1, 1), :, :].rearrange("a p n -> p (a n)")).then_inc(ld_3[r], 16)

            load_w(2, 0)
            sp.wait_ge(g_stored, 16)
            for r in range(4):
                load_gate(r, r)
            load_w(3, 1)
            for c in range(4, 10):
                load_w(c, c % 2)

            def gate_rest(c, r4):
                sp.wait_ge(pool_gate, 2 * (c - 4 - SHARED_CHUNKS) + 2)
                load_gate(c - SHARED_CHUNKS, r4)
                load_w(c, r4 % 2)

            with sp.Fori(0, 4) as i:
                for r in range(4):
                    gate_rest(10 + 4 * i + r, r)
            for r in range(2):
                gate_rest(26 + r, r)
            for t in range(TILES):
                sp.wait_ge(y_done, t + 1)
                sp.dma_start(out[P * t:P * t + TROWS[t], :], h[0:TROWS[t], t, :]).then_inc(out_stored, 16)
            sp.wait_ge(out_stored, 16 * TILES)

        def mm3(o, lhs, rhs, first, last):
            nc.tensor.matmul(o, lhs[0], rhs[0], start=first, stop=False)
            nc.tensor.matmul(o, lhs[0], rhs[1], start=False, stop=False)
            return nc.tensor.matmul(o, lhs[1], rhs[0], start=False, stop=last)

        @block.tensor
        def _(pe):
            pe.wait_ge(ld_const, 16 * 6)

            def patch_transposes(t):
                n = TROWS[t]
                pe.wait_ge(xn_ready, t + 1)
                if t >= 2:
                    pe.wait_ge(dve_t, 2 * (t - 1))
                for k in range(KC):
                    l = nc.tensor.transpose(ps[:, 2 * (t % 2) + k // 3, P * (k % 3):P * (k % 3) + n],
                                            xr[0:n, t, P * k:P * k + P], ident[0:n, 0:n])
                    if k % 3 == 2:
                        l.then_inc(pe_t, 1)

            def token_product(t):
                n = TROWS[t]
                pe.wait_ge(dve_t, 2 * (t + 1))
                if t == 0:
                    pe.wait_ge(tw_lo, 1)
                if t >= 2:
                    pe.wait_ge(h_ready, t - 1)
                for k in range(KC):
                    l = mm3(ps[0:n, 4 + t % 2, 0:D], [a[:, k, tcols(t)] for a in xT], [a[:, k, :] for a in tws],
                            k == 0, k == KC - 1)
                l.then_inc(pe_z, 1)

            def h_transposes(t):
                n = TROWS[t]
                pe.wait_ge(h_ready, t + 1)
                if t >= 2:
                    pe.wait_ge(dve_ht, t - 1)
                for k in range(DC):
                    l = nc.tensor.transpose(ps[:, 6 + t % 2, P * k:P * k + n], h[0:n, t, P * k:P * k + P], ident[0:n, 0:n])
                l.then_inc(pe_ht, 1)

            for t in range(TILES + 2):
                if t < TILES:
                    patch_transposes(t)
                if 1 <= t <= TILES:
                    token_product(t - 1)
                if t >= 2:
                    h_transposes(t - 2)
            pe.wait_ge(lam_prod, 1)
            pe.wait_ge(mem_ready, 1)
            nc.tensor.matmul(ps[:, 0, 0:2 * HEADS], ones[:, :], lprod[:, :], start=True, stop=True).then_inc(pe_lam, 1)
            pe.wait_ge(lam_exp, 1)

            def project(u, it, j):
                hd, hs, bank = u // 2, (u // 2) % 2, j
                if j == 0:
                    pe.wait_ge(lo_qk, hd + 1 + 2 * it)
                    if u == 0:
                        pe.wait_ge(dve_ht, TILES)
                if u >= 3:
                    if j < 2:
                        pe.wait_ge(dve_ax, 2 * (u - 3) + j + 1 + 8 * it)
                    else:
                        pe.wait_ge(dve_o, 2 * (u - 3) + j - 1 + 8 * it)
                c0 = (j % 2) * 2 * D + (j // 2) * P
                cols = slice(HALF * (u % 2), HALF * (u % 2) + HALF)
                for k in range(DC):
                    l = mm3(ps[:, bank, 0:HALF], [a[:, hs, c0 + k * D:c0 + k * D + P] for a in qks],
                            [a[:, k, cols] for a in hT], k == 0, k == DC - 1)
                l.then_inc(pe_q, 1)

            def scores(u, it):
                if u == 0:
                    pe.wait_ge(mask_ready, 1)
                pe.wait_ge(dve_q, 4 * u + 4 + 4 * 4 * it)
                if u >= 1:
                    pe.wait_ge(dve_sub, u + 4 * it)
                for j in range(2):
                    nc.tensor.matmul(ps[0:GRP, 4 + j, 0:HALF], mask[:, 0:GRP], mask[:, GRP:GRP + HALF], start=True, stop=False)
                    for g in range(GRPS):
                        c = slice(GRP * g, GRP * g + GRP)
                        l = mm3(ps[0:GRP, 4 + j, c], [a[:, 2 * j, c] for a in qkT], [a[:, 2 * j + 1, c] for a in qkT],
                                False, g == GRPS - 1)
                l.then_inc(pe_s, 1)

            def attn_transpose(s, it):
                u = s - 1
                pe.wait_ge(pool_attn, u + 1 + 4 * it)
                if s >= 4:
                    if s % 2 == 0:
                        pe.wait_ge(dve_f, 5 * ((s - 4) // 2) + 3 + 10 * it)
                    else:
                        pe.wait_ge(dve_f, 5 * ((s - 5) // 2) + 5 + 10 * it)
                for g in range(GRPS):
                    l = nc.tensor.transpose(ps[0:GRP, 6, GRP * g:GRP * g + GRP], attn[:, g, :], ident[0:GRP, 0:GRP])
                l.then_inc(pe_pt, 1)

            def attend(u, it):
                pe.wait_ge(dve_pt, u + 1 + 4 * it)
                if u == 0:
                    pe.wait_ge(xg_lo, 1)
                for k in range(DC):
                    if u + 2 < UNITS:
                        pe.wait_ge(dve_q, 4 * (u + 2) + k + 1 + 16 * it)
                    else:
                        pe.wait_ge(dve_ax, 2 * (u - 1) + k + 1)
                    for g in range(GRPS):
                        gg = GRPS * (u % 2) + g
                        l = mm3(ps[:, k, GRP * g:GRP * g + GRP], [a[:, gg, P * k:P * k + P] for a in xg],
                                [a[:, GRP * g:GRP * g + GRP] for a in aT], True, True)
                    l.then_inc(pe_ax, 1)

            def values(u, it):
                hd, hs = u // 2, (u // 2) % 2
                pe.wait_ge(dve_ax, 2 * u + 2 + 8 * it)
                if u % 2 == 0:
                    pe.wait_ge(lo_v, hd + 1 + 2 * it)
                for e in range(DC):
                    if u + 2 < UNITS:
                        pe.wait_ge(dve_q, 4 * (u + 2) + e + 3 + 16 * it)
                    else:
                        pe.wait_ge(dve_o, 2 * (u - 1) + e + 1)
                    for k in range(DC):
                        l = mm3(ps[:, 2 + e, 0:HALF], [a[:, hs, k * D + P * e:k * D + P * e + P] for a in vs],
                                [a[:, k, :] for a in axT], k == 0, k == DC - 1)
                    l.then_inc(pe_o, 1)

            def square_sums(hd, it):
                pe.wait_ge(pool_sq, 2 * hd + 2 + 4 * it)
                if hd >= 1:
                    pe.wait_ge(dve_f, 5 * hd + 10 * it)
                for t in range(TILES):
                    l = nc.tensor.matmul(ps[0:TROWS[t], 7, t:t + 1], sqs[:, hd % 2, tcols(t)], ones[:, 0:1],
                                         start=True, stop=True)
                l.then_inc(pe_stat, 1)

            def output_tiles(hd, it, tiles):
                for t in tiles:
                    n = TROWS[t]
                    if t == 0:
                        pe.wait_ge(lo_o, hd + 1 + 2 * it)
                        pe.wait_ge(dve_o, 4 * hd + 4 + 8 * it)
                        if hd >= 1:
                            pe.wait_ge(dve_f, 5 * hd + 10 * it)
                    elif t == 1:
                        pe.wait_ge(dve_stat, hd + 1 + 2 * it)
                    else:
                        pe.wait_ge(dve_f, 5 * hd + t - 1 + 10 * it)
                    bank = (6, 7, 6, 7, 6)[t]
                    for k in range(DC):
                        l = mm3(ps[0:n, bank, 0:D], [a[:, hd % 2, k, tcols(t)] for a in oT],
                                [a[:, hd % 2, k * D:k * D + D] for a in os_], k == 0, k == DC - 1)
                    l.then_inc(pe_f, 1)

            def step(s, it=0):
                if s + 1 < UNITS:
                    project(s + 1, it, 0)
                    project(s + 1, it, 1)
                if 1 <= s <= UNITS:
                    attn_transpose(s, it)
                if s + 1 < UNITS:
                    project(s + 1, it, 2)
                    project(s + 1, it, 3)
                if s % 2 == 1 and s >= 3:
                    square_sums((s - 3) // 2, it)
                if 1 <= s <= UNITS:
                    attend(s - 1, it)
                if s >= 3:
                    if s % 2 == 1:
                        output_tiles((s - 3) // 2, it, (0, 1, 2))
                    else:
                        output_tiles((s - 4) // 2, it, (3, 4))
                if 1 <= s <= UNITS:
                    values(s - 1, it)
                if s + 1 < UNITS:
                    scores(s + 1, it)

            for s in range(-1, 4):
                step(s)
            with pe.Fori(0, 2) as i:
                for r in range(4):
                    step(4 + r, i)
            for s in range(12, 19):
                step(s)

            pe.wait_ge(dve_f, 5 * HEADS)
            for t in range(TILES):
                n = TROWS[t]
                pe.wait_ge(h2_ready, t + 1)
                if t >= 2:
                    pe.wait_ge(dve_h2t, t - 1)
                for k in range(DC):
                    l = nc.tensor.transpose(ps[:, 4 + t % 2, P * k:P * k + n], h[0:n, t, P * k:P * k + P], ident[0:n, 0:n])
                l.then_inc(pe_h2t, 1)
            pe.wait_ge(dve_h2t, TILES)
            pe.wait_ge(wg_split, 2)
            for t in range(TILES):
                for k in range(DC):
                    l = mm3(ps[0:TROWS[t], 6, EXPERTS * t:EXPERTS * t + EXPERTS], [a[:, k, tcols(t)] for a in h2T],
                            [a[:, k, :] for a in wgs], k == 0, k == DC - 1)
            l.then_inc(pe_route, 1)

            def up(v, it=0):
                c, cs, m = v // 2, (v // 2) % 2, up_rows(v // 2)
                cols = slice(HALF * (v % 2), HALF * (v % 2) + HALF)
                if v % 2 == 0:
                    pe.wait_ge(lo_12, c + 1 + 2 * it)
                if v >= 2:
                    pe.wait_ge(act_sil, v - 1 + 4 * it)
                for i in range(2):
                    if v >= 2 and i == 1:
                        pe.wait_ge(dve_h, v - 1 + 4 * it)
                    for k in range(DC):
                        l = mm3(ps[0:m, 2 * (v % 2) + i, 0:HALF], [a[:, cs, i, k, 0:m] for a in w12s],
                                [a[:, k, cols] for a in h2T], k == 0, k == DC - 1)
                    l.then_inc(pe_up, 1)

            def down(v, it=0):
                c, cs, m = v // 2, (v // 2) % 2, up_rows(v // 2)
                if v % 2 == 0:
                    pe.wait_ge(lo_3, c + 1 + 2 * it)
                pe.wait_ge(dve_hl, v + 1 + 4 * it)
                for k in range(DC):
                    l = mm3(ps[:, 4 + 2 * (v % 2) + k, 0:HALF], [a[0:m, cs, P * k:P * k + P] for a in w3s],
                            [a[0:m, v % 2, :] for a in hh], c == 0, c == CHUNKS - 1)
                l.then_inc(pe_dn, 1)

            up(0)
            up(1)
            up(2)
            pe.wait_ge(gate_ready, 1)
            for t in range(TILES):
                l = nc.tensor.transpose(ps[0:EXPERTS, 6 + t // 3, P * (t % 3):P * (t % 3) + TROWS[t]],
                                        gate[0:TROWS[t], 0, t, :], ident[0:TROWS[t], 0:TROWS[t]])
            l.then_inc(pe_gt, 1)
            pe.wait_ge(gt_ready, 1)
            down(0)
            for v in range(1, 4):
                up(v + 2)
                down(v)
            with pe.Fori(0, 12) as i:
                for r in range(4):
                    up(6 + r, i)
                    down(4 + r, i)
            for v in range(52, 56):
                if v + 2 < 2 * CHUNKS:
                    up(v + 2)
                down(v)
            for t in range(TILES):
                n = TROWS[t]
                pe.wait_ge(y_ready, 4)
                if t >= 4:
                    pe.wait_ge(y_tok, t - 3)
                for k in range(DC):
                    l = nc.tensor.transpose(ps[0:n, t % 4, P * k:P * k + P], yT[:, k, tcols(t)], ident[:, :])
                l.then_inc(pe_yt, 1)

        @block.scalar
        def _(act):
            def copy(o, i, scale=1.0):
                return nc.scalar.activation(o, i, ACT.Copy, scale=scale)

            act.wait_ge(tw_scaled, 1)
            copy(tws[0][:], tw[:]).then_inc(tw_hi, 1)
            act.wait_ge(ld_qk[0], 16)
            copy(qks[0][:, 0, :], qk_raw[:, 0, :]).then_inc(hi_qk, 1)

            def patches_hi(t):
                n = TROWS[t]
                for b in range(2):
                    act.wait_ge(pe_t, 2 * t + b + 1)
                    copy(xT[0][:, 3 * b:3 * b + 3, tcols(t)],
                         ps[:, 2 * (t % 2) + b, 0:384].rearrange("p (k n) -> p k n", k=3)[:, :, 0:n]).then_inc(act_t, 1)

            def h_hi(t):
                n = TROWS[t]
                act.wait_ge(pe_ht, t + 1)
                copy(hT[0][:, :, tcols(t)],
                     ps[:, 6 + t % 2, 0:D].rearrange("p (k n) -> p k n", k=DC)[:, :, 0:n]).then_inc(act_ht, 1)

            for t in range(TILES + 2):
                if t < TILES:
                    patches_hi(t)
                if t >= 2:
                    h_hi(t - 2)
            act.wait_ge(pe_lam, 1)
            nc.scalar.activation(lexp[:], ps[:, 0, 0:2 * HEADS], ACT.Exp).then_inc(lam_exp, 1)

            def proj_hi(u, it, j):
                act.wait_ge(pe_q, 4 * u + j + 1 + 16 * it)
                copy(qkT[0][:, j, :], ps[:, j, 0:HALF]).then_inc(act_q, 1)

            def step(s, it=0):
                if s + 1 < UNITS:
                    proj_hi(s + 1, it, 0)
                    proj_hi(s + 1, it, 1)
                if 1 <= s <= UNITS:
                    act.wait_ge(pe_pt, s + 4 * it)
                    copy(aT[0][:], ps[0:GRP, 6, 0:HALF]).then_inc(act_pt, 1)
                if s + 1 < UNITS:
                    proj_hi(s + 1, it, 2)
                    proj_hi(s + 1, it, 3)
                if 0 <= s < UNITS:
                    act.wait_ge(dve_sub, s + 1 + 4 * it)
                    nc.scalar.activation(prob[:], prob[:], ACT.Exp, scale=SCALE).then_inc(act_exp, 1)
                if 1 <= s <= UNITS:
                    u = s - 1
                    for k in range(DC):
                        act.wait_ge(pe_ax, 2 * u + k + 1 + 8 * it)
                        copy(axT[0][:, k, :], ps[:, k, 0:HALF]).then_inc(act_ax, 1)
                    for e in range(DC):
                        act.wait_ge(pe_o, 2 * u + e + 1 + 8 * it)
                        copy(oT[0][:, (u // 2) % 2, e, HALF * (u % 2):HALF * (u % 2) + HALF], ps[:, 2 + e, 0:HALF],
                             rms[:, e:e + 1]).then_inc(act_hi, 1)
                        if u >= 1 and e == 0:
                            act.wait_ge(pool_sq, u + 4 * it)
                        nc.scalar.activation(sq[:, e, :], ps[:, 2 + e, 0:HALF], ACT.Square).then_inc(act_o, 1)
                if s % 2 == 1 and (s + 3) // 2 < HEADS:
                    hd = (s + 3) // 2
                    if s >= 1:
                        act.wait_ge(pe_q, 8 * (hd - 1) + 16 * it)
                    act.wait_ge(ld_qk[hd % 2], 16 * (hd // 2 + 1 + it))
                    copy(qks[0][:, hd % 2, :], qk_raw[:, hd % 2, :]).then_inc(hi_qk, 1)
                if s % 2 == 0 and s < UNITS:
                    hd = s // 2
                    if hd >= 2:
                        act.wait_ge(pe_o, 4 * (hd - 1) + 8 * it)
                    act.wait_ge(ld_v[hd % 2], 16 * (hd // 2 + 1 + it))
                    copy(vs[0][:, hd % 2, :], v_raw[:, hd % 2, :]).then_inc(hi_v, 1)
                    if hd >= 2:
                        act.wait_ge(pe_f, 5 * (hd - 1) + 10 * it)
                    act.wait_ge(ld_o[hd % 2], 16 * (hd // 2 + 1 + it))
                    copy(os_[0][:, hd % 2, :], o_raw[:, hd % 2, :]).then_inc(hi_o, 1)

            for s in range(-1, 4):
                step(s)
            with act.Fori(0, 2) as i:
                for r in range(4):
                    step(4 + r, i)
            for s in range(12, 17):
                step(s)

            for t in range(TILES):
                n = TROWS[t]
                act.wait_ge(pe_h2t, t + 1)
                copy(h2T[0][:, :, tcols(t)],
                     ps[:, 4 + t % 2, 0:D].rearrange("p (k n) -> p k n", k=DC)[:, :, 0:n]).then_inc(act_h2t, 1)
            act.wait_ge(dve_small, 3)
            nc.scalar.activation(prb[:, :, 1:2], prb[:, :, 0:1], ACT.Exp).then_inc(act_small, 1)

            def silu(v, it=0):
                m = up_rows(v // 2)
                act.wait_ge(pe_up, 2 * v + 1 + 8 * it)
                if v >= 2:
                    act.wait_ge(dve_h, v - 1 + 4 * it)
                nc.scalar.activation(sil[0:m, v % 2, :], ps[0:m, 2 * (v % 2), 0:HALF], ACT.Silu).then_inc(act_sil, 1)

            def hidden_hi(v, it=0):
                m = up_rows(v // 2)
                act.wait_ge(dve_h, v + 1 + 4 * it)
                if v >= 2:
                    act.wait_ge(pe_dn, v - 1 + 4 * it)
                copy(hh[0][0:m, v % 2, :], hraw[0:m, v % 2, :]).then_inc(act_h, 1)

            silu(0)
            for v in range(3):
                silu(v + 1)
                hidden_hi(v)
            with act.Fori(0, 13) as i:
                for r in range(4):
                    silu(4 + r, i)
                    hidden_hi(3 + r, i)
            hidden_hi(55)
            act.wait_ge(pe_dn, 2 * CHUNKS)
            for k in range(DC):
                copy(yT[:, k, HALF:TOK], ps[:, 6 + k, 0:HALF]).then_inc(y_ready, 1)

        @block.vector
        def _(dve):
            V = nc.vector

            V.memset(mhalf[:], -0.5)
            V.memset(ones[:], 1.0)
            V.memset(logit[:], 0.0)
            V.memset(ms[:], 1.0)
            V.memset(mv[:], 1.0).then_inc(mem_ready, 1)
            dve.wait_ge(mem_ready, 1)

            def scale_tok_weights():
                dve.wait_ge(ld_const, 96)
                dve.wait_ge(ld_tw, 16)
                for k in range(KC):
                    l = V.tensor_scalar(tw[:, k, :], tw[:, k, :], gam1[:, k:k + 1], None, ALU.mult)
                l.then_inc(tw_scaled, 1)

            def patch_norm(t):
                n = TROWS[t]
                dve.wait_ge(ld_x[t], 16)
                for b in range(2):
                    l = V.bn_stats(bns[0:n, t, b, :], xr[0:n, t, 384 * b:384 * b + 384])
                l.then_inc(stat1, 1)
                dve.wait_ge(stat1, 2 * t + 1)
                V.bn_aggr(mv[0:n, t, :], bns[0:n, t, :, :].rearrange("p b s -> p (b s)")).then_inc(stat1, 1)

            def patch_apply(t):
                n = TROWS[t]
                dve.wait_ge(rstd_ready, t + 1)
                V.tensor_scalar(xr[0:n, t, :], xr[0:n, t, :], mv[0:n, t, 0:1], rstd[0:n, t:t + 1],
                                ALU.subtract, ALU.mult).then_inc(xn_ready, 1)

            def patches_lo(t):
                n = TROWS[t]
                for b in range(2):
                    dve.wait_ge(act_t, 2 * t + b + 1)
                    c = slice(3 * b, 3 * b + 3)
                    V.tensor_tensor(xT[1][:, c, tcols(t)],
                                    ps[:, 2 * (t % 2) + b, 0:384].rearrange("p (k n) -> p k n", k=3)[:, :, 0:n],
                                    xT[0][:, c, tcols(t)].bitcast(F32), ALU.subtract).then_inc(dve_t, 1)

            def token_stats(t):
                n = TROWS[t]
                dve.wait_ge(pe_z, t + 1)
                dve.wait_ge(rstd_ready, t + 1)
                V.bn_stats(bns[0:n, t, 0, :], ps[0:n, 4 + t % 2, 0:D]).then_inc(stat2, 1)
                dve.wait_ge(stat2, 2 * t + 1)
                dve.wait_ge(xn_ready, t + 1)
                V.bn_aggr(mv[0:n, t, :], bns[0:n, t, 0, :]).then_inc(stat2, 1)

            def token_norm(t):
                n = TROWS[t]
                dve.wait_ge(rstd_ready, TILES + t + 1)
                V.tensor_scalar(h[0:n, t, :], ps[0:n, 4 + t % 2, 0:D], mv[0:n, t, 0:1], rstd[0:n, t:t + 1],
                                ALU.subtract, ALU.mult).then_inc(h_part, 1)
                dve.wait_ge(h_part, 2 * t + 1)
                V.tensor_tensor(h[0:n, t, :], h[0:n, t, :], g2b[0:n, :], ALU.mult).then_inc(h_part, 1)
                dve.wait_ge(h_part, 2 * t + 2)
                V.tensor_tensor(h[0:n, t, :], h[0:n, t, :], pet[0:n, t, :], ALU.add).then_inc(h_ready, 1)

            def h_lo(t):
                n = TROWS[t]
                dve.wait_ge(act_ht, t + 1)
                V.tensor_tensor(hT[1][:, :, tcols(t)],
                                ps[:, 6 + t % 2, 0:D].rearrange("p (k n) -> p k n", k=DC)[:, :, 0:n],
                                hT[0][:, :, tcols(t)].bitcast(F32), ALU.subtract).then_inc(dve_ht, 1)

            patch_norm(0)
            scale_tok_weights()
            for t in range(1, TILES):
                patch_norm(t)
            for t in range(TILES):
                patch_apply(t)
                patches_lo(t)
                if t >= 1:
                    token_stats(t - 1)
                if t >= 2:
                    token_norm(t - 2)
                if t >= 3:
                    h_lo(t - 3)
            V.tensor_tensor(lprod[:, :].rearrange("p (i h) -> p i h", i=2), lam4[:, :, 0, :], lam4[:, :, 1, :],
                            ALU.mult).then_inc(lam_prod, 1)
            dve.wait_ge(ld_mask, 16)
            V.tensor_copy(mask[:], mask_raw[:]).then_inc(mask_ready, 1)
            token_stats(TILES - 1)
            token_norm(TILES - 2)
            h_lo(2)
            token_norm(TILES - 1)
            h_lo(3)
            h_lo(4)
            dve.wait_ge(lam_exp, 1)
            V.tensor_tensor(nlam[:], lexp[:, HEADS:2 * HEADS], lexp[:, 0:HEADS], ALU.subtract).then_inc(lam_part, 1)
            dve.wait_ge(lam_part, 1)
            V.tensor_scalar(nlam[:], nlam[:], -LAMBDA_INIT, None, ALU.add).then_inc(lam_ready, 1)
            dve.wait_ge(lam_ready, 1)
            V.tensor_copy(wgs[0][:], wgr[:]).then_inc(wg_split, 1)
            dve.wait_ge(wg_split, 1)
            V.tensor_tensor(wgs[1][:], wgr[:], wgs[0][:].bitcast(F32), ALU.subtract).then_inc(wg_split, 1)

            s_view = ps[0:GRP, 4:6, 0:HALF].rearrange("p j (g n) -> p j g n", g=GRPS)
            p_view = prob[:, :, :].rearrange("p (j g) n -> p j g n", j=2)

            def stats_view(a):
                return a[:, :].rearrange("p (j g) -> p j g", j=2)

            def row_max(u, it):
                dve.wait_ge(pe_s, u + 1 + 4 * it)
                for j in range(2):
                    V.tensor_reduce(smax[:, GRPS * j:GRPS * j + GRPS], s_view[:, j, :, :], AX_X, ALU.max).then_inc(dve_max, 1)

            def subtract_max(u, it):
                dve.wait_ge(dve_max, 2 * u + 2 + 8 * it)
                if u >= 1:
                    dve.wait_ge(pool_attn, u + 4 * it)
                for j in range(2):
                    l = V.tensor_tensor(p_view[:, j, :, :], s_view[:, j, :, :],
                                        stats_view(smax)[:, j, :].unsqueeze(2).broadcast_to([GRP, GRPS, GRP]), ALU.subtract)
                l.then_inc(dve_sub, 1)

            def row_scale(u, it):
                dve.wait_ge(act_exp, u + 1 + 4 * it)
                V.tensor_reduce(ssum[:], prob[:], AX_X, ALU.add).then_inc(dve_sum, 1)
                dve.wait_ge(dve_sum, u + 1 + 4 * it)
                V.reciprocal(rsum[:], ssum[:]).then_inc(dve_rec, 1)
                dve.wait_ge(dve_rec, u + 1 + 4 * it)
                hcol = u // 2 if isinstance(it, int) else bass.ds(u // 2 + 2 * it, 1)
                lam = nlam[0:GRP, u // 2:u // 2 + 1] if isinstance(it, int) else nlam[0:GRP, hcol]
                V.tensor_scalar(rsum[:, GRPS:2 * GRPS], rsum[:, GRPS:2 * GRPS], lam, None, ALU.mult).then_inc(dve_r, 1)

            def proj_lo(u, it, j):
                dve.wait_ge(act_q, 4 * u + j + 1 + 16 * it)
                V.tensor_tensor(qkT[1][:, j, :], ps[:, j, 0:HALF], qkT[0][:, j, :].bitcast(F32),
                                ALU.subtract).then_inc(dve_q, 1)

            def add_tiles(hd, it, tiles):
                for t in tiles:
                    n = TROWS[t]
                    if t == 0:
                        dve.wait_ge(pool_rinv, hd + 1 + 2 * it)
                        if hd >= 1:
                            dve.wait_ge(dve_f, 5 * hd + 10 * it)
                    dve.wait_ge(pe_f, 5 * hd + t + 1 + 10 * it)
                    V.scalar_tensor_tensor(h[0:n, t, :], ps[0:n, (6, 7, 6, 7, 6)[t], 0:D], rinv[0:n, t:t + 1], h[0:n, t, :],
                                           ALU.mult, ALU.add).then_inc(dve_f, 1)

            def step(s, it=0):
                if 0 <= s < UNITS:
                    row_max(s, it)
                if s + 1 < UNITS:
                    proj_lo(s + 1, it, 0)
                    proj_lo(s + 1, it, 1)
                if 1 <= s <= UNITS:
                    dve.wait_ge(act_pt, s + 4 * it)
                    V.tensor_tensor(aT[1][:], ps[0:GRP, 6, 0:HALF], aT[0][:].bitcast(F32), ALU.subtract).then_inc(dve_pt, 1)
                if 0 <= s < UNITS:
                    subtract_max(s, it)
                if s + 1 < UNITS:
                    proj_lo(s + 1, it, 2)
                    proj_lo(s + 1, it, 3)
                if s % 2 == 1 and s >= 3:
                    hd = (s - 3) // 2
                    dve.wait_ge(pe_stat, hd + 1 + 2 * it)
                    if hd >= 1:
                        dve.wait_ge(pool_rinv, hd + 2 * it)
                    c = 1.0 / (OUT_C * OUT_C)
                    V.tensor_scalar(ms[:, 0:4], ps[:, 7, 0:4], c / D, EPS * c, ALU.mult, ALU.add)
                    V.tensor_scalar(ms[0:64, 4:5], ps[0:64, 7, 4:5], c / D, EPS * c, ALU.mult, ALU.add).then_inc(dve_stat, 1)
                if 1 <= s <= UNITS:
                    for k in range(DC):
                        dve.wait_ge(act_ax, 2 * (s - 1) + k + 1 + 8 * it)
                        V.tensor_tensor(axT[1][:, k, :], ps[:, k, 0:HALF], axT[0][:, k, :].bitcast(F32),
                                        ALU.subtract).then_inc(dve_ax, 1)
                if 0 <= s < UNITS:
                    row_scale(s, it)
                if s >= 3:
                    if s % 2 == 1:
                        add_tiles((s - 3) // 2, it, (0, 1, 2))
                    else:
                        add_tiles((s - 4) // 2, it, (3, 4))
                if 1 <= s <= UNITS:
                    u = s - 1
                    cols = slice(HALF * (u % 2), HALF * (u % 2) + HALF)
                    for e in range(DC):
                        dve.wait_ge(act_o, 2 * u + e + 1 + 8 * it)
                        V.scalar_tensor_tensor(oT[1][:, (u // 2) % 2, e, cols], ps[:, 2 + e, 0:HALF], rms[:, e:e + 1],
                                               oT[0][:, (u // 2) % 2, e, cols].bitcast(F32),
                                               ALU.mult, ALU.subtract).then_inc(dve_o, 1)

            for s in range(-1, 4):
                step(s)
            with dve.Fori(0, 2) as i:
                for r in range(4):
                    step(4 + r, i)

            def split12_hi(c, it=0):
                m = up_rows(c)
                if c >= 2:
                    dve.wait_ge(pe_up, 4 * (c - 1) + 8 * it)
                dve.wait_ge(ld_12[c % 2], 16 * (c // 2 + 1 + it))
                V.tensor_copy(w12s[0][:, c % 2, :, :, 0:m], r12[:, c % 2, :, :, 0:m]).then_inc(hi_12, 1)

            def split3_hi(c, it=0):
                m = up_rows(c)
                if c >= 2:
                    dve.wait_ge(pe_dn, 2 * (c - 1) + 4 * it)
                dve.wait_ge(ld_3[c % 2], 16 * (c // 2 + 1 + it))
                V.tensor_copy(w3s[0][0:m, c % 2, :], r3[0:m, c % 2, :]).then_inc(hi_3, 1)

            for s in range(12, 16):
                step(s)
            dve.wait_ge(dve_ht, TILES)
            split12_hi(0)
            split12_hi(1)
            split3_hi(0)
            step(16)
            step(17)
            step(18)

            def norm_stats(t, start, done):
                n = TROWS[t]
                V.bn_stats(bns[0:n, t, 0, :], h[0:n, t, :]).then_inc(done, 1)
                dve.wait_ge(done, start + 2 * t + 1)
                V.bn_aggr(mv[0:n, t, :], bns[0:n, t, 0, :]).then_inc(done, 1)

            dve.wait_ge(dve_f, 5 * HEADS)
            for t in range(TILES):
                norm_stats(t, 0, stat3)
            for t in range(TILES):
                n = TROWS[t]
                dve.wait_ge(rstd_ready, 2 * TILES + t + 1)
                V.tensor_scalar(h[0:n, t, :], h[0:n, t, :], mv[0:n, t, 0:1], rstd[0:n, t:t + 1],
                                ALU.subtract, ALU.mult).then_inc(h2_ready, 1)
            for t in range(TILES):
                n = TROWS[t]
                dve.wait_ge(act_h2t, t + 1)
                V.tensor_tensor(h2T[1][:, :, tcols(t)],
                                ps[:, 4 + t % 2, 0:D].rearrange("p (k n) -> p k n", k=DC)[:, :, 0:n],
                                h2T[0][:, :, tcols(t)].bitcast(F32), ALU.subtract).then_inc(dve_h2t, 1)

            def route():
                dve.wait_ge(pe_route, 1)
                dve.wait_ge(iota_ready, 1)
                V.tensor_copy(logit[:, 0:4, :], ps[:, 6, 0:32].rearrange("p (t e) -> p t e", e=EXPERTS))
                V.tensor_copy(logit[0:64, 4, :], ps[0:64, 6, 32:40]).then_inc(dve_small, 1)
                dve.wait_ge(dve_small, 1)
                for t in range(TILES):
                    l = V.max(top[:, t, :], logit[:, t, :])
                l.then_inc(dve_small, 1)
                dve.wait_ge(dve_small, 2)
                V.tensor_tensor(prb[:, :, 0:1], top[:, :, 1:2], top[:, :, 0:1], ALU.subtract).then_inc(dve_small, 1)
                for t in range(TILES):
                    l = V.max_index(topi[:, t, :], top[:, t, :], logit[:, t, :])
                l.then_inc(dve_small, 1)
                dve.wait_ge(dve_small, 4)
                V.tensor_copy(topf[:], topi[:, :, 0:2]).then_inc(dve_small, 1)
                dve.wait_ge(act_small, 1)
                V.tensor_scalar(prb[:, :, 2:3], prb[:, :, 1:2], 1.0, None, ALU.add).then_inc(dve_small, 1)
                dve.wait_ge(dve_small, 6)
                V.reciprocal(prb[:, :, 2:3], prb[:, :, 2:3]).then_inc(dve_small, 1)
                dve.wait_ge(dve_small, 7)
                V.tensor_tensor(prb[:, :, 3:4], prb[:, :, 1:2], prb[:, :, 2:3], ALU.mult).then_inc(dve_small, 1)
                dve.wait_ge(dve_small, 8)
                for t in range(TILES):
                    for i in range(2):
                        l = V.tensor_scalar(gate[:, i, t, :], iota[:], topf[:, t, i:i + 1], prb[:, t, 2 + i:3 + i],
                                            ALU.is_equal, ALU.mult)
                l.then_inc(dve_small, 1)
                dve.wait_ge(dve_small, 9)
                V.tensor_tensor(gate[:, 0, :, :], gate[:, 0, :, :], gate[:, 1, :, :], ALU.add).then_inc(gate_ready, 1)

            def hidden(v, it=0):
                m = up_rows(v // 2)
                if v < 2 * SHARED_CHUNKS:
                    dve.wait_ge(act_sil, v + 1 + 4 * it)
                else:
                    dve.wait_ge(pool_gate, v - 2 * SHARED_CHUNKS + 1 + 4 * it)
                dve.wait_ge(pe_up, 2 * v + 2 + 8 * it)
                if v >= 2:
                    dve.wait_ge(act_h, v - 1 + 4 * it)
                    dve.wait_ge(dve_hl, v - 1 + 4 * it)
                V.tensor_tensor(hraw[0:m, v % 2, :], ps[0:m, 2 * (v % 2) + 1, 0:HALF], sil[0:m, v % 2, :],
                                ALU.mult).then_inc(dve_h, 1)

            def hidden_lo(v, it=0):
                m = up_rows(v // 2)
                dve.wait_ge(act_h, v + 1 + 4 * it)
                V.tensor_tensor(hh[1][0:m, v % 2, :], hraw[0:m, v % 2, :], hh[0][0:m, v % 2, :].bitcast(F32),
                                ALU.subtract).then_inc(dve_hl, 1)

            def ffn_step(v, it=0):
                if v < 2 * CHUNKS:
                    hidden(v, it)
                if v >= 1:
                    hidden_lo(v - 1, it)
                if v % 2 == 1:
                    if v // 2 + 2 < CHUNKS:
                        split12_hi(v // 2 + 2, it)
                    if v // 2 + 1 < CHUNKS:
                        split3_hi(v // 2 + 1, it)

            route()
            ffn_step(0)
            dve.wait_ge(pe_gt, 1)
            V.tensor_copy(gateT[:, 0:384], ps[0:EXPERTS, 6, 0:384])
            V.tensor_copy(gateT[:, 384:TOK], ps[0:EXPERTS, 7, 0:192]).then_inc(gt_ready, 1)
            for v in range(1, 2 * SHARED_CHUNKS):
                ffn_step(v)
            with dve.Fori(0, 10) as i:
                for r in range(4):
                    ffn_step(2 * SHARED_CHUNKS + r, i)
            for v in range(52, 57):
                ffn_step(v)
            dve.wait_ge(pe_dn, 2 * CHUNKS)
            for k in range(DC):
                V.tensor_copy(yT[:, k, 0:HALF], ps[:, 4 + k, 0:HALF]).then_inc(y_ready, 1)
            for t in range(TILES):
                n = TROWS[t]
                dve.wait_ge(pe_yt, t + 1)
                V.tensor_tensor(h[0:n, t, :], ps[0:n, t % 4, 0:D], h[0:n, t, :], ALU.add).then_inc(y_tok, 1)
                dve.wait_ge(y_tok, t + 1)
                norm_stats(t, 0, stat4)
            for t in range(TILES):
                n = TROWS[t]
                dve.wait_ge(rstd_ready, 3 * TILES + t + 1)
                V.tensor_scalar(h[0:n, t, :], h[0:n, t, :], mv[0:n, t, 0:1], rstd[0:n, t:t + 1],
                                ALU.subtract, ALU.mult).then_inc(y_done, 1)

        @block.gpsimd
        def _(pool):
            G = nc.gpsimd
            steps = [0]

            def lo(o, i, hi, done):
                return G.tensor_tensor(o, i, hi.bitcast(F32), ALU.subtract).then_inc(done, 1)

            def inv_std(t, done, start):
                pool.wait_ge(done, start + 2 * t + 2)
                n = TROWS[t]
                G.tensor_scalar(mv[0:n, t, 1:2], mv[0:n, t, 1:2], EPS, 1.0, ALU.add, ALU.mult).then_inc(stat3a, 1)
                steps[0] += 1
                pool.wait_ge(stat3a, steps[0])
                G.tensor_tensor(rstd[0:n, t:t + 1], mv[0:n, t, 1:2], mhalf[0:n, 0:1], ALU.pow).then_inc(rstd_ready, 1)

            G.iota(iota[:], pattern=[[1, EXPERTS]], base=0, channel_multiplier=0,
                   allow_small_or_imprecise_dtypes=True).then_inc(iota_ready, 1)
            pool.wait_ge(mem_ready, 1)
            inv_std(0, stat1, 0)
            pool.wait_ge(tw_hi, 1)
            inv_std(1, stat1, 0)
            inv_std(2, stat1, 0)
            inv_std(3, stat1, 0)
            inv_std(4, stat1, 0)
            lo(tws[1][:], tw[:], tws[0][:], tw_lo)
            for t in range(3):
                inv_std(t, stat2, 0)
            pool.wait_ge(hi_qk, 1)
            lo(qks[1][:, 0, :], qk_raw[:, 0, :], qks[0][:, 0, :], lo_qk)
            for t in range(3, TILES):
                inv_std(t, stat2, 0)
            pool.wait_ge(ld_xg, 16)
            G.tensor_copy(xg[0][:], xg_raw).then_inc(xg_hi, 1)
            pool.wait_ge(xg_hi, 1)
            lo(xg[1][:], xg_raw, xg[0][:], xg_lo)

            def step(s, it=0):
                if s % 2 == 0 and (s + 2) // 2 < HEADS:
                    hd = (s + 2) // 2
                    pool.wait_ge(hi_qk, hd + 1 + 2 * it)
                    lo(qks[1][:, hd % 2, :], qk_raw[:, hd % 2, :], qks[0][:, hd % 2, :], lo_qk)
                if s % 2 == 1 and 0 <= s - 1 < UNITS:
                    hd = (s - 1) // 2
                    pool.wait_ge(hi_v, hd + 1 + 2 * it)
                    lo(vs[1][:, hd % 2, :], v_raw[:, hd % 2, :], vs[0][:, hd % 2, :], lo_v)
                    pool.wait_ge(hi_o, hd + 1 + 2 * it)
                    lo(os_[1][:, hd % 2, :], o_raw[:, hd % 2, :], os_[0][:, hd % 2, :], lo_o)
                if s % 2 == 1 and s >= 3:
                    hd = (s - 3) // 2
                    pool.wait_ge(dve_stat, hd + 1 + 2 * it)
                    if hd >= 1:
                        pool.wait_ge(dve_f, 5 * hd + 10 * it)
                    G.tensor_tensor(rinv[:], ms[:], mhalf[:], ALU.pow).then_inc(pool_rinv, 1)
                if 0 <= s < UNITS:
                    pool.wait_ge(dve_r, s + 1 + 4 * it)
                    G.tensor_tensor(prob[:], prob[:], rsum[:, :].unsqueeze(2).broadcast_to([GRP, 2 * GRPS, GRP]),
                                    ALU.mult).then_inc(pool_mul, 1)
                    pool.wait_ge(pool_mul, s + 1 + 4 * it)
                    if s >= 1:
                        pool.wait_ge(pe_pt, s + 4 * it)
                    G.tensor_tensor(attn[:], prob[:, 0:GRPS, :], prob[:, GRPS:2 * GRPS, :], ALU.add).then_inc(pool_attn, 1)
                if 1 <= s <= UNITS:
                    u = s - 1
                    pool.wait_ge(act_o, 2 * u + 2 + 8 * it)
                    G.tensor_tensor(sqs[:, (u // 2) % 2, HALF * (u % 2):HALF * (u % 2) + HALF], sq[:, 0, :], sq[:, 1, :],
                                    ALU.add).then_inc(pool_sq, 1)

            for s in range(0, 4):
                step(s)
            with pool.Fori(0, 2) as i:
                for r in range(4):
                    step(4 + r, i)
            for s in range(12, 16):
                step(s)
            pool.wait_ge(dve_ht, TILES)

            def split12_lo(c, it=0):
                m = up_rows(c)
                pool.wait_ge(hi_12, c + 1 + 2 * it)
                lo(w12s[1][:, c % 2, :, :, 0:m], r12[:, c % 2, :, :, 0:m], w12s[0][:, c % 2, :, :, 0:m], lo_12)

            def split3_lo(c, it=0):
                m = up_rows(c)
                pool.wait_ge(hi_3, c + 1 + 2 * it)
                lo(w3s[1][0:m, c % 2, :], r3[0:m, c % 2, :], w3s[0][0:m, c % 2, :], lo_3)

            step(16)
            step(17)
            split12_lo(0)
            split12_lo(1)
            split3_lo(0)
            for t in range(TILES):
                inv_std(t, stat3, 0)

            def ffn_step(v, it=0):
                if v >= 2 * SHARED_CHUNKS:
                    c = v // 2
                    pool.wait_ge(act_sil, v + 1 + 4 * it)
                    if v % 2 == 0:
                        g = c - SHARED_CHUNKS
                        gate_loads(g, it)
                    cols = slice(HALF * (v % 2), HALF * (v % 2) + HALF)
                    G.tensor_tensor(sil[:, v % 2, :], sil[:, v % 2, :], gates[:, (c - SHARED_CHUNKS) % 4, cols],
                                    ALU.mult).then_inc(pool_gate, 1)
                if v % 2 == 1:
                    if v // 2 + 2 < CHUNKS:
                        split12_lo(v // 2 + 2, it)
                    if v // 2 + 1 < CHUNKS:
                        split3_lo(v // 2 + 1, it)

            def gate_loads(g, it):
                pool.wait_ge(ld_g[g % 4], 64 * (g // 4 + 1 + it))

            for v in range(0, 2 * SHARED_CHUNKS):
                ffn_step(v)

            def ffn_step8(v, i):
                c = v // 2
                cols = slice(HALF * (v % 2), HALF * (v % 2) + HALF)
                pool.wait_ge(act_sil, v + 1 + 8 * i)
                if v % 2 == 0:
                    gate_loads(c - SHARED_CHUNKS, i)
                G.tensor_tensor(sil[:, v % 2, :], sil[:, v % 2, :], gates[:, (c - SHARED_CHUNKS) % 4, cols],
                                ALU.mult).then_inc(pool_gate, 1)
                if v % 2 == 1:
                    split12_lo(c + 2, 2 * i)
                    split3_lo(c + 1, 2 * i)

            with pool.Fori(0, 5) as i:
                for r in range(8):
                    ffn_step8(2 * SHARED_CHUNKS + r, i)
            for v in range(52, 56):
                ffn_step(v)
            for t in range(TILES):
                inv_std(t, stat4, 0)


def kernel(**inputs):
    import numpy as np
    import concourse.bacc as bacc
    from concourse.bass_utils import run_bass_kernel_spmd as run

    f = {k: np.asarray(v) for k, v in inputs.items()}
    c = np.ascontiguousarray
    a = {}
    a["x"] = c(f["x"].reshape(16, 3, 6, 16, 6, 16).transpose(0, 2, 4, 1, 3, 5).reshape(TOK, PATCH))
    a["tokw"] = c(f["L0_tok_W"].T.reshape(KC, P, D).transpose(1, 0, 2))
    a["consts"] = c(np.concatenate([
        f["L0_tok_ln1_w"].reshape(KC, P).T, f["L0_attn_rms_scale"].reshape(2, P).T,
        f["L0_attn_lambda_q1"].T, f["L0_attn_lambda_k1"].T, f["L0_attn_lambda_q2"].T, f["L0_attn_lambda_k2"].T], axis=1))
    omega = np.arange(D // 4, dtype=np.float32) / np.float32(D // 4 - 1)
    omega = (np.float32(1.0) / np.float32(10000.0) ** omega).astype(np.float32)
    yy, xx = np.meshgrid(np.arange(6, dtype=np.float32), np.arange(6, dtype=np.float32), indexing="ij")
    yo, xo = yy.reshape(-1)[:, None] * omega[None, :], xx.reshape(-1)[:, None] * omega[None, :]
    a["pe_tab"] = c(np.tile(np.concatenate([np.sin(xo), np.cos(xo), np.sin(yo), np.cos(yo)], axis=1), (IMAGES, 1)).astype(np.float32))
    a["g2"] = c(f["L0_tok_ln2_w"].reshape(1, D))

    def head_in(w):
        return w.reshape(HEADS, D, DC, P).transpose(0, 3, 2, 1).reshape(HEADS, P, DC * D)

    a["wqk"] = c(np.concatenate([head_in(f["L0_attn_Wq"]), head_in(f["L0_attn_Wk"])], axis=2))
    a["wv"] = c(head_in(f["L0_attn_Wv"]))
    a["wo"] = c(f["L0_attn_Wo"].T.reshape(HEADS, DC, P, D).transpose(0, 2, 1, 3).reshape(HEADS, P, DC * D))
    a["ident"] = np.eye(P, dtype=np.float32)
    masks = np.zeros((2, GRP + HALF), np.float32)
    for i in range(2):
        masks[i, IMG_TOK * i:IMG_TOK * (i + 1)] = 1.0
        for g in range(GRPS):
            masks[i, GRP + GRP * g + IMG_TOK * (1 - i):GRP + GRP * g + IMG_TOK * (2 - i)] = -1e30
    a["masks"] = masks
    a["wg"] = c(f["L0_ffn_Wg"].reshape(DC, P, EXPERTS).transpose(1, 0, 2))
    r1 = np.concatenate([f["L0_ffn_Ws1"].T, f["L0_ffn_W1"].transpose(0, 2, 1).reshape(-1, D)])
    r2 = np.concatenate([f["L0_ffn_Ws2"].T, f["L0_ffn_W2"].transpose(0, 2, 1).reshape(-1, D)])
    r3 = np.concatenate([f["L0_ffn_Ws3"], f["L0_ffn_W3"].reshape(-1, D)])

    def chunked(r, m):
        return r.reshape(-1, m, DC, P).transpose(0, 3, 2, 1)

    a["s12"] = c(np.stack([chunked(r1[:SHARED0], SHARED0)[0], chunked(r2[:SHARED0], SHARED0)[0]], axis=1))
    a["s3"] = c(r3[:SHARED0])
    a["w12"] = c(np.stack([chunked(r1[SHARED0:], P), chunked(r2[SHARED0:], P)], axis=2).reshape(CHUNKS - 1, P, 4 * P))
    a["w3"] = c(r3[SHARED0:].reshape(CHUNKS - 1, P, D))

    nc = bacc.Bacc("TRN2", target_bir_lowering=False, num_devices=1)
    order = ["x", "tokw", "consts", "pe_tab", "g2", "wqk", "wv", "wo", "ident", "masks", "wg", "s12", "s3", "w12", "w3"]
    args = [nc.dram_tensor(f"in_{n}", a[n].shape, F32, kind="ExternalInput").ap() for n in order]
    out = nc.dram_tensor("out", (TOK, D), F32, kind="ExternalOutput").ap()
    build(nc, *args, out)
    r = run(nc, [{f"in_{n}": a[n] for n in order}], core_ids=[0])
    return r.results[0]["out"].reshape(IMAGES, IMG_TOK, D)
```

```python
from contextlib import ExitStack

import concourse.bass as bass
from concourse import mybir

F32 = mybir.dt.float32
F32R = mybir.dt.float32r
U32 = mybir.dt.uint32
ACT = mybir.ActivationFunctionType
ALU = mybir.AluOpType
AX_X = mybir.AxisListType.X

P = 128
IMAGES = 16
IMG_TOK = 36
TOK = IMAGES * IMG_TOK
TILES = 5
TROWS = [min(P, TOK - P * t) for t in range(TILES)]
D = 256
DC = D // P
PATCH = 768
KC = PATCH // P
HEADS = 8
HALF = TOK // 2
GRP = 2 * IMG_TOK
GRPS = HALF // GRP
UNITS = 2 * HEADS
EXPERTS = 8
SHARED0 = 64
CHUNKS = 28
SHARED_CHUNKS = 6
EPS = 1e-5
LAMBDA_INIT = 0.8 - 0.6 * 0.7408182206817179
SCALE = 1.0 / 128 ** 0.5
OUT_C = 1.0 - LAMBDA_INIT


def build(nc, x, tokw, consts, pe_tab, g2, wqk, wv, wo, ident_d, masks, wg, s12, s3, w12, w3, out):
    ctx = ExitStack()
    with ctx:
        def sb(name, shape, dt=F32):
            return ctx.enter_context(nc.sbuf_tensor(name, shape, dt))

        def sem(name):
            return ctx.enter_context(nc.semaphore(name))

        region = sb("region", [P, TILES * PATCH])
        xr = region[:, :].rearrange("p (t f) -> p t f", t=TILES)
        xg_raw = region[0:GRP, 0:2 * GRPS * D].rearrange("p (g d) -> p g d", d=D)
        gates = region[:, 0:4 * TOK].rearrange("p (s n) -> p s n", s=4)
        split_region = sb("split_region", [P, 2 * KC * TOK], F32R)
        xT = [split_region[:, i * KC * TOK:(i + 1) * KC * TOK].rearrange("p (k n) -> p k n", k=KC) for i in range(2)]
        h2T = [split_region[:, i * DC * TOK:(i + 1) * DC * TOK].rearrange("p (k n) -> p k n", k=DC) for i in range(2)]
        base12 = 2 * DC * TOK
        w12s = [split_region[:, base12 + 1024 * i:base12 + 1024 * (i + 1)].rearrange("p (s w k m) -> p s w k m", s=2, w=2, k=DC)
                for i in range(2)]
        base3 = base12 + 2048
        w3s = [split_region[:, base3 + 512 * i:base3 + 512 * (i + 1)].rearrange("p (s n) -> p s n", s=2) for i in range(2)]
        tw = sb("tw", [P, KC, D])
        tws = [sb(f"tws{i}", [P, KC, D], F32R) for i in range(2)]
        cst = sb("cst", [P, KC + 2 + 4 * HEADS])
        gam1 = cst[:, 0:KC]
        rms = cst[:, KC:KC + 2]
        lam4 = cst[:, KC + 2:KC + 2 + 4 * HEADS].rearrange("p (i j h) -> p i j h", i=2, j=2)
        ident = sb("ident", [P, P])
        ones = sb("ones", [P, P])
        pet = sb("pet", [P, TILES, D])
        g2b = sb("g2b", [P, D])
        mask_raw = sb("mask_raw", [2, GRP + HALF])
        mask = sb("mask", [2, GRP + HALF], F32R)
        bns = sb("bns", [P, TILES, 2, 6])
        mv = sb("mv", [P, TILES, 2])
        rstd = sb("rstd", [P, TILES])
        mhalf = sb("mhalf", [P, TILES])
        h = sb("h", [P, TILES, D])
        hT = [sb(f"hT{i}", [P, DC, TOK], F32R) for i in range(2)]
        xg = [sb(f"xg{i}", [GRP, 2 * GRPS, D], F32R) for i in range(2)]
        lprod = sb("lprod", [P, 2 * HEADS])
        lexp = sb("lexp", [P, 2 * HEADS])
        nlam = sb("nlam", [P, HEADS])
        qk_raw = sb("qk_raw", [P, 2, 4 * D])
        v_raw = sb("v_raw", [P, 2, 2 * D])
        o_raw = sb("o_raw", [P, 2, 2 * D])
        qks = [sb(f"qks{i}", [P, 2, 4 * D], F32R) for i in range(2)]
        vs = [sb(f"vs{i}", [P, 2, 2 * D], F32R) for i in range(2)]
        os_ = [sb(f"os{i}", [P, 2, 2 * D], F32R) for i in range(2)]
        qkT = [sb(f"qkT{i}", [P, 4, HALF], F32R) for i in range(2)]
        prob = sb("prob", [GRP, 2 * GRPS, GRP])
        smax = sb("smax", [GRP, 2 * GRPS])
        ssum = sb("ssum", [GRP, 2 * GRPS])
        rsum = sb("rsum", [GRP, 2 * GRPS])
        attn = sb("attn", [GRP, GRPS, GRP])
        aT = [sb(f"aT{i}", [GRP, HALF], F32R) for i in range(2)]
        axT = [sb(f"axT{i}", [P, DC, HALF], F32R) for i in range(2)]
        oT = [sb(f"oT{i}", [P, 2, DC, TOK], F32R) for i in range(2)]
        sq = sb("sq", [P, DC, HALF])
        sqs = sb("sqs", [P, 2, TOK])
        ms = sb("ms", [P, TILES])
        rinv = sb("rinv", [P, TILES])
        wgr = sb("wgr", [P, DC, EXPERTS])
        wgs = [sb(f"wgs{i}", [P, DC, EXPERTS], F32R) for i in range(2)]
        logit = sb("logit", [P, TILES, EXPERTS])
        top = sb("top", [P, TILES, 8])
        topi = sb("topi", [P, TILES, 8], U32)
        topf = sb("topf", [P, TILES, 2])
        iota = sb("iota", [P, EXPERTS])
        prb = sb("prb", [P, TILES, 4])
        gate = sb("gate", [P, 2, TILES, EXPERTS])
        gateT = sb("gateT", [EXPERTS, TOK])
        r12 = sb("r12", [P, 2, 2, DC, P])
        r3 = sb("r3", [P, 2, D])
        ffn_rows = pet[:, :, :].rearrange("p t d -> p (t d)")
        sil = ffn_rows[:, 0:TOK].rearrange("p (s n) -> p s n", s=2)
        hraw = ffn_rows[:, TOK:2 * TOK].rearrange("p (s n) -> p s n", s=2)
        hh = [a[:, :, :].rearrange("p k d -> p (k d)")[:, 0:TOK].rearrange("p (s n) -> p s n", s=2) for a in tws]
        yT = tw[:, :, :].rearrange("p k d -> p (k d)")[:, 0:DC * TOK].rearrange("p (k n) -> p k n", k=DC)

        ax = tw[:, :, :].rearrange("p k d -> p (k d)")[0:GRP, 0:GRPS * D].rearrange("p (g d) -> p g d", g=GRPS)

        ps = ctx.enter_context(nc.psum_tensor("ps", [P, 8, 512], F32))

        h_dram = nc.dram_tensor("h_scratch", (TOK, D), F32, kind="Internal").ap()
        g_dram = nc.dram_tensor("gate_scratch", (EXPERTS * 11, TOK), F32, kind="Internal").ap()

        ld_const = sem("ld_const")
        ld_mask = sem("ld_mask")
        ld_tw = sem("ld_tw")
        h_stored = sem("h_stored")
        ld_xg = sem("ld_xg")
        g_stored = sem("g_stored")
        out_stored = sem("out_stored")
        mem_ready = sem("mem_ready")
        stat1 = sem("stat1")
        rstd1 = sem("rstd1")
        rstd2 = sem("rstd2")
        rstd3 = sem("rstd3")
        rstd4 = sem("rstd4")
        ld_ident = sem("ld_ident")
        eps_added = sem("eps_added")
        xn_ready = sem("xn_ready")
        pe_t = sem("pe_t")
        act_t = sem("act_t")
        dve_t = sem("dve_t")
        pe_z = sem("pe_z")
        stat2 = sem("stat2")
        h_part = sem("h_part")
        h_ready = sem("h_ready")
        pe_ht = sem("pe_ht")
        act_ht = sem("act_ht")
        dve_ht = sem("dve_ht")
        tw_scaled = sem("tw_scaled")
        tw_hi = sem("tw_hi")
        tw_lo = sem("tw_lo")
        xg_hi = sem("xg_hi")
        xg_lo = sem("xg_lo")
        lam_prod = sem("lam_prod")
        pe_lam = sem("pe_lam")
        lam_exp = sem("lam_exp")
        lam_part = sem("lam_part")
        lam_ready = sem("lam_ready")
        mask_ready = sem("mask_ready")
        wg_split = sem("wg_split")
        pe_q = sem("pe_q")
        act_q = sem("act_q")
        dve_q = sem("dve_q")
        pe_s = sem("pe_s")
        dve_max = sem("dve_max")
        dve_sub = sem("dve_sub")
        act_exp = sem("act_exp")
        dve_sum = sem("dve_sum")
        dve_rec = sem("dve_rec")
        dve_r = sem("dve_r")
        pool_mul = sem("pool_mul")
        pool_attn = sem("pool_attn")
        pe_pt = sem("pe_pt")
        act_pt = sem("act_pt")
        dve_pt = sem("dve_pt")
        pe_av = sem("pe_av")
        act_av = sem("act_av")
        pe_ax = sem("pe_ax")
        act_ax = sem("act_ax")
        dve_ax = sem("dve_ax")
        pe_o = sem("pe_o")
        act_hi = sem("act_hi")
        act_o = sem("act_o")
        dve_o = sem("dve_o")
        pool_sq = sem("pool_sq")
        pe_stat = sem("pe_stat")
        dve_stat = sem("dve_stat")
        pool_rinv = sem("pool_rinv")
        pe_f = sem("pe_f")
        dve_f = sem("dve_f")
        hi_qk = sem("hi_qk")
        lo_qk = sem("lo_qk")
        hi_v = sem("hi_v")
        lo_v = sem("lo_v")
        hi_o = sem("hi_o")
        lo_o = sem("lo_o")
        stat3 = sem("stat3")
        h2_ready = sem("h2_ready")
        pe_h2t = sem("pe_h2t")
        act_h2t = sem("act_h2t")
        dve_h2t = sem("dve_h2t")
        pe_route = sem("pe_route")
        dve_small = sem("dve_small")
        act_small = sem("act_small")
        gate_ready = sem("gate_ready")
        pe_gt = sem("pe_gt")
        gt_ready = sem("gt_ready")
        hi_12 = sem("hi_12")
        lo_12 = sem("lo_12")
        hi_3 = sem("hi_3")
        lo_3 = sem("lo_3")
        pe_up = sem("pe_up")
        act_sil = sem("act_sil")
        pool_gate = sem("pool_gate")
        dve_h = sem("dve_h")
        act_h = sem("act_h")
        dve_hl = sem("dve_hl")
        pe_dn = sem("pe_dn")
        y_ready = sem("y_ready")
        pe_yt = sem("pe_yt")
        y_tok = sem("y_tok")
        stat4 = sem("stat4")
        y_done = sem("y_done")
        iota_ready = sem("iota_ready")
        ld_x = [sem(f"ld_x{t}") for t in range(TILES)]
        ld_qk = [sem(f"ld_qk{i}") for i in range(2)]
        ld_v = [sem(f"ld_v{i}") for i in range(2)]
        ld_o = [sem(f"ld_o{i}") for i in range(2)]
        ld_12 = [sem(f"ld_12_{i}") for i in range(2)]
        ld_3 = [sem(f"ld_3_{i}") for i in range(2)]
        ld_g = [sem(f"ld_g{i}") for i in range(4)]
        block = ctx.enter_context(nc.Block())

        def tcols(t):
            return slice(P * t, P * t + TROWS[t])

        def up_rows(c):
            return SHARED0 if c == 0 else P

        @block.sync
        def _(sp):
            for t in range(TILES):
                sp.dma_start(xr[0:TROWS[t], t, :], x[P * t:P * t + TROWS[t], :]).then_inc(ld_x[t], 16)
                if t == 0:
                    sp.dma_start(ident[:], ident_d).then_inc(ld_ident, 16)
                    sp.dma_start(cst[:], consts).then_inc(ld_tw, 16)
                    sp.dma_start(tw[:], tokw).then_inc(ld_tw, 16)
            sp.dma_start(qk_raw[:, 0, :], wqk[0, :, :]).then_inc(ld_qk[0], 16)
            sp.dma_start(g2b[:], g2.broadcast_to([P, D])).then_inc(ld_const, 16)
            sp.dma_start(pet[:, 0:4, :], pe_tab[0:512, :].rearrange("(t p) d -> p t d", p=P)).then_inc(ld_const, 16)
            sp.dma_start(pet[0:64, 4, :], pe_tab[512:TOK, :]).then_inc(ld_const, 16)
            sp.dma_start(wgr[:], wg).then_inc(ld_const, 16)
            sp.dma_start(mask_raw[:], masks).then_inc(ld_mask, 16)
            sp.dma_start(qk_raw[:, 1, :], wqk[1, :, :]).then_inc(ld_qk[1], 16)
            for i in range(2):
                sp.dma_start(v_raw[:, i, :], wv[i, :, :]).then_inc(ld_v[i], 16)
                sp.dma_start(o_raw[:, i, :], wo[i, :, :]).then_inc(ld_o[i], 16)
            for t in range(TILES):
                sp.wait_ge(h_ready, t + 1)
                sp.dma_start(h_dram[P * t:P * t + TROWS[t], :], h[0:TROWS[t], t, :]).then_inc(h_stored, 16)
            sp.wait_ge(h_stored, 16 * TILES)
            sp.dma_start(xg_raw, h_dram.rearrange("(g p) d -> p g d", p=GRP)).then_inc(ld_xg, 16)
            sp.dma_start(r12[:, 0, :, :, 0:SHARED0], s12).then_inc(ld_12[0], 16)
            sp.dma_start(r3[0:SHARED0, 0, :], s3).then_inc(ld_3[0], 16)
            sp.dma_start(r12[:, 1, :, :, :], w12[0, :, :]).then_inc(ld_12[1], 16)
            sp.dma_start(r3[:, 1, :], w3[0, :, :]).then_inc(ld_3[1], 16)

            def head_pair(i):
                for r in range(2):
                    hd = 2 + 2 * i + r
                    sp.wait_ge(lo_qk, 2 * i + r + 1)
                    sp.dma_start(qk_raw[:, r, :], wqk[bass.ds(hd, 1), :, :].rearrange("a p n -> p (a n)")).then_inc(ld_qk[r], 16)
                    sp.wait_ge(lo_v, 2 * i + r + 1)
                    sp.dma_start(v_raw[:, r, :], wv[bass.ds(hd, 1), :, :].rearrange("a p n -> p (a n)")).then_inc(ld_v[r], 16)
                    sp.wait_ge(lo_o, 2 * i + r + 1)
                    sp.dma_start(o_raw[:, r, :], wo[bass.ds(hd, 1), :, :].rearrange("a p n -> p (a n)")).then_inc(ld_o[r], 16)

            with sp.Fori(0, HEADS // 2 - 1) as i:
                head_pair(i)
            def load_gate(i, r):
                for b in range(4):
                    sp.dma_start(gates[32 * b:32 * b + 32, r, :],
                                 g_dram[bass.ds(4 * i + b, 1), :].broadcast_to([32, TOK])).then_inc(ld_g[r], 16)

            def load_w(c, r):
                sp.wait_ge(lo_12, c - 1)
                sp.dma_start(r12[:, r, :, :, :], w12[bass.ds(c - 1, 1), :, :].rearrange("a p n -> p (a n)")).then_inc(ld_12[r], 16)
                sp.wait_ge(lo_3, c - 1)
                sp.dma_start(r3[:, r, :], w3[bass.ds(c - 1, 1), :, :].rearrange("a p n -> p (a n)")).then_inc(ld_3[r], 16)

            for c in range(2, 5):
                load_w(c, c % 2)
            sp.wait_ge(gt_ready, 1)
            sp.dma_start(g_dram.rearrange("(e k) n -> e k n", k=11),
                         gateT[:, :].unsqueeze(1).broadcast_to([EXPERTS, 11, TOK])).then_inc(g_stored, 16)
            load_w(5, 1)
            sp.wait_ge(g_stored, 16)
            for r in range(4):
                load_gate(r, r)
            for c in range(6, 10):
                load_w(c, c % 2)

            def gate_rest(c, r4):
                sp.wait_ge(pool_gate, 2 * (c - 4 - SHARED_CHUNKS) + 2)
                load_gate(c - SHARED_CHUNKS, r4)
                load_w(c, r4 % 2)

            with sp.Fori(0, 4) as i:
                for r in range(4):
                    gate_rest(10 + 4 * i + r, r)
            for r in range(2):
                gate_rest(26 + r, r)
            for t in range(TILES):
                sp.wait_ge(y_done, t + 1)
                sp.dma_start(out[P * t:P * t + TROWS[t], :], h[0:TROWS[t], t, :]).then_inc(out_stored, 16)
            sp.wait_ge(out_stored, 16 * TILES)

        def mm3(o, lhs, rhs, first, last):
            nc.tensor.matmul(o, lhs[0], rhs[0], start=first, stop=False)
            nc.tensor.matmul(o, lhs[0], rhs[1], start=False, stop=False)
            return nc.tensor.matmul(o, lhs[1], rhs[0], start=False, stop=last)

        @block.tensor
        def _(pe):
            pe.wait_ge(ld_ident, 16)

            def patch_transposes(t):
                n = TROWS[t]
                pe.wait_ge(xn_ready, t + 1)
                if t >= 2:
                    pe.wait_ge(dve_t, 2 * (t - 1))
                for k in range(KC):
                    l = nc.tensor.transpose(ps[:, 2 * (t % 2) + k // 3, P * (k % 3):P * (k % 3) + n],
                                            xr[0:n, t, P * k:P * k + P], ident[0:n, 0:n])
                    if k % 3 == 2:
                        l.then_inc(pe_t, 1)

            def token_product(t):
                n = TROWS[t]
                pe.wait_ge(dve_t, 2 * (t + 1))
                if t == 0:
                    pe.wait_ge(tw_lo, 2)
                if t >= 2:
                    pe.wait_ge(h_ready, t - 1)
                for k in range(KC):
                    l = mm3(ps[0:n, 4 + t % 2, 0:D], [a[:, k, tcols(t)] for a in xT], [a[:, k, :] for a in tws],
                            k == 0, k == KC - 1)
                l.then_inc(pe_z, 1)

            def h_transposes(t):
                n = TROWS[t]
                pe.wait_ge(h_ready, t + 1)
                if t >= 2:
                    pe.wait_ge(dve_ht, t - 1)
                for k in range(DC):
                    l = nc.tensor.transpose(ps[:, 6 + t % 2, P * k:P * k + n], h[0:n, t, P * k:P * k + P], ident[0:n, 0:n])
                l.then_inc(pe_ht, 1)

            def lambda_sums():
                pe.wait_ge(mem_ready, 1)
                pe.wait_ge(lam_prod, 1)
                nc.tensor.matmul(ps[:, 7, 0:2 * HEADS], ones[:, :], lprod[:, :], start=True, stop=True).then_inc(pe_lam, 1)

            patch_transposes(0)
            lambda_sums()
            patch_transposes(1)
            token_product(0)
            patch_transposes(2)
            token_product(1)
            patch_transposes(3)
            token_product(2)
            h_transposes(0)
            patch_transposes(4)
            token_product(3)
            pe.wait_ge(lam_exp, 1)
            h_transposes(1)
            token_product(4)
            h_transposes(2)

            def project(u, it, j):
                hd, hs, bank = u // 2, (u // 2) % 2, j
                if j == 0:
                    pe.wait_ge(lo_qk, hd + 1 + 2 * it)
                    if u <= 1:
                        pe.wait_ge(dve_ht, 3 if u == 0 else TILES)
                if u >= 3:
                    if j < 2:
                        pe.wait_ge(dve_ax, 2 * (u - 3) + j + 1 + 8 * it)
                    else:
                        pe.wait_ge(dve_o, 2 * (u - 3) + j - 1 + 8 * it)
                c0 = (j % 2) * 2 * D + (j // 2) * P
                cols = slice(HALF * (u % 2), HALF * (u % 2) + HALF)
                for k in range(DC):
                    l = mm3(ps[:, bank, 0:HALF], [a[:, hs, c0 + k * D:c0 + k * D + P] for a in qks],
                            [a[:, k, cols] for a in hT], k == 0, k == DC - 1)
                l.then_inc(pe_q, 1)

            def scores(u, it):
                if u == 0:
                    pe.wait_ge(mask_ready, 1)
                pe.wait_ge(dve_q, 4 * u + 4 + 4 * 4 * it)
                if u >= 1:
                    pe.wait_ge(dve_sub, u + 4 * it)
                for j in range(2):
                    nc.tensor.matmul(ps[0:GRP, 4 + j, 0:HALF], mask[:, 0:GRP], mask[:, GRP:GRP + HALF], start=True, stop=False)
                    for g in range(GRPS):
                        c = slice(GRP * g, GRP * g + GRP)
                        l = mm3(ps[0:GRP, 4 + j, c], [a[:, 2 * j, c] for a in qkT], [a[:, 2 * j + 1, c] for a in qkT],
                                False, g == GRPS - 1)
                l.then_inc(pe_s, 1)

            def attn_transpose(s, it):
                u = s - 1
                pe.wait_ge(pool_attn, u + 1 + 4 * it)
                if s >= 4:
                    if s % 2 == 0:
                        pe.wait_ge(dve_f, 5 * ((s - 4) // 2) + 3 + 10 * it)
                    else:
                        pe.wait_ge(dve_f, 5 * ((s - 5) // 2) + 5 + 10 * it)
                for g in range(GRPS):
                    l = nc.tensor.transpose(ps[0:GRP, 6, GRP * g:GRP * g + GRP], attn[:, g, :], ident[0:GRP, 0:GRP])
                l.then_inc(pe_pt, 1)

            def attend(u, it):
                pe.wait_ge(dve_pt, u + 1 + 4 * it)
                if u == 0:
                    pe.wait_ge(xg_lo, 1)
                for b in range(2):
                    if u + 2 < UNITS:
                        pe.wait_ge(dve_q, 4 * (u + 2) + b + 1 + 16 * it)
                    else:
                        pe.wait_ge(dve_ax, 2 * (u - 1) + b + 1)
                    for g in (2 * b, 2 * b + 1):
                        l = mm3(ps[0:GRP, b, D * (g % 2):D * (g % 2) + D], [a[:, GRP * g:GRP * g + GRP] for a in aT],
                                [a[:, GRPS * (u % 2) + g, :] for a in xg], True, True)
                    l.then_inc(pe_av, 1)

            def ax_transposes(u, it):
                pe.wait_ge(act_av, 2 * u + 2 + 8 * it)
                for k in range(DC):
                    for g in range(GRPS):
                        l = nc.tensor.transpose(ps[:, k, GRP * g:GRP * g + GRP], ax[:, g, P * k:P * k + P],
                                                ident[0:GRP, 0:GRP])
                    l.then_inc(pe_ax, 1)

            def values(u, it):
                hd, hs = u // 2, (u // 2) % 2
                pe.wait_ge(dve_ax, 2 * u + 2 + 8 * it)
                if u % 2 == 0:
                    pe.wait_ge(lo_v, hd + 1 + 2 * it)
                for e in range(DC):
                    if u + 2 < UNITS:
                        pe.wait_ge(dve_q, 4 * (u + 2) + e + 3 + 16 * it)
                    else:
                        pe.wait_ge(dve_o, 2 * (u - 1) + e + 1)
                    for k in range(DC):
                        l = mm3(ps[:, 2 + e, 0:HALF], [a[:, hs, k * D + P * e:k * D + P * e + P] for a in vs],
                                [a[:, k, :] for a in axT], k == 0, k == DC - 1)
                    l.then_inc(pe_o, 1)

            def square_sums(hd, it):
                pe.wait_ge(pool_sq, 2 * hd + 2 + 4 * it)
                if hd >= 1:
                    pe.wait_ge(dve_f, 5 * hd + 10 * it)
                for t in range(TILES):
                    l = nc.tensor.matmul(ps[0:TROWS[t], 7, t:t + 1], sqs[:, hd % 2, tcols(t)], ones[:, 0:1],
                                         start=True, stop=True)
                l.then_inc(pe_stat, 1)

            def output_tiles(hd, it, tiles):
                for t in tiles:
                    n = TROWS[t]
                    if t == 0:
                        pe.wait_ge(lo_o, hd + 1 + 2 * it)
                        pe.wait_ge(dve_o, 4 * hd + 4 + 8 * it)
                        if hd >= 1:
                            pe.wait_ge(dve_f, 5 * hd + 10 * it)
                    elif t == 1:
                        pe.wait_ge(dve_stat, hd + 1 + 2 * it)
                    else:
                        pe.wait_ge(dve_f, 5 * hd + t - 1 + 10 * it)
                    bank = (6, 7, 6, 7, 6)[t]
                    for k in range(DC):
                        l = mm3(ps[0:n, bank, 0:D], [a[:, hd % 2, k, tcols(t)] for a in oT],
                                [a[:, hd % 2, k * D:k * D + D] for a in os_], k == 0, k == DC - 1)
                    l.then_inc(pe_f, 1)

            for j in range(4):
                project(0, 0, j)
            h_transposes(3)
            h_transposes(4)
            scores(0, 0)

            def step(s, it=0):
                if s + 1 < UNITS:
                    project(s + 1, it, 0)
                    project(s + 1, it, 1)
                if 1 <= s <= UNITS:
                    attn_transpose(s, it)
                if s + 1 < UNITS:
                    project(s + 1, it, 2)
                    project(s + 1, it, 3)
                if s % 2 == 1 and s >= 3:
                    square_sums((s - 3) // 2, it)
                if 1 <= s <= UNITS:
                    attend(s - 1, it)
                if s >= 3:
                    if s % 2 == 1:
                        output_tiles((s - 3) // 2, it, (0, 1, 2))
                    else:
                        output_tiles((s - 4) // 2, it, (3, 4))
                if 1 <= s <= UNITS:
                    ax_transposes(s - 1, it)
                if s + 1 < UNITS:
                    scores(s + 1, it)
                if 1 <= s <= UNITS:
                    values(s - 1, it)

            for s in range(0, 4):
                step(s)
            with pe.Fori(0, 2) as i:
                for r in range(4):
                    step(4 + r, i)
            for s in range(12, 19):
                step(s)

            pe.wait_ge(dve_f, 5 * HEADS)
            for t in range(TILES):
                n = TROWS[t]
                pe.wait_ge(h2_ready, t + 1)
                if t >= 2:
                    pe.wait_ge(dve_h2t, t - 1)
                for k in range(DC):
                    l = nc.tensor.transpose(ps[:, 4 + t % 2, P * k:P * k + n], h[0:n, t, P * k:P * k + P], ident[0:n, 0:n])
                l.then_inc(pe_h2t, 1)
            pe.wait_ge(dve_h2t, TILES)

            def up(v, it=0):
                c, cs, m = v // 2, (v // 2) % 2, up_rows(v // 2)
                cols = slice(HALF * (v % 2), HALF * (v % 2) + HALF)
                if v % 2 == 0:
                    pe.wait_ge(lo_12, c + 1 + 2 * it)
                if v >= 2:
                    pe.wait_ge(act_sil, v - 1 + 4 * it)
                for i in range(2):
                    if v >= 2 and i == 1:
                        pe.wait_ge(dve_h, v - 1 + 4 * it)
                    for k in range(DC):
                        l = mm3(ps[0:m, 2 * (v % 2) + i, 0:HALF], [a[:, cs, i, k, 0:m] for a in w12s],
                                [a[:, k, cols] for a in h2T], k == 0, k == DC - 1)
                    l.then_inc(pe_up, 1)

            def down(v, it=0):
                c, cs, m = v // 2, (v // 2) % 2, up_rows(v // 2)
                if v % 2 == 0:
                    pe.wait_ge(lo_3, c + 1 + 2 * it)
                pe.wait_ge(dve_hl, v + 1 + 4 * it)
                for k in range(DC):
                    l = mm3(ps[:, 4 + 2 * (v % 2) + k, 0:HALF], [a[0:m, cs, P * k:P * k + P] for a in w3s],
                            [a[0:m, v % 2, :] for a in hh], c == 0, c == CHUNKS - 1)
                l.then_inc(pe_dn, 1)

            up(0)
            up(1)
            pe.wait_ge(wg_split, 2)
            for t in range(TILES):
                for k in range(DC):
                    l = mm3(ps[0:TROWS[t], 6, EXPERTS * t:EXPERTS * t + EXPERTS], [a[:, k, tcols(t)] for a in h2T],
                            [a[:, k, :] for a in wgs], k == 0, k == DC - 1)
            l.then_inc(pe_route, 1)
            up(2)
            down(0)
            up(3)
            pe.wait_ge(dve_small, 1)
            down(1)
            up(4)
            down(2)
            up(5)
            down(3)
            pe.wait_ge(gate_ready, 1)
            pe.wait_ge(act_sil, 5)
            pe.wait_ge(dve_h, 5)
            for t in range(TILES):
                l = nc.tensor.transpose(ps[0:EXPERTS, t // 3, P * (t % 3):P * (t % 3) + TROWS[t]],
                                        gate[0:TROWS[t], 0, t, :], ident[0:TROWS[t], 0:TROWS[t]])
            l.then_inc(pe_gt, 1)
            pe.wait_ge(gt_ready, 1)
            with pe.Fori(0, 12) as i:
                for r in range(4):
                    up(6 + r, i)
                    down(4 + r, i)
            for v in range(52, 56):
                if v + 2 < 2 * CHUNKS:
                    up(v + 2)
                down(v)
            for t in range(TILES):
                n = TROWS[t]
                pe.wait_ge(y_ready, 4)
                if t >= 4:
                    pe.wait_ge(y_tok, t - 3)
                for k in range(DC):
                    l = nc.tensor.transpose(ps[0:n, t % 4, P * k:P * k + P], yT[:, k, tcols(t)], ident[:, :])
                l.then_inc(pe_yt, 1)

        @block.scalar
        def _(act):
            def copy(o, i, scale=1.0):
                return nc.scalar.activation(o, i, ACT.Copy, scale=scale)

            act.wait_ge(tw_scaled, 1)
            copy(tws[0][:], tw[:]).then_inc(tw_hi, 1)

            def patches_hi(t):
                n = TROWS[t]
                for b in range(2):
                    act.wait_ge(pe_t, 2 * t + b + 1)
                    copy(xT[0][:, 3 * b:3 * b + 3, tcols(t)],
                         ps[:, 2 * (t % 2) + b, 0:384].rearrange("p (k n) -> p k n", k=3)[:, :, 0:n]).then_inc(act_t, 1)

            def h_hi(t):
                n = TROWS[t]
                act.wait_ge(pe_ht, t + 1)
                copy(hT[0][:, :, tcols(t)],
                     ps[:, 6 + t % 2, 0:D].rearrange("p (k n) -> p k n", k=DC)[:, :, 0:n]).then_inc(act_ht, 1)

            patches_hi(0)
            act.wait_ge(pe_lam, 1)
            nc.scalar.activation(lexp[:], ps[:, 7, 0:2 * HEADS], ACT.Exp).then_inc(lam_exp, 1)
            patches_hi(1)
            act.wait_ge(ld_qk[0], 16)
            copy(qks[0][:, 0, :], qk_raw[:, 0, :]).then_inc(hi_qk, 1)
            patches_hi(2)
            patches_hi(3)
            h_hi(0)
            patches_hi(4)
            h_hi(1)
            h_hi(2)

            def proj_hi(u, it, j):
                act.wait_ge(pe_q, 4 * u + j + 1 + 16 * it)
                copy(qkT[0][:, j, :], ps[:, j, 0:HALF]).then_inc(act_q, 1)

            def step(s, it=0):
                if s + 1 < UNITS:
                    proj_hi(s + 1, it, 0)
                    proj_hi(s + 1, it, 1)
                if 1 <= s <= UNITS:
                    act.wait_ge(pe_pt, s + 4 * it)
                    copy(aT[0][:], ps[0:GRP, 6, 0:HALF]).then_inc(act_pt, 1)
                if s + 1 < UNITS:
                    proj_hi(s + 1, it, 2)
                    proj_hi(s + 1, it, 3)
                if 0 <= s < UNITS:
                    act.wait_ge(dve_sub, s + 1 + 4 * it)
                    nc.scalar.activation(prob[:], prob[:], ACT.Exp, scale=SCALE).then_inc(act_exp, 1)
                if 1 <= s <= UNITS:
                    u = s - 1
                    for b in range(2):
                        act.wait_ge(pe_av, 2 * u + b + 1 + 8 * it)
                        if u >= 1:
                            act.wait_ge(pe_ax, 2 * u + 8 * it)
                        copy(ax[:, 2 * b:2 * b + 2, :], ps[0:GRP, b, 0:2 * D].rearrange("p (g d) -> p g d", g=2)).then_inc(act_av, 1)
                if s % 2 == 1 and (s + 3) // 2 < HEADS:
                    hd = (s + 3) // 2
                    if hd >= 2:
                        act.wait_ge(pe_q, 8 * (hd - 1) + 16 * it)
                    act.wait_ge(ld_qk[hd % 2], 16 * (hd // 2 + 1 + it))
                    copy(qks[0][:, hd % 2, :], qk_raw[:, hd % 2, :]).then_inc(hi_qk, 1)
                if s % 2 == 0 and s < UNITS:
                    hd = s // 2
                    if hd >= 2:
                        act.wait_ge(pe_o, 4 * (hd - 1) + 8 * it)
                    act.wait_ge(ld_v[hd % 2], 16 * (hd // 2 + 1 + it))
                    copy(vs[0][:, hd % 2, :], v_raw[:, hd % 2, :]).then_inc(hi_v, 1)
                if 1 <= s <= UNITS:
                    for k in range(DC):
                        act.wait_ge(pe_ax, 2 * u + k + 1 + 8 * it)
                        copy(axT[0][:, k, :], ps[:, k, 0:HALF]).then_inc(act_ax, 1)
                    for e in range(DC):
                        act.wait_ge(pe_o, 2 * u + e + 1 + 8 * it)
                        copy(oT[0][:, (u // 2) % 2, e, HALF * (u % 2):HALF * (u % 2) + HALF], ps[:, 2 + e, 0:HALF],
                             rms[:, e:e + 1]).then_inc(act_hi, 1)
                        if u >= 1 and e == 0:
                            act.wait_ge(pool_sq, u + 4 * it)
                        nc.scalar.activation(sq[:, e, :], ps[:, 2 + e, 0:HALF], ACT.Square).then_inc(act_o, 1)
                if s % 2 == 0 and s < UNITS:
                    if hd >= 2:
                        act.wait_ge(pe_f, 5 * (hd - 1) + 10 * it)
                    act.wait_ge(ld_o[hd % 2], 16 * (hd // 2 + 1 + it))
                    copy(os_[0][:, hd % 2, :], o_raw[:, hd % 2, :]).then_inc(hi_o, 1)

            for j in range(4):
                proj_hi(0, 0, j)
            h_hi(3)
            h_hi(4)
            act.wait_ge(ld_qk[1], 16)
            copy(qks[0][:, 1, :], qk_raw[:, 1, :]).then_inc(hi_qk, 1)
            act.wait_ge(ld_xg, 16)
            copy(xg[0][:], xg_raw).then_inc(xg_hi, 1)
            for s in range(0, 4):
                step(s)
            with act.Fori(0, 2) as i:
                for r in range(4):
                    step(4 + r, i)
            for s in range(12, 17):
                step(s)

            for t in range(TILES):
                n = TROWS[t]
                act.wait_ge(pe_h2t, t + 1)
                copy(h2T[0][:, :, tcols(t)],
                     ps[:, 4 + t % 2, 0:D].rearrange("p (k n) -> p k n", k=DC)[:, :, 0:n]).then_inc(act_h2t, 1)

            def silu(v, it=0):
                m = up_rows(v // 2)
                act.wait_ge(pe_up, 2 * v + 1 + 8 * it)
                if v >= 2:
                    act.wait_ge(dve_h, v - 1 + 4 * it)
                nc.scalar.activation(sil[0:m, v % 2, :], ps[0:m, 2 * (v % 2), 0:HALF], ACT.Silu).then_inc(act_sil, 1)

            def hidden_hi(v, it=0):
                m = up_rows(v // 2)
                act.wait_ge(dve_h, v + 1 + 4 * it)
                if v >= 2:
                    act.wait_ge(pe_dn, v - 1 + 4 * it)
                copy(hh[0][0:m, v % 2, :], hraw[0:m, v % 2, :]).then_inc(act_h, 1)

            for v in range(4):
                silu(v)
                hidden_hi(v)
                if v == 1:
                    act.wait_ge(dve_small, 3)
                    nc.scalar.activation(prb[:, :, 1:2], prb[:, :, 0:1], ACT.Exp).then_inc(act_small, 1)
            with act.Fori(0, 13) as i:
                for r in range(4):
                    silu(4 + r, i)
                    hidden_hi(4 + r, i)
            act.wait_ge(pe_dn, 2 * CHUNKS)
            for k in range(DC):
                copy(yT[:, k, HALF:TOK], ps[:, 6 + k, 0:HALF]).then_inc(y_ready, 1)

        @block.vector
        def _(dve):
            V = nc.vector

            V.memset(mhalf[:], -0.5)
            V.memset(ones[:], 1.0)
            V.memset(logit[:], 0.0)
            V.memset(ms[:], 1.0)
            V.memset(mv[:], 1.0).then_inc(mem_ready, 1)
            dve.wait_ge(mem_ready, 1)

            def scale_tok_weights():
                dve.wait_ge(ld_tw, 32)
                for k in range(KC):
                    l = V.tensor_scalar(tw[:, k, :], tw[:, k, :], gam1[:, k:k + 1], None, ALU.mult)
                l.then_inc(tw_scaled, 1)
                V.tensor_tensor(lprod[:, :].rearrange("p (i h) -> p i h", i=2), lam4[:, :, 0, :], lam4[:, :, 1, :],
                                ALU.mult).then_inc(lam_prod, 1)

            def tok_weights_lo():
                dve.wait_ge(tw_hi, 1)
                V.tensor_tensor(tws[1][:, 3:KC, :], tw[:, 3:KC, :], tws[0][:, 3:KC, :].bitcast(F32),
                                ALU.subtract).then_inc(tw_lo, 1)

            def patch_norm(t):
                n = TROWS[t]
                dve.wait_ge(ld_x[t], 16)
                for b in range(2):
                    l = V.bn_stats(bns[0:n, t, b, :], xr[0:n, t, 384 * b:384 * b + 384])
                l.then_inc(stat1, 1)
                dve.wait_ge(stat1, 2 * t + 1)
                V.bn_aggr(mv[0:n, t, :], bns[0:n, t, :, :].rearrange("p b s -> p (b s)")).then_inc(stat1, 1)

            def patch_apply(t):
                n = TROWS[t]
                dve.wait_ge(rstd1, t + 1)
                V.tensor_scalar(xr[0:n, t, :], xr[0:n, t, :], mv[0:n, t, 0:1], rstd[0:n, t:t + 1],
                                ALU.subtract, ALU.mult).then_inc(xn_ready, 1)

            def patches_lo(t):
                n = TROWS[t]
                for b in range(2):
                    dve.wait_ge(act_t, 2 * t + b + 1)
                    c = slice(3 * b, 3 * b + 3)
                    V.tensor_tensor(xT[1][:, c, tcols(t)],
                                    ps[:, 2 * (t % 2) + b, 0:384].rearrange("p (k n) -> p k n", k=3)[:, :, 0:n],
                                    xT[0][:, c, tcols(t)].bitcast(F32), ALU.subtract).then_inc(dve_t, 1)

            def token_stats(t):
                n = TROWS[t]
                dve.wait_ge(pe_z, t + 1)
                V.bn_stats(bns[0:n, t, 0, :], ps[0:n, 4 + t % 2, 0:D]).then_inc(stat2, 1)
                dve.wait_ge(stat2, 2 * t + 1)
                dve.wait_ge(xn_ready, t + 1)
                V.bn_aggr(mv[0:n, t, :], bns[0:n, t, 0, :]).then_inc(stat2, 1)

            def token_norm(t):
                n = TROWS[t]
                if t == 0:
                    dve.wait_ge(ld_const, 16 * 4)
                dve.wait_ge(stat2, 2 * t + 2)
                V.scalar_tensor_tensor(h[0:n, t, :], ps[0:n, 4 + t % 2, 0:D], mv[0:n, t, 0:1], g2b[0:n, :],
                                       ALU.subtract, ALU.mult).then_inc(h_part, 1)
                dve.wait_ge(h_part, t + 1)
                dve.wait_ge(rstd2, t + 1)
                V.scalar_tensor_tensor(h[0:n, t, :], h[0:n, t, :], rstd[0:n, t:t + 1], pet[0:n, t, :],
                                       ALU.mult, ALU.add).then_inc(h_ready, 1)

            def h_lo(t):
                n = TROWS[t]
                dve.wait_ge(act_ht, t + 1)
                V.tensor_tensor(hT[1][:, :, tcols(t)],
                                ps[:, 6 + t % 2, 0:D].rearrange("p (k n) -> p k n", k=DC)[:, :, 0:n],
                                hT[0][:, :, tcols(t)].bitcast(F32), ALU.subtract).then_inc(dve_ht, 1)

            patch_norm(0)
            scale_tok_weights()
            patch_apply(0)
            patch_norm(1)
            tok_weights_lo()
            patch_apply(1)
            patches_lo(0)
            patch_norm(2)
            patch_apply(2)
            patches_lo(1)
            patch_norm(3)
            patch_apply(3)
            token_stats(0)
            patches_lo(2)
            patch_norm(4)
            patch_apply(4)
            token_norm(0)
            token_stats(1)
            patches_lo(3)
            token_norm(1)
            h_lo(0)
            token_stats(2)
            patches_lo(4)
            token_norm(2)
            h_lo(1)
            token_stats(3)
            token_norm(3)
            h_lo(2)
            dve.wait_ge(lam_exp, 1)
            V.tensor_tensor(nlam[:], lexp[:, HEADS:2 * HEADS], lexp[:, 0:HEADS], ALU.subtract).then_inc(lam_part, 1)
            dve.wait_ge(lam_part, 1)
            V.tensor_scalar(nlam[:], nlam[:], -LAMBDA_INIT, None, ALU.add).then_inc(lam_ready, 1)
            dve.wait_ge(ld_mask, 16)
            V.tensor_copy(mask[:], mask_raw[:]).then_inc(mask_ready, 1)

            s_view = ps[0:GRP, 4:6, 0:HALF].rearrange("p j (g n) -> p j g n", g=GRPS)
            p_view = prob[:, :, :].rearrange("p (j g) n -> p j g n", j=2)

            def stats_view(a):
                return a[:, :].rearrange("p (j g) -> p j g", j=2)

            def row_max(u, it):
                dve.wait_ge(pe_s, u + 1 + 4 * it)
                for j in range(2):
                    V.tensor_reduce(smax[:, GRPS * j:GRPS * j + GRPS], s_view[:, j, :, :], AX_X, ALU.max).then_inc(dve_max, 1)

            def subtract_max(u, it):
                dve.wait_ge(dve_max, 2 * u + 2 + 8 * it)
                if u >= 1:
                    dve.wait_ge(pool_attn, u + 4 * it)
                for j in range(2):
                    l = V.tensor_tensor(p_view[:, j, :, :], s_view[:, j, :, :],
                                        stats_view(smax)[:, j, :].unsqueeze(2).broadcast_to([GRP, GRPS, GRP]), ALU.subtract)
                l.then_inc(dve_sub, 1)

            def row_sum(u, it):
                dve.wait_ge(act_exp, u + 1 + 4 * it)
                V.tensor_reduce(ssum[:], prob[:], AX_X, ALU.add).then_inc(dve_sum, 1)

            def row_reciprocal(u, it):
                dve.wait_ge(dve_sum, u + 1 + 4 * it)
                V.reciprocal(rsum[:], ssum[:]).then_inc(dve_rec, 1)

            def lambda_scale(u, it):
                dve.wait_ge(dve_rec, u + 1 + 4 * it)
                lam = nlam[0:GRP, u // 2:u // 2 + 1] if isinstance(it, int) else nlam[0:GRP, bass.ds(u // 2 + 2 * it, 1)]
                V.tensor_scalar(rsum[:, GRPS:2 * GRPS], rsum[:, GRPS:2 * GRPS], lam, None, ALU.mult).then_inc(dve_r, 1)

            def proj_lo(u, it, j):
                dve.wait_ge(act_q, 4 * u + j + 1 + 16 * it)
                V.tensor_tensor(qkT[1][:, j, :], ps[:, j, 0:HALF], qkT[0][:, j, :].bitcast(F32),
                                ALU.subtract).then_inc(dve_q, 1)

            def add_tiles(hd, it, tiles):
                for t in tiles:
                    n = TROWS[t]
                    if t == 0:
                        dve.wait_ge(pool_rinv, hd + 1 + 2 * it)
                        if hd >= 1:
                            dve.wait_ge(dve_f, 5 * hd + 10 * it)
                    dve.wait_ge(pe_f, 5 * hd + t + 1 + 10 * it)
                    V.scalar_tensor_tensor(h[0:n, t, :], ps[0:n, (6, 7, 6, 7, 6)[t], 0:D], rinv[0:n, t:t + 1], h[0:n, t, :],
                                           ALU.mult, ALU.add).then_inc(dve_f, 1)

            def step(s, it=0):
                if s + 1 < UNITS:
                    proj_lo(s + 1, it, 0)
                    proj_lo(s + 1, it, 1)
                if 1 <= s <= UNITS:
                    dve.wait_ge(act_pt, s + 4 * it)
                    V.tensor_tensor(aT[1][:], ps[0:GRP, 6, 0:HALF], aT[0][:].bitcast(F32), ALU.subtract).then_inc(dve_pt, 1)
                if 0 <= s < UNITS:
                    subtract_max(s, it)
                if s + 1 < UNITS:
                    proj_lo(s + 1, it, 2)
                    proj_lo(s + 1, it, 3)
                if s % 2 == 1 and s >= 3:
                    hd = (s - 3) // 2
                    dve.wait_ge(pe_stat, hd + 1 + 2 * it)
                    if hd >= 1:
                        dve.wait_ge(pool_rinv, hd + 2 * it)
                    c = 1.0 / (OUT_C * OUT_C)
                    V.tensor_scalar(ms[:, 0:4], ps[:, 7, 0:4], c / D, EPS * c, ALU.mult, ALU.add)
                    V.tensor_scalar(ms[0:64, 4:5], ps[0:64, 7, 4:5], c / D, EPS * c, ALU.mult, ALU.add).then_inc(dve_stat, 1)
                hd, tiles = ((s - 3) // 2, [0, 1, 2]) if s % 2 == 1 else ((s - 4) // 2, [3, 4])
                adding = s >= 3
                scaling = 0 <= s < UNITS
                if adding:
                    add_tiles(hd, it, tiles[0:1])
                if scaling:
                    row_sum(s, it)
                if adding:
                    add_tiles(hd, it, tiles[1:2])
                if scaling:
                    row_reciprocal(s, it)
                if adding:
                    add_tiles(hd, it, tiles[2:3])
                if scaling:
                    lambda_scale(s, it)
                if 1 <= s <= UNITS:
                    for k in range(DC):
                        dve.wait_ge(act_ax, 2 * (s - 1) + k + 1 + 8 * it)
                        V.tensor_tensor(axT[1][:, k, :], ps[:, k, 0:HALF], axT[0][:, k, :].bitcast(F32),
                                        ALU.subtract).then_inc(dve_ax, 1)
                if s + 1 < UNITS:
                    row_max(s + 1, it)
                if 1 <= s <= UNITS:
                    u = s - 1
                    cols = slice(HALF * (u % 2), HALF * (u % 2) + HALF)
                    for e in range(DC):
                        dve.wait_ge(act_o, 2 * u + e + 1 + 8 * it)
                        V.scalar_tensor_tensor(oT[1][:, (u // 2) % 2, e, cols], ps[:, 2 + e, 0:HALF], rms[:, e:e + 1],
                                               oT[0][:, (u // 2) % 2, e, cols].bitcast(F32),
                                               ALU.mult, ALU.subtract).then_inc(dve_o, 1)

            proj_lo(0, 0, 0)
            proj_lo(0, 0, 1)
            token_stats(4)
            token_norm(4)
            proj_lo(0, 0, 2)
            proj_lo(0, 0, 3)
            h_lo(3)
            h_lo(4)
            dve.wait_ge(lam_ready, 1)
            V.tensor_copy(wgs[0][:], wgr[:]).then_inc(wg_split, 1)
            dve.wait_ge(wg_split, 1)
            V.tensor_tensor(wgs[1][:], wgr[:], wgs[0][:].bitcast(F32), ALU.subtract).then_inc(wg_split, 1)
            row_max(0, 0)
            step(0)
            dve.wait_ge(xg_hi, 1)
            V.tensor_tensor(xg[1][:], xg_raw, xg[0][:].bitcast(F32), ALU.subtract).then_inc(xg_lo, 1)
            for s in range(1, 4):
                step(s)
            with dve.Fori(0, 2) as i:
                for r in range(4):
                    step(4 + r, i)

            def split12_hi(c, it=0):
                m = up_rows(c)
                if c >= 2:
                    dve.wait_ge(pe_up, 4 * (c - 1) + 8 * it)
                dve.wait_ge(ld_12[c % 2], 16 * (c // 2 + 1 + it))
                V.tensor_copy(w12s[0][:, c % 2, :, :, 0:m], r12[:, c % 2, :, :, 0:m]).then_inc(hi_12, 1)

            def split3_hi(c, it=0):
                m = up_rows(c)
                if c >= 2:
                    dve.wait_ge(pe_dn, 2 * (c - 1) + 4 * it)
                dve.wait_ge(ld_3[c % 2], 16 * (c // 2 + 1 + it))
                V.tensor_copy(w3s[0][0:m, c % 2, :], r3[0:m, c % 2, :]).then_inc(hi_3, 1)

            def split3_lo(c, it=0):
                m = up_rows(c)
                dve.wait_ge(hi_3, c + 1 + 2 * it)
                V.tensor_tensor(w3s[1][0:m, c % 2, :], r3[0:m, c % 2, :], w3s[0][0:m, c % 2, :].bitcast(F32),
                                ALU.subtract).then_inc(lo_3, 1)

            for s in range(12, 16):
                step(s)
            dve.wait_ge(dve_ht, TILES)
            split12_hi(0)
            split12_hi(1)
            split3_hi(0)
            split3_lo(0)
            step(16)
            step(17)
            step(18)

            def norm_stats(t, start, done):
                n = TROWS[t]
                V.bn_stats(bns[0:n, t, 0, :], h[0:n, t, :]).then_inc(done, 1)
                dve.wait_ge(done, start + 2 * t + 1)
                V.bn_aggr(mv[0:n, t, :], bns[0:n, t, 0, :]).then_inc(done, 1)

            dve.wait_ge(dve_f, 5 * HEADS)
            for t in range(TILES):
                norm_stats(t, 0, stat3)
            for t in range(TILES):
                n = TROWS[t]
                dve.wait_ge(rstd3, t + 1)
                V.tensor_scalar(h[0:n, t, :], h[0:n, t, :], mv[0:n, t, 0:1], rstd[0:n, t:t + 1],
                                ALU.subtract, ALU.mult).then_inc(h2_ready, 1)
            for t in range(TILES):
                n = TROWS[t]
                dve.wait_ge(act_h2t, t + 1)
                V.tensor_tensor(h2T[1][:, :, tcols(t)],
                                ps[:, 4 + t % 2, 0:D].rearrange("p (k n) -> p k n", k=DC)[:, :, 0:n],
                                h2T[0][:, :, tcols(t)].bitcast(F32), ALU.subtract).then_inc(dve_h2t, 1)

            def route():
                dve.wait_ge(pe_route, 1)
                dve.wait_ge(iota_ready, 1)
                V.tensor_copy(logit[:, 0:4, :], ps[:, 6, 0:32].rearrange("p (t e) -> p t e", e=EXPERTS))
                V.tensor_copy(logit[0:64, 4, :], ps[0:64, 6, 32:40]).then_inc(dve_small, 1)
                dve.wait_ge(dve_small, 1)
                for t in range(TILES):
                    l = V.max(top[:, t, :], logit[:, t, :])
                l.then_inc(dve_small, 1)
                dve.wait_ge(dve_small, 2)
                V.tensor_tensor(prb[:, :, 0:1], top[:, :, 1:2], top[:, :, 0:1], ALU.subtract).then_inc(dve_small, 1)
                for t in range(TILES):
                    l = V.max_index(topi[:, t, :], top[:, t, :], logit[:, t, :])
                l.then_inc(dve_small, 1)
                dve.wait_ge(dve_small, 4)
                V.tensor_copy(topf[:], topi[:, :, 0:2]).then_inc(dve_small, 1)
                dve.wait_ge(act_small, 1)
                V.tensor_scalar(prb[:, :, 2:3], prb[:, :, 1:2], 1.0, None, ALU.add).then_inc(dve_small, 1)
                dve.wait_ge(dve_small, 6)
                V.reciprocal(prb[:, :, 2:3], prb[:, :, 2:3]).then_inc(dve_small, 1)
                dve.wait_ge(dve_small, 7)
                V.tensor_tensor(prb[:, :, 3:4], prb[:, :, 1:2], prb[:, :, 2:3], ALU.mult).then_inc(dve_small, 1)
                dve.wait_ge(dve_small, 8)
                for t in range(TILES):
                    for i in range(2):
                        l = V.tensor_scalar(gate[:, i, t, :], iota[:], topf[:, t, i:i + 1], prb[:, t, 2 + i:3 + i],
                                            ALU.is_equal, ALU.mult)
                l.then_inc(dve_small, 1)
                dve.wait_ge(dve_small, 9)
                V.tensor_tensor(gate[:, 0, :, :], gate[:, 0, :, :], gate[:, 1, :, :], ALU.add).then_inc(gate_ready, 1)

            def hidden(v, it=0):
                m = up_rows(v // 2)
                if v < 2 * SHARED_CHUNKS:
                    dve.wait_ge(act_sil, v + 1 + 4 * it)
                else:
                    dve.wait_ge(pool_gate, v - 2 * SHARED_CHUNKS + 1 + 4 * it)
                dve.wait_ge(pe_up, 2 * v + 2 + 8 * it)
                if v >= 2:
                    dve.wait_ge(act_h, v - 1 + 4 * it)
                    dve.wait_ge(dve_hl, v - 1 + 4 * it)
                V.tensor_tensor(hraw[0:m, v % 2, :], ps[0:m, 2 * (v % 2) + 1, 0:HALF], sil[0:m, v % 2, :],
                                ALU.mult).then_inc(dve_h, 1)

            def hidden_lo(v, it=0):
                m = up_rows(v // 2)
                dve.wait_ge(act_h, v + 1 + 4 * it)
                V.tensor_tensor(hh[1][0:m, v % 2, :], hraw[0:m, v % 2, :], hh[0][0:m, v % 2, :].bitcast(F32),
                                ALU.subtract).then_inc(dve_hl, 1)

            def ffn_step(v, it=0):
                if v % 2 == 1 and v // 2 + 2 < CHUNKS:
                    split12_hi(v // 2 + 2, it)
                hidden(v, it)
                if v % 2 == 1 and v // 2 + 1 < CHUNKS:
                    split3_hi(v // 2 + 1, it)
                hidden_lo(v, it)
                if v % 2 == 1 and v // 2 + 1 < CHUNKS:
                    split3_lo(v // 2 + 1, it)

            ffn_step(0)
            ffn_step(1)
            route()
            for v in range(2, 5):
                ffn_step(v)
            dve.wait_ge(pe_gt, 1)
            V.tensor_copy(gateT[:, 0:384], ps[0:EXPERTS, 0, 0:384])
            V.tensor_copy(gateT[:, 384:TOK], ps[0:EXPERTS, 1, 0:192]).then_inc(gt_ready, 1)
            for v in range(5, 2 * SHARED_CHUNKS):
                ffn_step(v)
            with dve.Fori(0, 10) as i:
                for r in range(4):
                    ffn_step(2 * SHARED_CHUNKS + r, i)
            for v in range(52, 56):
                ffn_step(v)
            dve.wait_ge(pe_dn, 2 * CHUNKS)
            for k in range(DC):
                V.tensor_copy(yT[:, k, 0:HALF], ps[:, 4 + k, 0:HALF]).then_inc(y_ready, 1)
            for t in range(TILES):
                n = TROWS[t]
                dve.wait_ge(pe_yt, t + 1)
                V.tensor_tensor(h[0:n, t, :], ps[0:n, t % 4, 0:D], h[0:n, t, :], ALU.add).then_inc(y_tok, 1)
                dve.wait_ge(y_tok, t + 1)
                norm_stats(t, 0, stat4)
            for t in range(TILES):
                n = TROWS[t]
                dve.wait_ge(rstd4, t + 1)
                V.tensor_scalar(h[0:n, t, :], h[0:n, t, :], mv[0:n, t, 0:1], rstd[0:n, t:t + 1],
                                ALU.subtract, ALU.mult).then_inc(y_done, 1)

        @block.gpsimd
        def _(pool):
            G = nc.gpsimd
            steps = [0]

            def lo(o, i, hi, done):
                return G.tensor_tensor(o, i, hi.bitcast(F32), ALU.subtract).then_inc(done, 1)

            def inv_std(t, done, start, ready):
                pool.wait_ge(done, start + 2 * t + 2)
                n = TROWS[t]
                G.tensor_scalar(mv[0:n, t, 1:2], mv[0:n, t, 1:2], EPS, 1.0, ALU.add, ALU.mult).then_inc(eps_added, 1)
                steps[0] += 1
                pool.wait_ge(eps_added, steps[0])
                G.tensor_tensor(rstd[0:n, t:t + 1], mv[0:n, t, 1:2], mhalf[0:n, 0:1], ALU.pow).then_inc(ready, 1)

            G.iota(iota[:], pattern=[[1, EXPERTS]], base=0, channel_multiplier=0,
                   allow_small_or_imprecise_dtypes=True).then_inc(iota_ready, 1)
            pool.wait_ge(mem_ready, 1)
            inv_std(0, stat1, 0, rstd1)
            inv_std(1, stat1, 0, rstd1)
            pool.wait_ge(tw_hi, 1)
            lo(tws[1][:, 0:3, :], tw[:, 0:3, :], tws[0][:, 0:3, :], tw_lo)
            inv_std(2, stat1, 0, rstd1)
            inv_std(3, stat1, 0, rstd1)
            inv_std(0, stat2, 0, rstd2)
            inv_std(4, stat1, 0, rstd1)
            inv_std(1, stat2, 0, rstd2)
            pool.wait_ge(hi_qk, 1)
            lo(qks[1][:, 0, :], qk_raw[:, 0, :], qks[0][:, 0, :], lo_qk)
            for t in range(2, TILES):
                inv_std(t, stat2, 0, rstd2)

            def step(s, it=0):
                if s % 2 == 0 and (s + 2) // 2 < HEADS:
                    hd = (s + 2) // 2
                    pool.wait_ge(hi_qk, hd + 1 + 2 * it)
                    lo(qks[1][:, hd % 2, :], qk_raw[:, hd % 2, :], qks[0][:, hd % 2, :], lo_qk)
                if s % 2 == 1 and 0 <= s - 1 < UNITS:
                    hd = (s - 1) // 2
                    pool.wait_ge(hi_v, hd + 1 + 2 * it)
                    lo(vs[1][:, hd % 2, :], v_raw[:, hd % 2, :], vs[0][:, hd % 2, :], lo_v)
                    pool.wait_ge(hi_o, hd + 1 + 2 * it)
                    lo(os_[1][:, hd % 2, :], o_raw[:, hd % 2, :], os_[0][:, hd % 2, :], lo_o)
                if s % 2 == 1 and s >= 3:
                    hd = (s - 3) // 2
                    pool.wait_ge(dve_stat, hd + 1 + 2 * it)
                    if hd >= 1:
                        pool.wait_ge(dve_f, 5 * hd + 10 * it)
                    G.tensor_tensor(rinv[:], ms[:], mhalf[:], ALU.pow).then_inc(pool_rinv, 1)
                if 0 <= s < UNITS:
                    pool.wait_ge(dve_r, s + 1 + 4 * it)
                    G.tensor_tensor(prob[:], prob[:], rsum[:, :].unsqueeze(2).broadcast_to([GRP, 2 * GRPS, GRP]),
                                    ALU.mult).then_inc(pool_mul, 1)
                    pool.wait_ge(pool_mul, s + 1 + 4 * it)
                    if s >= 1:
                        pool.wait_ge(pe_pt, s + 4 * it)
                    G.tensor_tensor(attn[:], prob[:, 0:GRPS, :], prob[:, GRPS:2 * GRPS, :], ALU.add).then_inc(pool_attn, 1)
                if 1 <= s <= UNITS:
                    u = s - 1
                    pool.wait_ge(act_o, 2 * u + 2 + 8 * it)
                    G.tensor_tensor(sqs[:, (u // 2) % 2, HALF * (u % 2):HALF * (u % 2) + HALF], sq[:, 0, :], sq[:, 1, :],
                                    ALU.add).then_inc(pool_sq, 1)

            for s in range(0, 4):
                step(s)
            with pool.Fori(0, 2) as i:
                for r in range(4):
                    step(4 + r, i)
            for s in range(12, 16):
                step(s)
            pool.wait_ge(dve_ht, TILES)

            def split12_lo(c, it=0):
                m = up_rows(c)
                pool.wait_ge(hi_12, c + 1 + 2 * it)
                lo(w12s[1][:, c % 2, :, :, 0:m], r12[:, c % 2, :, :, 0:m], w12s[0][:, c % 2, :, :, 0:m], lo_12)

            step(16)
            step(17)
            split12_lo(0)
            split12_lo(1)
            for t in range(TILES):
                inv_std(t, stat3, 0, rstd3)

            def ffn_step(v, it=0):
                if v >= 2 * SHARED_CHUNKS:
                    c = v // 2
                    pool.wait_ge(act_sil, v + 1 + 4 * it)
                    if v % 2 == 0:
                        g = c - SHARED_CHUNKS
                        gate_loads(g, it)
                    cols = slice(HALF * (v % 2), HALF * (v % 2) + HALF)
                    G.tensor_tensor(sil[:, v % 2, :], sil[:, v % 2, :], gates[:, (c - SHARED_CHUNKS) % 4, cols],
                                    ALU.mult).then_inc(pool_gate, 1)
                if v % 2 == 1 and v // 2 + 2 < CHUNKS:
                    split12_lo(v // 2 + 2, it)

            def gate_loads(g, it):
                pool.wait_ge(ld_g[g % 4], 64 * (g // 4 + 1 + it))

            for v in range(0, 2 * SHARED_CHUNKS):
                ffn_step(v)

            def ffn_step8(v, i):
                c = v // 2
                cols = slice(HALF * (v % 2), HALF * (v % 2) + HALF)
                pool.wait_ge(act_sil, v + 1 + 8 * i)
                if v % 2 == 0:
                    gate_loads(c - SHARED_CHUNKS, i)
                G.tensor_tensor(sil[:, v % 2, :], sil[:, v % 2, :], gates[:, (c - SHARED_CHUNKS) % 4, cols],
                                ALU.mult).then_inc(pool_gate, 1)
                if v % 2 == 1:
                    split12_lo(c + 2, 2 * i)

            with pool.Fori(0, 5) as i:
                for r in range(8):
                    ffn_step8(2 * SHARED_CHUNKS + r, i)
            for v in range(52, 56):
                ffn_step(v)
            for t in range(TILES):
                inv_std(t, stat4, 0, rstd4)


def kernel(**inputs):
    import numpy as np
    import concourse.bacc as bacc
    from concourse.bass_utils import run_bass_kernel_spmd as run

    f = {k: np.asarray(v) for k, v in inputs.items()}
    c = np.ascontiguousarray
    a = {}
    a["x"] = c(f["x"].reshape(16, 3, 6, 16, 6, 16).transpose(0, 2, 4, 1, 3, 5).reshape(TOK, PATCH))
    a["tokw"] = c(f["L0_tok_W"].T.reshape(KC, P, D).transpose(1, 0, 2))
    a["consts"] = c(np.concatenate([
        f["L0_tok_ln1_w"].reshape(KC, P).T, f["L0_attn_rms_scale"].reshape(2, P).T,
        f["L0_attn_lambda_q1"].T, f["L0_attn_lambda_k1"].T, f["L0_attn_lambda_q2"].T, f["L0_attn_lambda_k2"].T], axis=1))
    omega = np.arange(D // 4, dtype=np.float32) / np.float32(D // 4 - 1)
    omega = (np.float32(1.0) / np.float32(10000.0) ** omega).astype(np.float32)
    yy, xx = np.meshgrid(np.arange(6, dtype=np.float32), np.arange(6, dtype=np.float32), indexing="ij")
    yo, xo = yy.reshape(-1)[:, None] * omega[None, :], xx.reshape(-1)[:, None] * omega[None, :]
    a["pe_tab"] = c(np.tile(np.concatenate([np.sin(xo), np.cos(xo), np.sin(yo), np.cos(yo)], axis=1), (IMAGES, 1)).astype(np.float32))
    a["g2"] = c(f["L0_tok_ln2_w"].reshape(1, D))

    def head_in(w):
        return w.reshape(HEADS, D, DC, P).transpose(0, 3, 2, 1).reshape(HEADS, P, DC * D)

    a["wqk"] = c(np.concatenate([head_in(f["L0_attn_Wq"]), head_in(f["L0_attn_Wk"])], axis=2))
    a["wv"] = c(head_in(f["L0_attn_Wv"]))
    a["wo"] = c(f["L0_attn_Wo"].T.reshape(HEADS, DC, P, D).transpose(0, 2, 1, 3).reshape(HEADS, P, DC * D))
    a["ident"] = np.eye(P, dtype=np.float32)
    masks = np.zeros((2, GRP + HALF), np.float32)
    for i in range(2):
        masks[i, IMG_TOK * i:IMG_TOK * (i + 1)] = 1.0
        for g in range(GRPS):
            masks[i, GRP + GRP * g + IMG_TOK * (1 - i):GRP + GRP * g + IMG_TOK * (2 - i)] = -1e30
    a["masks"] = masks
    a["wg"] = c(f["L0_ffn_Wg"].reshape(DC, P, EXPERTS).transpose(1, 0, 2))
    r1 = np.concatenate([f["L0_ffn_Ws1"].T, f["L0_ffn_W1"].transpose(0, 2, 1).reshape(-1, D)])
    r2 = np.concatenate([f["L0_ffn_Ws2"].T, f["L0_ffn_W2"].transpose(0, 2, 1).reshape(-1, D)])
    r3 = np.concatenate([f["L0_ffn_Ws3"], f["L0_ffn_W3"].reshape(-1, D)])

    def chunked(r, m):
        return r.reshape(-1, m, DC, P).transpose(0, 3, 2, 1)

    a["s12"] = c(np.stack([chunked(r1[:SHARED0], SHARED0)[0], chunked(r2[:SHARED0], SHARED0)[0]], axis=1))
    a["s3"] = c(r3[:SHARED0])
    a["w12"] = c(np.stack([chunked(r1[SHARED0:], P), chunked(r2[SHARED0:], P)], axis=2).reshape(CHUNKS - 1, P, 4 * P))
    a["w3"] = c(r3[SHARED0:].reshape(CHUNKS - 1, P, D))

    nc = bacc.Bacc("TRN2", target_bir_lowering=False, num_devices=1)
    order = ["x", "tokw", "consts", "pe_tab", "g2", "wqk", "wv", "wo", "ident", "masks", "wg", "s12", "s3", "w12", "w3"]
    args = [nc.dram_tensor(f"in_{n}", a[n].shape, F32, kind="ExternalInput").ap() for n in order]
    out = nc.dram_tensor("out", (TOK, D), F32, kind="ExternalOutput").ap()
    build(nc, *args, out)
    r = run(nc, [{f"in_{n}": a[n] for n in order}], core_ids=[0])
    return r.results[0]["out"].reshape(IMAGES, IMG_TOK, D)
```

```python
from contextlib import ExitStack

import concourse.bass as bass
from concourse import mybir

F32 = mybir.dt.float32
F32R = mybir.dt.float32r
U32 = mybir.dt.uint32
ACT = mybir.ActivationFunctionType
ALU = mybir.AluOpType
AX_X = mybir.AxisListType.X

P = 128
IMAGES = 16
IMG_TOK = 36
TOK = IMAGES * IMG_TOK
TILES = 5
TROWS = [min(P, TOK - P * t) for t in range(TILES)]
D = 256
DC = D // P
PATCH = 768
KC = PATCH // P
HEADS = 8
HALF = TOK // 2
GRP = 3 * IMG_TOK
F_BANK = (6, 7, 6, 7, 6)
GRPS = -(-HALF // GRP)
GROWS = [min(GRP, HALF - GRP * g) for g in range(GRPS)]
SCORES = GRPS * GRP
UNITS = 2 * HEADS
EXPERTS = 8
SHARED0 = 64
CHUNKS = 28
SHARED_CHUNKS = 6
EPS = 1e-5
LAMBDA_INIT = 0.8 - 0.6 * 0.7408182206817179
SCALE = 1.0 / 128 ** 0.5
OUT_C = 1.0 - LAMBDA_INIT


def build(nc, x, tokw, consts, pe_tab, g2, wqk, wv, wo, ident_d, masks, wg, s12, s3, w12, w3, out):
    ctx = ExitStack()
    with ctx:
        def sb(name, shape, dt=F32):
            return ctx.enter_context(nc.sbuf_tensor(name, shape, dt))

        def sem(name):
            return ctx.enter_context(nc.semaphore(name))

        region = sb("region", [P, TILES * PATCH])
        xr = region[:, :].rearrange("p (t f) -> p t f", t=TILES)
        xg_raw = region[0:GRP, 0:2 * GRPS * D].rearrange("p (g d) -> p g d", d=D)
        gates = region[:, 0:4 * TOK].rearrange("p (s n) -> p s n", s=4)
        split_region = sb("split_region", [P, 2 * KC * TOK], F32R)
        xT = [split_region[:, i * KC * TOK:(i + 1) * KC * TOK].rearrange("p (k n) -> p k n", k=KC) for i in range(2)]
        h2T = [split_region[:, i * DC * TOK:(i + 1) * DC * TOK].rearrange("p (k n) -> p k n", k=DC) for i in range(2)]
        base12 = 2 * DC * TOK
        w12s = [split_region[:, base12 + 1024 * i:base12 + 1024 * (i + 1)].rearrange("p (s w k m) -> p s w k m", s=2, w=2, k=DC)
                for i in range(2)]
        base3 = base12 + 2048
        w3s = [split_region[:, base3 + 512 * i:base3 + 512 * (i + 1)].rearrange("p (s n) -> p s n", s=2) for i in range(2)]
        tw = sb("tw", [P, KC, D])
        tws = [sb(f"tws{i}", [P, KC, D], F32R) for i in range(2)]
        cst = sb("cst", [P, KC + 2 + 4 * HEADS])
        gam1 = cst[:, 0:KC]
        rms = cst[:, KC:KC + 2]
        lam4 = cst[:, KC + 2:KC + 2 + 4 * HEADS].rearrange("p (i j h) -> p i j h", i=2, j=2)
        ident = sb("ident", [P, P])
        ones = sb("ones", [P, P])
        pet = sb("pet", [P, TILES, D])
        g2b = sb("g2b", [P, D])
        mask = sb("mask", [GRP, GRP])
        bns = sb("bns", [P, TILES, 2, 6])
        mv = sb("mv", [P, TILES, 2])
        rstd = sb("rstd", [P, TILES])
        mhalf = sb("mhalf", [P, TILES])
        euler = sb("euler", [P, TILES])
        nmr = sb("nmr", [P, TILES])
        h = sb("h", [P, TILES, D])
        hT = [sb(f"hT{i}", [P, DC, TOK], F32R) for i in range(2)]
        xg = [sb(f"xg{i}", [GRP, 2 * GRPS, D], F32R) for i in range(2)]
        lprod = sb("lprod", [P, 2 * HEADS])
        lexp = sb("lexp", [P, 2 * HEADS])
        nlam = sb("nlam", [P, HEADS])
        qk_raw = sb("qk_raw", [P, 2, 4 * D])
        v_raw = sb("v_raw", [P, 2, 2 * D])
        o_raw = sb("o_raw", [P, 2, 2 * D])
        qks = [sb(f"qks{i}", [P, 2, 4 * D], F32R) for i in range(2)]
        vs = [sb(f"vs{i}", [P, 2, 2 * D], F32R) for i in range(2)]
        os_ = [sb(f"os{i}", [P, 2, 2 * D], F32R) for i in range(2)]
        qkT = sb("qkT", [P, 4, HALF])
        prob = sb("prob", [GRP, 2 * GRPS, GRP])
        masked = sb("masked", [GRP, 2 * GRPS, GRP])
        smax = sb("smax", [GRP, 2 * GRPS])
        ssum = sb("ssum", [GRP, 2 * GRPS])
        rsum = sb("rsum", [GRP, 2 * GRPS])
        attn = sb("attn", [GRP, GRPS, GRP])
        aT = [sb(f"aT{i}", [GRP, HALF], F32R) for i in range(2)]
        axT = [sb(f"axT{i}", [P, DC, HALF], F32R) for i in range(2)]
        oT = [sb(f"oT{i}", [P, 2, DC, TOK], F32R) for i in range(2)]
        sq = sb("sq", [P, DC, HALF])
        sqs = sb("sqs", [P, 2, TOK])
        ms = sb("ms", [P, TILES])
        rinv = sb("rinv", [P, TILES])
        wgr = sb("wgr", [P, DC, EXPERTS])
        wgs = [sb(f"wgs{i}", [P, DC, EXPERTS], F32R) for i in range(2)]
        logit = sb("logit", [P, TILES, EXPERTS])
        top = sb("top", [P, TILES, 8])
        topi = sb("topi", [P, TILES, 8], U32)
        topf = sb("topf", [P, TILES, 2])
        iota = sb("iota", [P, EXPERTS])
        prb = sb("prb", [P, TILES, 4])
        gate = sb("gate", [P, 2, TILES, EXPERTS])
        gateT = sb("gateT", [EXPERTS, TOK])
        logitT = sb("logitT", [EXPERTS, TOK])
        r12 = sb("r12", [P, 2, 2, DC, P])
        r3 = sb("r3", [P, 2, D])
        ffn_rows = pet[:, :, :].rearrange("p t d -> p (t d)")
        sil = ffn_rows[:, 0:TOK].rearrange("p (s n) -> p s n", s=2)
        hraw = ffn_rows[:, TOK:2 * TOK].rearrange("p (s n) -> p s n", s=2)
        hh = [a[:, :, :].rearrange("p k d -> p (k d)")[:, 0:TOK].rearrange("p (s n) -> p s n", s=2) for a in tws]
        yT = tw[:, :, :].rearrange("p k d -> p (k d)")[:, 0:DC * TOK].rearrange("p (k n) -> p k n", k=DC)

        ax = tw[:, :, :].rearrange("p k d -> p (k d)")[0:GRP, 0:GRPS * D].rearrange("p (g d) -> p g d", g=GRPS)

        ps = ctx.enter_context(nc.psum_tensor("ps", [P, 8, 512], F32))

        h_dram = nc.dram_tensor("h_scratch", (TOK, D), F32, kind="Internal").ap()
        g_dram = nc.dram_tensor("gate_scratch", (EXPERTS * 11, TOK), F32, kind="Internal").ap()

        ld_const = sem("ld_const")
        ld_mask = sem("ld_mask")
        ld_tw = sem("ld_tw")
        h_stored = sem("h_stored")
        ld_xg = sem("ld_xg")
        g_stored = sem("g_stored")
        out_stored = sem("out_stored")
        mem_ready = sem("mem_ready")
        stat1 = sem("stat1")
        rstd1 = sem("rstd1")
        rstd2 = sem("rstd2")
        rstd3 = sem("rstd3")
        rstd4 = sem("rstd4")
        ld_ident = sem("ld_ident")
        eps_added = sem("eps_added")
        neg_mean = sem("neg_mean")
        nmr_ready = sem("nmr_ready")
        xn_ready = sem("xn_ready")
        pe_t = sem("pe_t")
        act_t = sem("act_t")
        dve_t = sem("dve_t")
        pe_z = sem("pe_z")
        stat2 = sem("stat2")
        h_part = sem("h_part")
        h_ready = sem("h_ready")
        pe_ht = sem("pe_ht")
        act_ht = sem("act_ht")
        dve_ht = sem("dve_ht")
        tw_hi = sem("tw_hi")
        tw_lo = sem("tw_lo")
        xg_hi = sem("xg_hi")
        xg_lo = sem("xg_lo")
        lam_prod = sem("lam_prod")
        pe_lam = sem("pe_lam")
        lam_exp = sem("lam_exp")
        lam_part = sem("lam_part")
        lam_ready = sem("lam_ready")
        dve_zero = sem("dve_zero")
        dve_mask = sem("dve_mask")
        wg_split = sem("wg_split")
        pe_q = sem("pe_q")
        act_q = sem("act_q")
        pe_s = sem("pe_s")
        dve_max = sem("dve_max")
        dve_sub = sem("dve_sub")
        act_exp = sem("act_exp")
        dve_sum = sem("dve_sum")
        dve_rec = sem("dve_rec")
        dve_r = sem("dve_r")
        weighed = sem("weighed")
        attn_ready = sem("attn_ready")
        pe_pt = sem("pe_pt")
        act_pt = sem("act_pt")
        dve_pt = sem("dve_pt")
        pe_av = sem("pe_av")
        act_av = sem("act_av")
        pe_ax = sem("pe_ax")
        act_ax = sem("act_ax")
        dve_ax = sem("dve_ax")
        pe_o = sem("pe_o")
        act_hi = sem("act_hi")
        act_o = sem("act_o")
        dve_o = sem("dve_o")
        pool_sq = sem("pool_sq")
        pe_stat = sem("pe_stat")
        dve_stat = sem("dve_stat")
        pool_rinv = sem("pool_rinv")
        pe_f = sem("pe_f")
        dve_f = sem("dve_f")
        hi_qk = sem("hi_qk")
        lo_qk = sem("lo_qk")
        hi_v = sem("hi_v")
        lo_v = sem("lo_v")
        hi_o = sem("hi_o")
        lo_o = sem("lo_o")
        stat3 = sem("stat3")
        h2_ready = sem("h2_ready")
        pe_h2t = sem("pe_h2t")
        act_h2t = sem("act_h2t")
        dve_h2t = sem("dve_h2t")
        pe_route = sem("pe_route")
        logit_t = sem("logit_t")
        logit_ready = sem("logit_ready")
        top_ready = sem("top_ready")
        diff_ready = sem("diff_ready")
        index_ready = sem("index_ready")
        exp_ready = sem("exp_ready")
        weight_part = sem("weight_part")
        gate_part = sem("gate_part")
        gate_ready = sem("gate_ready")
        pe_gt = sem("pe_gt")
        gt_ready = sem("gt_ready")
        hi_12 = sem("hi_12")
        lo_12 = sem("lo_12")
        hi_3 = sem("hi_3")
        lo_3 = sem("lo_3")
        pe_up = sem("pe_up")
        act_sil = sem("act_sil")
        pool_gate = sem("pool_gate")
        dve_h = sem("dve_h")
        act_h = sem("act_h")
        dve_hl = sem("dve_hl")
        pe_dn = sem("pe_dn")
        y_first = sem("y_first")
        y_second = sem("y_second")
        pe_yt = sem("pe_yt")
        y_tok = sem("y_tok")
        stat4 = sem("stat4")
        y_done = sem("y_done")
        iota_ready = sem("iota_ready")
        ld_x = [sem(f"ld_x{t}") for t in range(TILES)]
        ld_qk = [sem(f"ld_qk{i}") for i in range(2)]
        ld_v = [sem(f"ld_v{i}") for i in range(2)]
        ld_o = [sem(f"ld_o{i}") for i in range(2)]
        ld_12 = [sem(f"ld_12_{i}") for i in range(2)]
        ld_3 = [sem(f"ld_3_{i}") for i in range(2)]
        ld_g = [sem(f"ld_g{i}") for i in range(4)]
        block = ctx.enter_context(nc.Block())

        def tcols(t):
            return slice(P * t, P * t + TROWS[t])

        def up_rows(c):
            return SHARED0 if c == 0 else P

        @block.sync
        def _(sp):
            for t in range(TILES):
                sp.dma_start(xr[0:TROWS[t], t, :], x[P * t:P * t + TROWS[t], :]).then_inc(ld_x[t], 16)
                if t == 0:
                    sp.dma_start(ident[:], ident_d).then_inc(ld_ident, 16)
                    sp.dma_start(cst[:], consts).then_inc(ld_tw, 16)
                    sp.dma_start(tw[:], tokw).then_inc(ld_tw, 16)
            sp.dma_start(qk_raw[:, 0, :], wqk[0, :, :]).then_inc(ld_qk[0], 16)
            sp.dma_start(g2b[:], g2.broadcast_to([P, D])).then_inc(ld_const, 16)
            sp.dma_start(pet[:, 0:4, :], pe_tab[0:512, :].rearrange("(t p) d -> p t d", p=P)).then_inc(ld_const, 16)
            sp.dma_start(pet[0:64, 4, :], pe_tab[512:TOK, :]).then_inc(ld_const, 16)
            sp.dma_start(wgr[:], wg).then_inc(ld_const, 16)
            sp.dma_start(mask[:], masks).then_inc(ld_mask, 16)
            sp.dma_start(qk_raw[:, 1, :], wqk[1, :, :]).then_inc(ld_qk[1], 16)
            for i in range(2):
                sp.dma_start(v_raw[:, i, :], wv[i, :, :]).then_inc(ld_v[i], 16)
                sp.dma_start(o_raw[:, i, :], wo[i, :, :]).then_inc(ld_o[i], 16)
            for t in range(TILES):
                sp.wait_ge(h_ready, t + 1)
                sp.dma_start(h_dram[P * t:P * t + TROWS[t], :], h[0:TROWS[t], t, :]).then_inc(h_stored, 16)
            sp.wait_ge(h_stored, 16 * TILES)
            h_halves = h_dram.rearrange("(i p) d -> p i d", i=2)
            for g in range(GRPS):
                sp.dma_start(xg_raw.rearrange("p (i g) d -> p i g d", i=2)[0:GROWS[g], :, g, :],
                             h_halves[GRP * g:GRP * g + GROWS[g], :, :]).then_inc(ld_xg, 16)
            sp.dma_start(r12[:, 0, :, :, 0:SHARED0], s12).then_inc(ld_12[0], 16)
            sp.dma_start(r3[0:SHARED0, 0, :], s3).then_inc(ld_3[0], 16)
            sp.dma_start(r12[:, 1, :, :, :], w12[0, :, :]).then_inc(ld_12[1], 16)
            sp.dma_start(r3[:, 1, :], w3[0, :, :]).then_inc(ld_3[1], 16)

            def head_pair(i):
                for r in range(2):
                    hd = 2 + 2 * i + r
                    sp.wait_ge(lo_qk, 2 * i + r + 1)
                    sp.dma_start(qk_raw[:, r, :], wqk[bass.ds(hd, 1), :, :].rearrange("a p n -> p (a n)")).then_inc(ld_qk[r], 16)
                    sp.wait_ge(lo_v, 2 * i + r + 1)
                    sp.dma_start(v_raw[:, r, :], wv[bass.ds(hd, 1), :, :].rearrange("a p n -> p (a n)")).then_inc(ld_v[r], 16)
                    sp.wait_ge(lo_o, 2 * i + r + 1)
                    sp.dma_start(o_raw[:, r, :], wo[bass.ds(hd, 1), :, :].rearrange("a p n -> p (a n)")).then_inc(ld_o[r], 16)

            with sp.Fori(0, HEADS // 2 - 1) as i:
                head_pair(i)
            def load_gate(i, r):
                rows = g_dram[bass.ds(4 * i, 4), :].unsqueeze(1).broadcast_to([4, 32, TOK])
                sp.dma_start(gates[:, r, :], rows).then_inc(ld_g[r], 16)

            def load_w(c, r):
                sp.wait_ge(lo_12, c - 1)
                sp.dma_start(r12[:, r, :, :, :], w12[bass.ds(c - 1, 1), :, :].rearrange("a p n -> p (a n)")).then_inc(ld_12[r], 16)
                sp.wait_ge(lo_3, c - 1)
                sp.dma_start(r3[:, r, :], w3[bass.ds(c - 1, 1), :, :].rearrange("a p n -> p (a n)")).then_inc(ld_3[r], 16)

            for c in range(2, 5):
                load_w(c, c % 2)
            sp.wait_ge(gt_ready, 1)
            sp.dma_start(g_dram.rearrange("(e k) n -> e k n", k=11),
                         gateT[:, :].unsqueeze(1).broadcast_to([EXPERTS, 11, TOK])).then_inc(g_stored, 16)
            for c in range(5, 7):
                load_w(c, c % 2)
            sp.wait_ge(g_stored, 16)
            for r in range(4):
                load_gate(r, r)
            for c in range(7, 10):
                load_w(c, c % 2)

            def gate_rest(c, r4):
                sp.wait_ge(pool_gate, 2 * (c - 4 - SHARED_CHUNKS) + 2)
                load_gate(c - SHARED_CHUNKS, r4)
                load_w(c, r4 % 2)

            with sp.Fori(0, 4) as i:
                for r in range(4):
                    gate_rest(10 + 4 * i + r, r)
            for r in range(2):
                gate_rest(26 + r, r)
            for t in range(TILES):
                sp.wait_ge(y_done, t + 1)
                sp.dma_start(out[P * t:P * t + TROWS[t], :], h[0:TROWS[t], t, :]).then_inc(out_stored, 16)
            sp.wait_ge(out_stored, 16 * TILES)

        def group_blocks(i):
            last = GRPS * i + GRPS - 1
            return (slice(0, GRP), slice(GRPS * i, last)), (slice(0, GROWS[-1]), slice(last, last + 1))

        def mm3(o, lhs, rhs, first, last):
            nc.tensor.matmul(o, lhs[0], rhs[0], start=first, stop=False)
            nc.tensor.matmul(o, lhs[0], rhs[1], start=False, stop=False)
            return nc.tensor.matmul(o, lhs[1], rhs[0], start=False, stop=last)

        @block.tensor
        def _(pe):
            def keep_busy(n, bank):
                for _ in range(n):
                    nc.tensor.matmul(ps[:, bank, 0:P], ones[:, :], ones[:, :], start=True, stop=True)

            pe.wait_ge(mem_ready, 1)
            keep_busy(16, 7)
            pe.wait_ge(ld_ident, 16)

            def patch_transposes(t):
                n = TROWS[t]
                pe.wait_ge(xn_ready, t + 1)
                if t >= 2:
                    pe.wait_ge(dve_t, 2 * (t - 1))
                for k in range(KC):
                    l = nc.tensor.transpose(ps[:, 2 * (t % 2) + k // 3, P * (k % 3):P * (k % 3) + n],
                                            xr[0:n, t, P * k:P * k + P], ident[0:n, 0:n])
                    if k % 3 == 2:
                        l.then_inc(pe_t, 1)

            def token_product(t):
                n = TROWS[t]
                pe.wait_ge(dve_t, 2 * (t + 1))
                if t == 0:
                    pe.wait_ge(tw_lo, KC)
                if t >= 3:
                    pe.wait_ge(h_part, t - 2)
                for k in range(KC):
                    l = mm3(ps[0:n, 4 + t % 3, 0:D], [a[:, k, tcols(t)] for a in xT], [a[:, k, :] for a in tws],
                            k == 0, k == KC - 1)
                l.then_inc(pe_z, 1)

            def h_transposes(t):
                n = TROWS[t]
                pe.wait_ge(h_ready, t + 1)
                if t >= 1:
                    pe.wait_ge(dve_ht, t)
                for k in range(DC):
                    l = nc.tensor.transpose(ps[:, 7, P * k:P * k + n], h[0:n, t, P * k:P * k + P], ident[0:n, 0:n])
                l.then_inc(pe_ht, 1)

            def lambda_sums():
                pe.wait_ge(mem_ready, 1)
                pe.wait_ge(lam_prod, 1)
                nc.tensor.matmul(ps[:, 7, 0:2 * HEADS], ones[:, :], lprod[:, :], start=True, stop=True).then_inc(pe_lam, 1)

            patch_transposes(0)
            lambda_sums()
            keep_busy(12, 6)
            patch_transposes(1)
            token_product(0)
            token_product(1)
            patch_transposes(2)
            patch_transposes(3)
            token_product(2)
            patch_transposes(4)
            pe.wait_ge(lam_exp, 1)
            h_transposes(0)
            token_product(3)
            h_transposes(1)
            token_product(4)
            h_transposes(2)

            def project(u, it, j):
                hd, hs, bank = u // 2, (u // 2) % 2, j
                if j == 0:
                    pe.wait_ge(lo_qk, hd + 1 + 2 * it)
                    if u <= 1:
                        pe.wait_ge(dve_ht, 3 if u == 0 else TILES)
                if u >= 3:
                    if j < 2:
                        pe.wait_ge(dve_ax, 2 * (u - 3) + j + 1 + 8 * it)
                    else:
                        pe.wait_ge(dve_o, 2 * (u - 3) + j - 1 + 8 * it)
                c0 = (j % 2) * 2 * D + (j // 2) * P
                cols = slice(HALF * (u % 2), HALF * (u % 2) + HALF)
                for k in range(DC):
                    l = mm3(ps[:, bank, 0:HALF], [a[:, hs, c0 + k * D:c0 + k * D + P] for a in qks],
                            [a[:, k, cols] for a in hT], k == 0, k == DC - 1)
                l.then_inc(pe_q, 1)

            def scores(u, it):
                if u == 0:
                    pe.wait_ge(dve_zero, 1)
                pe.wait_ge(act_q, 4 * u + 4 + 4 * 4 * it)
                if u >= 1:
                    pe.wait_ge(dve_mask, u + 4 * it)
                for j in range(2):
                    for g in range(GRPS):
                        n = GROWS[g]
                        c = slice(GRP * g, GRP * g + n)
                        l = nc.tensor.matmul(ps[0:n, 4 + j, c], qkT[:, 2 * j, c], qkT[:, 2 * j + 1, c],
                                             start=True, stop=True)
                l.then_inc(pe_s, 1)

            def attn_transpose(s, it):
                u = s - 1
                pe.wait_ge(attn_ready, u + 1 + 4 * it)
                if s >= 4:
                    if s % 2 == 0:
                        pe.wait_ge(dve_f, 5 * ((s - 4) // 2) + 3 + 10 * it)
                    else:
                        pe.wait_ge(dve_f, 5 * ((s - 5) // 2) + 5 + 10 * it)
                for g in range(GRPS):
                    n = GROWS[g]
                    l = nc.tensor.transpose(ps[0:GRP, 6, GRP * g:GRP * g + n], attn[0:n, g, :], ident[0:n, 0:n])
                l.then_inc(pe_pt, 1)

            def attend(u, it):
                pe.wait_ge(dve_pt, u + 1 + 4 * it)
                if u <= 1:
                    pe.wait_ge(xg_lo, u + 1)
                for b in range(2):
                    if u + 2 < UNITS:
                        pe.wait_ge(act_q, 4 * (u + 2) + b + 1 + 16 * it)
                    else:
                        pe.wait_ge(dve_ax, 2 * (u - 1) + b + 1)
                    for g in range(2 * b, min(2 * b + 2, GRPS)):
                        n = GROWS[g]
                        l = mm3(ps[0:n, b, D * (g % 2):D * (g % 2) + D], [a[0:n, GRP * g:GRP * g + n] for a in aT],
                                [a[0:n, GRPS * (u % 2) + g, :] for a in xg], True, True)
                    l.then_inc(pe_av, 1)

            def ax_transposes(u, it):
                pe.wait_ge(act_av, 2 * u + 2 + 8 * it)
                for k in range(DC):
                    for g in range(GRPS):
                        n = GROWS[g]
                        l = nc.tensor.transpose(ps[:, k, GRP * g:GRP * g + n], ax[0:n, g, P * k:P * k + P],
                                                ident[0:n, 0:n])
                    l.then_inc(pe_ax, 1)

            def values(u, it):
                hd, hs = u // 2, (u // 2) % 2
                if u % 2 == 0:
                    pe.wait_ge(lo_v, hd + 1 + 2 * it)
                for e in range(DC):
                    if u + 2 < UNITS:
                        pe.wait_ge(act_q, 4 * (u + 2) + e + 3 + 16 * it)
                    else:
                        pe.wait_ge(dve_o, 2 * (u - 1) + e + 1)
                    for k in range(DC):
                        if e == 0:
                            pe.wait_ge(dve_ax, 2 * u + k + 1 + 8 * it)
                        l = mm3(ps[:, 2 + e, 0:HALF], [a[:, hs, k * D + P * e:k * D + P * e + P] for a in vs],
                                [a[:, k, :] for a in axT], k == 0, k == DC - 1)
                    l.then_inc(pe_o, 1)

            def sum_squares(hd, t, bank):
                return nc.tensor.matmul(ps[0:TROWS[t], bank, t:t + 1], sqs[:, hd % 2, tcols(t)], ones[:, 0:1],
                                        start=True, stop=True)

            def square_sums(hd, it):
                pe.wait_ge(pool_sq, 2 * hd + 2 + 4 * it)
                if hd >= 1:
                    pe.wait_ge(dve_f, 5 * hd + 10 * it)
                for t in range(TILES):
                    l = sum_squares(hd, t, 7)
                l.then_inc(pe_stat, 1)

            def output_tile(hd, t, bank):
                for k in range(DC):
                    l = mm3(ps[0:TROWS[t], bank, 0:D], [a[:, hd % 2, k, tcols(t)] for a in oT],
                            [a[:, hd % 2, k * D:k * D + D] for a in os_], k == 0, k == DC - 1)
                l.then_inc(pe_f, 1)

            def output_tiles(hd, it, tiles):
                for t in tiles:
                    if t == 0:
                        pe.wait_ge(lo_o, hd + 1 + 2 * it)
                        pe.wait_ge(dve_o, 4 * hd + 4 + 8 * it)
                        if hd >= 1:
                            pe.wait_ge(dve_f, 5 * hd + 10 * it)
                    elif t == 1:
                        pe.wait_ge(dve_stat, hd + 1 + 2 * it)
                    else:
                        pe.wait_ge(dve_f, 5 * hd + t - 1 + 10 * it)
                    output_tile(hd, t, F_BANK[t])

            h_transposes(3)
            for j in range(4):
                project(0, 0, j)
            h_transposes(4)
            keep_busy(4, 6)
            scores(0, 0)

            def step(s, it=0):
                if s + 1 < UNITS:
                    project(s + 1, it, 0)
                    project(s + 1, it, 1)
                if 1 <= s <= UNITS:
                    attn_transpose(s, it)
                if s + 1 < UNITS:
                    project(s + 1, it, 2)
                if s % 2 == 1 and s >= 3:
                    square_sums((s - 3) // 2, it)
                if s + 1 < UNITS:
                    project(s + 1, it, 3)
                if 1 <= s <= UNITS:
                    attend(s - 1, it)
                if s >= 3:
                    if s % 2 == 1:
                        output_tiles((s - 3) // 2, it, (0, 1))
                    else:
                        output_tiles((s - 4) // 2, it, (3, 4))
                if s <= 2:
                    keep_busy(4, 6)
                if 1 <= s <= UNITS:
                    ax_transposes(s - 1, it)
                if s >= 3 and s % 2 == 1:
                    output_tiles((s - 3) // 2, it, (2,))
                if s + 1 < UNITS:
                    scores(s + 1, it)
                if 1 <= s <= UNITS:
                    values(s - 1, it)

            for s in range(0, 4):
                step(s)
            with pe.Fori(0, 2) as i:
                for r in range(4):
                    step(4 + r, i)
            for s in range(12, 15):
                step(s)

            attn_transpose(15, 0)
            keep_busy(8, 0)
            square_sums(6, 0)
            attend(14, 0)
            output_tiles(6, 0, (0, 1))
            ax_transposes(14, 0)
            output_tiles(6, 0, (2, 3))
            values(14, 0)
            attn_transpose(16, 0)
            output_tile(6, 4, 4)
            attend(15, 0)
            pe.wait_ge(pool_sq, 15)
            for t in range(2):
                l = sum_squares(7, t, 5)
            l.then_inc(pe_stat, 1)
            pe.wait_ge(lo_o, HEADS)
            pe.wait_ge(dve_o, 30)
            output_tile(7, 0, 6)
            pe.wait_ge(dve_f, 34)
            output_tile(7, 1, 7)
            ax_transposes(15, 0)
            pe.wait_ge(dve_f, 35)
            keep_busy(5, 4)
            values(15, 0)

            def h2_transposes(t):
                n = TROWS[t]
                pe.wait_ge(h2_ready, t + 1)
                for k in range(DC):
                    l = nc.tensor.transpose(ps[:, t, P * k:P * k + n], h[0:n, t, P * k:P * k + P], ident[0:n, 0:n])
                l.then_inc(pe_h2t, 1)

            pe.wait_ge(dve_ax, 2 * UNITS)
            keep_busy(8, 0)
            pe.wait_ge(pool_sq, UNITS)
            pe.wait_ge(dve_stat, HEADS)
            for t in range(2, TILES):
                l = sum_squares(7, t, 5)
            l.then_inc(pe_stat, 1)
            pe.wait_ge(dve_o, 2 * UNITS)
            pe.wait_ge(dve_f, 36)
            output_tile(7, 2, 6)
            pe.wait_ge(dve_f, 37)
            output_tile(7, 3, 7)
            output_tile(7, 4, 4)
            h2_transposes(0)
            h2_transposes(1)
            pe.wait_ge(dve_stat, 9)
            keep_busy(6, 5)
            h2_transposes(2)
            h2_transposes(3)
            keep_busy(2, 5)

            def up(v, it=0, halves=(0, 1)):
                c, cs, m = v // 2, (v // 2) % 2, up_rows(v // 2)
                cols = slice(HALF * (v % 2), HALF * (v % 2) + HALF)
                if v <= 1:
                    pe.wait_ge(dve_h2t, 3 + 2 * v)
                if v % 2 == 0:
                    pe.wait_ge(lo_12, c + 1 + 2 * it)
                if v >= 2:
                    pe.wait_ge(act_sil, v - 1 + 4 * it)
                for i in halves:
                    if v >= 2 and i == 1:
                        pe.wait_ge(dve_h, v - 1 + 4 * it)
                    for k in range(DC):
                        l = mm3(ps[0:m, 2 * (v % 2) + i, 0:HALF], [a[:, cs, i, k, 0:m] for a in w12s],
                                [a[:, k, cols] for a in h2T], k == 0, k == DC - 1)
                    l.then_inc(pe_up, 1)

            def down(v, it=0):
                c, cs, m = v // 2, (v // 2) % 2, up_rows(v // 2)
                if v % 2 == 0:
                    pe.wait_ge(lo_3, c + 1 + 2 * it)
                pe.wait_ge(dve_hl, v + 1 + 4 * it)
                for k in range(DC):
                    l = mm3(ps[:, 4 + 2 * (v % 2) + k, 0:HALF], [a[0:m, cs, P * k:P * k + P] for a in w3s],
                            [a[0:m, v % 2, :] for a in hh], c == 0, c == CHUNKS - 1)
                l.then_inc(pe_dn, 1)

            up(0, 0, (0,))
            h2_transposes(4)
            up(0, 0, (1,))
            up(1)
            pe.wait_ge(wg_split, 2)
            for b in range(2):
                for k in range(DC):
                    l = mm3(ps[0:EXPERTS, 6 + b, 0:HALF], [a[:, k, :] for a in wgs],
                            [a[:, k, HALF * b:HALF * b + HALF] for a in h2T], k == 0, k == DC - 1)
            l.then_inc(pe_route, 1)
            up(2)
            pe.wait_ge(logit_t, 2)
            for t in range(TILES):
                l = nc.tensor.transpose(ps[0:TROWS[t], 6, EXPERTS * t:EXPERTS * t + EXPERTS], logitT[:, tcols(t)],
                                        ident[0:EXPERTS, 0:EXPERTS])
            l.then_inc(pe_route, 1)
            down(0)
            up(3)
            pe.wait_ge(logit_ready, 1)
            down(1)
            up(4)
            down(2)
            up(5)
            pe.wait_ge(gate_ready, 1)
            pe.wait_ge(act_sil, 5)
            pe.wait_ge(dve_h, 5)
            for t in range(TILES):
                l = nc.tensor.transpose(ps[0:EXPERTS, t // 3, P * (t % 3):P * (t % 3) + TROWS[t]],
                                        gate[0:TROWS[t], 0, t, :], ident[0:TROWS[t], 0:TROWS[t]])
            l.then_inc(pe_gt, 1)
            down(3)
            with pe.Fori(0, 12) as i:
                pe.wait_ge(gt_ready, 1)
                for r in range(4):
                    up(6 + r, i)
                    down(4 + r, i)
            for v in range(52, 56):
                if v + 2 < 2 * CHUNKS:
                    up(v + 2)
                down(v)
            for t in range(TILES):
                n = TROWS[t]
                if t == 0:
                    pe.wait_ge(y_first, 2)
                elif t == 2:
                    pe.wait_ge(y_second, 2)
                if t >= 4:
                    pe.wait_ge(y_tok, t - 3)
                for k in range(DC):
                    l = nc.tensor.transpose(ps[0:n, t % 4, P * k:P * k + P], yT[:, k, tcols(t)], ident[:, :])
                l.then_inc(pe_yt, 1)

        @block.scalar
        def _(act):
            def copy(o, i, scale=1.0):
                return nc.scalar.activation(o, i, ACT.Copy, scale=scale)

            def patch_apply(t):
                n = TROWS[t]
                act.wait_ge(nmr_ready, t + 1)
                nc.scalar.activation(xr[0:n, t, :], xr[0:n, t, :], ACT.Identity, bias=nmr[0:n, t:t + 1],
                                     scale=rstd[0:n, t:t + 1]).then_inc(xn_ready, 1)

            def patches_hi(t):
                n = TROWS[t]
                for b in range(2):
                    act.wait_ge(pe_t, 2 * t + b + 1)
                    copy(xT[0][:, 3 * b:3 * b + 3, tcols(t)],
                         ps[:, 2 * (t % 2) + b, 0:384].rearrange("p (k n) -> p k n", k=3)[:, :, 0:n]).then_inc(act_t, 1)

            def h_hi(t):
                n = TROWS[t]
                act.wait_ge(pe_ht, t + 1)
                copy(hT[0][:, :, tcols(t)],
                     ps[:, 7, 0:D].rearrange("p (k n) -> p k n", k=DC)[:, :, 0:n]).then_inc(act_ht, 1)

            patch_apply(0)
            act.wait_ge(ld_tw, 32)
            for k in range(KC):
                copy(tws[0][:, k, :], tw[:, k, :], gam1[:, k:k + 1]).then_inc(tw_hi, 1)
            patches_hi(0)
            patch_apply(1)
            act.wait_ge(pe_lam, 1)
            nc.scalar.activation(lexp[:], ps[:, 7, 0:2 * HEADS], ACT.Exp).then_inc(lam_exp, 1)
            patches_hi(1)
            act.wait_ge(ld_qk[0], 16)
            copy(qks[0][:, 0, :], qk_raw[:, 0, :]).then_inc(hi_qk, 1)
            patch_apply(2)
            patch_apply(3)
            patches_hi(2)
            patch_apply(4)
            patches_hi(3)
            h_hi(0)
            patches_hi(4)
            h_hi(1)
            h_hi(2)

            def proj_copy(u, it, j):
                act.wait_ge(pe_q, 4 * u + j + 1 + 16 * it)
                copy(qkT[:, j, :], ps[:, j, 0:HALF]).then_inc(act_q, 1)

            def attn_hi(u, it):
                act.wait_ge(pe_pt, u + 1 + 4 * it)
                copy(aT[0][:], ps[0:GRP, 6, 0:HALF]).then_inc(act_pt, 1)

            def exponentials(u, it):
                act.wait_ge(dve_sub, u + 1 + 4 * it)
                nc.scalar.activation(prob[:], prob[:], ACT.Exp, scale=SCALE).then_inc(act_exp, 1)

            def ax_copies(u, it):
                for b in range(2):
                    act.wait_ge(pe_av, 2 * u + b + 1 + 8 * it)
                    if u >= 1:
                        act.wait_ge(pe_ax, 2 * u + 8 * it)
                    n, rows = min(2, GRPS - 2 * b), GROWS[2 * b]
                    copy(ax[0:rows, 2 * b:2 * b + n, :],
                         ps[0:rows, b, 0:n * D].rearrange("p (g d) -> p g d", g=n)).then_inc(act_av, 1)

            def ax_hi(u, it):
                for k in range(DC):
                    act.wait_ge(pe_ax, 2 * u + k + 1 + 8 * it)
                    copy(axT[0][:, k, :], ps[:, k, 0:HALF]).then_inc(act_ax, 1)

            def o_hi(u, it, e):
                act.wait_ge(pe_o, 2 * u + e + 1 + 8 * it)
                copy(oT[0][:, (u // 2) % 2, e, HALF * (u % 2):HALF * (u % 2) + HALF], ps[:, 2 + e, 0:HALF],
                     rms[:, e:e + 1]).then_inc(act_hi, 1)
                if u >= 1 and e == 0:
                    act.wait_ge(pool_sq, u + 4 * it)
                nc.scalar.activation(sq[:, e, :], ps[:, 2 + e, 0:HALF], ACT.Square).then_inc(act_o, 1)

            def groups_hi(i):
                if i == 0:
                    act.wait_ge(ld_xg, 16 * GRPS)
                for rows, g in group_blocks(i):
                    l = copy(xg[0][rows, g, :], xg_raw[rows, g, :])
                l.then_inc(xg_hi, 1)

            def step(s, it=0):
                if s + 1 < UNITS:
                    proj_copy(s + 1, it, 0)
                    proj_copy(s + 1, it, 1)
                if 1 <= s <= UNITS:
                    attn_hi(s - 1, it)
                if s + 1 < UNITS:
                    proj_copy(s + 1, it, 2)
                if s % 2 == 0 and s >= 1 and s + 1 < UNITS:
                    proj_copy(s + 1, it, 3)
                if s == 1:
                    ax_copies(0, 0)
                if 0 <= s < UNITS:
                    exponentials(s, it)
                if (s == 0 or s % 2 == 1) and s + 1 < UNITS:
                    proj_copy(s + 1, it, 3)
                if s == 0:
                    groups_hi(0)
                if 2 <= s <= UNITS:
                    ax_copies(s - 1, it)
                if s % 2 == 0 and s < UNITS:
                    hd = s // 2
                    if hd >= 2:
                        act.wait_ge(pe_o, 4 * (hd - 1) + 8 * it)
                    act.wait_ge(ld_v[hd % 2], 16 * (hd // 2 + 1 + it))
                    copy(vs[0][:, hd % 2, :], v_raw[:, hd % 2, :]).then_inc(hi_v, 1)
                if 1 <= s <= UNITS:
                    ax_hi(s - 1, it)
                if s % 2 == 1 and (s + 3) // 2 < HEADS:
                    hd = (s + 3) // 2
                    if hd >= 2:
                        act.wait_ge(pe_q, 8 * (hd - 1) + 16 * it)
                    act.wait_ge(ld_qk[hd % 2], 16 * (hd // 2 + 1 + it))
                    copy(qks[0][:, hd % 2, :], qk_raw[:, hd % 2, :]).then_inc(hi_qk, 1)
                if 1 <= s <= UNITS:
                    for e in range(DC):
                        o_hi(s - 1, it, e)
                if s % 2 == 0 and s < UNITS:
                    if hd >= 2:
                        act.wait_ge(pe_f, 5 * (hd - 1) + 10 * it)
                    act.wait_ge(ld_o[hd % 2], 16 * (hd // 2 + 1 + it))
                    copy(os_[0][:, hd % 2, :], o_raw[:, hd % 2, :]).then_inc(hi_o, 1)

            h_hi(3)
            for j in range(4):
                proj_copy(0, 0, j)
            h_hi(4)
            act.wait_ge(ld_qk[1], 16)
            copy(qks[0][:, 1, :], qk_raw[:, 1, :]).then_inc(hi_qk, 1)
            step(0)
            groups_hi(1)
            for s in range(1, 4):
                step(s)
            with act.Fori(0, 2) as i:
                for r in range(4):
                    step(4 + r, i)
            for s in range(12, 15):
                step(s)
            attn_hi(14, 0)
            exponentials(15, 0)
            ax_copies(14, 0)
            ax_hi(14, 0)
            o_hi(14, 0, 0)
            attn_hi(15, 0)
            o_hi(14, 0, 1)
            ax_copies(15, 0)
            ax_hi(15, 0)
            o_hi(15, 0, 0)
            o_hi(15, 0, 1)

            def h2_hi(t):
                n = TROWS[t]
                act.wait_ge(pe_h2t, t + 1)
                copy(h2T[0][:, :, tcols(t)],
                     ps[:, t, 0:D].rearrange("p (k n) -> p k n", k=DC)[:, :, 0:n]).then_inc(act_h2t, 1)

            for t in range(4):
                h2_hi(t)

            def silu(v, it=0):
                m = up_rows(v // 2)
                act.wait_ge(pe_up, 2 * v + 1 + 8 * it)
                if v >= 2:
                    act.wait_ge(dve_h, v - 1 + 4 * it)
                nc.scalar.activation(sil[0:m, v % 2, :], ps[0:m, 2 * (v % 2), 0:HALF], ACT.Silu).then_inc(act_sil, 1)

            def hidden_hi(v, it=0):
                m = up_rows(v // 2)
                act.wait_ge(dve_h, v + 1 + 4 * it)
                if v >= 2:
                    act.wait_ge(pe_dn, v - 1 + 4 * it)
                copy(hh[0][0:m, v % 2, :], hraw[0:m, v % 2, :]).then_inc(act_h, 1)

            h2_hi(4)
            silu(0)
            for v in range(4):
                silu(v + 1)
                hidden_hi(v)
                if v == 0:
                    act.wait_ge(pe_route, 1)
                    for b in range(2):
                        copy(logitT[:, HALF * b:HALF * b + HALF], ps[0:EXPERTS, 6 + b, 0:HALF]).then_inc(logit_t, 1)
            with act.Fori(0, 12) as i:
                for r in range(4):
                    silu(5 + r, i)
                    hidden_hi(4 + r, i)
            for v in range(52, 2 * CHUNKS):
                if v + 1 < 2 * CHUNKS:
                    silu(v + 1)
                hidden_hi(v)
            act.wait_ge(pe_dn, 2 * CHUNKS)
            copy(yT[:, 0, HALF:TOK], ps[:, 6, 0:HALF]).then_inc(y_second, 1)

        @block.vector
        def _(dve):
            V = nc.vector

            V.memset(mhalf[:], -0.5)
            V.memset(euler[:], 2.718281828459045)
            V.memset(ones[:], 1.0)
            V.memset(logit[:], 0.0)
            V.memset(ms[:], 1.0)
            V.memset(mv[:], 1.0).then_inc(mem_ready, 1)
            dve.wait_ge(mem_ready, 1)

            def lambda_products():
                dve.wait_ge(ld_tw, 32)
                V.tensor_tensor(lprod[:, :].rearrange("p (i h) -> p i h", i=2), lam4[:, :, 0, :], lam4[:, :, 1, :],
                                ALU.mult).then_inc(lam_prod, 1)

            def tok_weights_lo():
                for k in range(KC):
                    dve.wait_ge(tw_hi, k + 1)
                    V.scalar_tensor_tensor(tws[1][:, k, :], tw[:, k, :], gam1[:, k:k + 1], tws[0][:, k, :].bitcast(F32),
                                           ALU.mult, ALU.subtract).then_inc(tw_lo, 1)

            def patch_norm(t):
                n = TROWS[t]
                dve.wait_ge(ld_x[t], 16)
                for b in range(2):
                    l = V.bn_stats(bns[0:n, t, b, :], xr[0:n, t, 384 * b:384 * b + 384])
                l.then_inc(stat1, 1)
                dve.wait_ge(stat1, 2 * t + 1)
                V.bn_aggr(mv[0:n, t, :], bns[0:n, t, :, :].rearrange("p b s -> p (b s)")).then_inc(stat1, 1)

            def patches_lo(t):
                n = TROWS[t]
                for b in range(2):
                    dve.wait_ge(act_t, 2 * t + b + 1)
                    c = slice(3 * b, 3 * b + 3)
                    V.tensor_tensor(xT[1][:, c, tcols(t)],
                                    ps[:, 2 * (t % 2) + b, 0:384].rearrange("p (k n) -> p k n", k=3)[:, :, 0:n],
                                    xT[0][:, c, tcols(t)].bitcast(F32), ALU.subtract).then_inc(dve_t, 1)

            def token_stats(t):
                n = TROWS[t]
                dve.wait_ge(pe_z, t + 1)
                V.bn_stats(bns[0:n, t, 0, :], ps[0:n, 4 + t % 3, 0:D]).then_inc(stat2, 1)
                dve.wait_ge(stat2, 2 * t + 1)
                dve.wait_ge(xn_ready, t + 1)
                V.bn_aggr(mv[0:n, t, :], bns[0:n, t, 0, :]).then_inc(stat2, 1)

            def token_norm(t):
                n = TROWS[t]
                if t == 0:
                    dve.wait_ge(ld_const, 16 * 4)
                dve.wait_ge(stat2, 2 * t + 2)
                V.scalar_tensor_tensor(h[0:n, t, :], ps[0:n, 4 + t % 3, 0:D], mv[0:n, t, 0:1], g2b[0:n, :],
                                       ALU.subtract, ALU.mult).then_inc(h_part, 1)
                dve.wait_ge(h_part, t + 1)
                dve.wait_ge(rstd2, t + 1)
                V.scalar_tensor_tensor(h[0:n, t, :], h[0:n, t, :], rstd[0:n, t:t + 1], pet[0:n, t, :],
                                       ALU.mult, ALU.add).then_inc(h_ready, 1)

            def h_lo(t):
                n = TROWS[t]
                dve.wait_ge(act_ht, t + 1)
                V.tensor_tensor(hT[1][:, :, tcols(t)],
                                ps[:, 7, 0:D].rearrange("p (k n) -> p k n", k=DC)[:, :, 0:n],
                                hT[0][:, :, tcols(t)].bitcast(F32), ALU.subtract).then_inc(dve_ht, 1)

            patch_norm(0)
            lambda_products()
            patch_norm(1)
            tok_weights_lo()
            patches_lo(0)
            patch_norm(2)
            patches_lo(1)
            patch_norm(3)
            token_stats(0)
            patch_norm(4)
            dve.wait_ge(lam_exp, 1)
            V.tensor_tensor(nlam[:], lexp[:, HEADS:2 * HEADS], lexp[:, 0:HEADS], ALU.subtract).then_inc(lam_part, 1)
            dve.wait_ge(lam_part, 1)
            V.tensor_scalar(nlam[:], nlam[:], -LAMBDA_INIT, None, ALU.add).then_inc(lam_ready, 1)
            token_norm(0)
            patches_lo(2)
            token_stats(1)
            patches_lo(3)
            token_norm(1)
            h_lo(0)
            token_stats(2)
            patches_lo(4)
            token_norm(2)
            h_lo(1)
            token_stats(3)
            token_norm(3)
            h_lo(2)

            s_view = ps[0:GRP, 4:6, 0:SCORES].rearrange("p j (g n) -> p j g n", g=GRPS)
            m_view = masked[:, :, :].rearrange("p (j g) n -> p j g n", j=2)

            def row_max(u, it):
                if u == 0:
                    dve.wait_ge(ld_mask, 16)
                else:
                    dve.wait_ge(dve_sub, u + 4 * it)
                dve.wait_ge(pe_s, u + 1 + 4 * it)
                for j in range(2):
                    l = V.tensor_tensor(m_view[:, j, :, :], s_view[:, j, :, :],
                                        mask[:].unsqueeze(1).broadcast_to([GRP, GRPS, GRP]), ALU.add)
                l.then_inc(dve_mask, 1)
                if u == 1:
                    attn_lo(0, 0)
                dve.wait_ge(dve_mask, u + 1 + 4 * it)
                V.tensor_reduce(smax[:], masked[:], AX_X, ALU.max).then_inc(dve_max, 1)

            def subtract_max(u, it):
                dve.wait_ge(dve_max, u + 1 + 4 * it)
                if u >= 1:
                    dve.wait_ge(attn_ready, u + 4 * it)
                V.tensor_tensor(prob[:], masked[:], smax[:].unsqueeze(2).broadcast_to([GRP, 2 * GRPS, GRP]),
                                ALU.subtract).then_inc(dve_sub, 1)

            def row_sum(u, it):
                dve.wait_ge(act_exp, u + 1 + 4 * it)
                V.tensor_reduce(ssum[:], prob[:], AX_X, ALU.add).then_inc(dve_sum, 1)

            def row_reciprocal(u, it):
                dve.wait_ge(dve_sum, u + 1 + 4 * it)
                V.reciprocal(rsum[:], ssum[:]).then_inc(dve_rec, 1)

            def lambda_scale(u, it):
                dve.wait_ge(dve_rec, u + 1 + 4 * it)
                lam = nlam[0:GRP, u // 2:u // 2 + 1] if isinstance(it, int) else nlam[0:GRP, bass.ds(u // 2 + 2 * it, 1)]
                V.tensor_scalar(rsum[:, GRPS:2 * GRPS], rsum[:, GRPS:2 * GRPS], lam, None, ALU.mult).then_inc(dve_r, 1)

            def weigh_first():
                dve.wait_ge(dve_r, 1)
                V.tensor_tensor(prob[:], prob[:], rsum[:, :].unsqueeze(2).broadcast_to([GRP, 2 * GRPS, GRP]),
                                ALU.mult).then_inc(weighed, 1)
                dve.wait_ge(weighed, 1)
                V.tensor_tensor(attn[:], prob[:, 0:GRPS, :], prob[:, GRPS:2 * GRPS, :], ALU.add).then_inc(attn_ready, 1)

            def add_tile(t, bank):
                n = TROWS[t]
                V.scalar_tensor_tensor(h[0:n, t, :], ps[0:n, bank, 0:D], rinv[0:n, t:t + 1], h[0:n, t, :],
                                       ALU.mult, ALU.add).then_inc(dve_f, 1)

            def add_tiles(hd, it, tiles):
                for t in tiles:
                    if t == 0:
                        dve.wait_ge(pool_rinv, hd + 1 + 2 * it)
                        if hd >= 1:
                            dve.wait_ge(dve_f, 5 * hd + 10 * it)
                    dve.wait_ge(pe_f, 5 * hd + t + 1 + 10 * it)
                    add_tile(t, F_BANK[t])

            def attn_lo(u, it):
                dve.wait_ge(act_pt, u + 1 + 4 * it)
                V.tensor_tensor(aT[1][:], ps[0:GRP, 6, 0:HALF], aT[0][:].bitcast(F32), ALU.subtract).then_inc(dve_pt, 1)

            def mean_squares(rows, cols, bank):
                c = 1.0 / (OUT_C * OUT_C)
                return V.tensor_scalar(ms[0:rows, cols], ps[0:rows, bank, cols], c / D, EPS * c, ALU.mult, ALU.add)

            def ax_lo(u, it):
                for k in range(DC):
                    dve.wait_ge(act_ax, 2 * u + k + 1 + 8 * it)
                    V.tensor_tensor(axT[1][:, k, :], ps[:, k, 0:HALF], axT[0][:, k, :].bitcast(F32),
                                    ALU.subtract).then_inc(dve_ax, 1)

            def o_lo(u, it, halves=(0, 1)):
                cols = slice(HALF * (u % 2), HALF * (u % 2) + HALF)
                for e in halves:
                    dve.wait_ge(act_o, 2 * u + e + 1 + 8 * it)
                    V.scalar_tensor_tensor(oT[1][:, (u // 2) % 2, e, cols], ps[:, 2 + e, 0:HALF], rms[:, e:e + 1],
                                           oT[0][:, (u // 2) % 2, e, cols].bitcast(F32),
                                           ALU.mult, ALU.subtract).then_inc(dve_o, 1)

            def groups_lo(i):
                dve.wait_ge(xg_hi, i + 1)
                for rows, g in group_blocks(i):
                    l = V.tensor_tensor(xg[1][rows, g, :], xg_raw[rows, g, :], xg[0][rows, g, :].bitcast(F32), ALU.subtract)
                l.then_inc(xg_lo, 1)

            def step(s, it=0):
                if 2 <= s <= UNITS:
                    attn_lo(s - 1, it)
                if 0 <= s < UNITS:
                    subtract_max(s, it)
                if s % 2 == 1 and s >= 3:
                    hd = (s - 3) // 2
                    dve.wait_ge(pe_stat, hd + 1 + 2 * it)
                    if hd >= 1:
                        dve.wait_ge(pool_rinv, hd + 2 * it)
                    mean_squares(P, slice(0, 4), 7)
                    mean_squares(64, slice(4, 5), 7).then_inc(dve_stat, 1)
                hd, tiles = ((s - 3) // 2, [0, 1]) if s % 2 == 1 else ((s - 4) // 2, [3, 4])
                adding = s >= 3
                if 0 <= s < UNITS:
                    row_sum(s, it)
                if adding:
                    add_tiles(hd, it, tiles[0:1])
                if 0 <= s < UNITS:
                    row_reciprocal(s, it)
                if adding:
                    add_tiles(hd, it, tiles[1:2])
                if 0 <= s < UNITS:
                    lambda_scale(s, it)
                if 1 <= s <= UNITS:
                    ax_lo(s - 1, it)
                if adding and s % 2 == 1:
                    add_tiles(hd, it, [2])
                if s == 0:
                    weigh_first()
                    groups_lo(0)
                if s + 1 < UNITS:
                    row_max(s + 1, it)
                if s == 1:
                    groups_lo(1)
                if 1 <= s <= UNITS:
                    o_lo(s - 1, it)

            token_stats(4)
            token_norm(4)
            h_lo(3)
            V.memset(ps[0:GRP, 4:6, SCORES - GRP:SCORES], 0.0).then_inc(dve_zero, 1)
            h_lo(4)
            dve.wait_ge(lam_ready, 1)
            V.tensor_copy(wgs[0][:], wgr[:]).then_inc(wg_split, 1)
            dve.wait_ge(wg_split, 1)
            V.tensor_tensor(wgs[1][:], wgr[:], wgs[0][:].bitcast(F32), ALU.subtract).then_inc(wg_split, 1)
            row_max(0, 0)
            step(0)
            for s in range(1, 4):
                step(s)
            with dve.Fori(0, 2) as i:
                for r in range(4):
                    step(4 + r, i)

            def split12_hi(c, it=0):
                m = up_rows(c)
                if c >= 2:
                    dve.wait_ge(pe_up, 4 * (c - 1) + 8 * it)
                dve.wait_ge(ld_12[c % 2], 16 * (c // 2 + 1 + it))
                V.tensor_copy(w12s[0][:, c % 2, :, :, 0:m], r12[:, c % 2, :, :, 0:m]).then_inc(hi_12, 1)

            def split3_hi(c, it=0):
                m = up_rows(c)
                if c >= 2:
                    dve.wait_ge(pe_dn, 2 * (c - 1) + 4 * it)
                dve.wait_ge(ld_3[c % 2], 16 * (c // 2 + 1 + it))
                V.tensor_copy(w3s[0][0:m, c % 2, :], r3[0:m, c % 2, :]).then_inc(hi_3, 1)

            def split3_lo(c, it=0):
                m = up_rows(c)
                dve.wait_ge(hi_3, c + 1 + 2 * it)
                V.tensor_tensor(w3s[1][0:m, c % 2, :], r3[0:m, c % 2, :], w3s[0][0:m, c % 2, :].bitcast(F32),
                                ALU.subtract).then_inc(lo_3, 1)

            def row_stats(t):
                n = TROWS[t]
                V.bn_stats(bns[0:n, t, 0, :], h[0:n, t, :]).then_inc(stat3, 1)

            def row_mean(t):
                n = TROWS[t]
                dve.wait_ge(stat3, 2 * t + 1)
                V.bn_aggr(mv[0:n, t, :], bns[0:n, t, 0, :]).then_inc(stat3, 1)

            def normalise(t):
                n = TROWS[t]
                dve.wait_ge(rstd3, t + 1)
                V.tensor_scalar(h[0:n, t, :], h[0:n, t, :], mv[0:n, t, 0:1], rstd[0:n, t:t + 1],
                                ALU.subtract, ALU.mult).then_inc(h2_ready, 1)

            def h2_lo(t):
                n = TROWS[t]
                dve.wait_ge(act_h2t, t + 1)
                V.tensor_tensor(h2T[1][:, :, tcols(t)],
                                ps[:, t, 0:D].rearrange("p (k n) -> p k n", k=DC)[:, :, 0:n],
                                h2T[0][:, :, tcols(t)].bitcast(F32), ALU.subtract).then_inc(dve_h2t, 1)

            step(12)
            split12_hi(0)
            split3_hi(0)
            split3_lo(0)
            step(13)
            split12_hi(1)
            step(14)
            attn_lo(14, 0)
            subtract_max(15, 0)
            dve.wait_ge(pe_stat, 7)
            dve.wait_ge(pool_rinv, 6)
            mean_squares(P, slice(0, 4), 7)
            mean_squares(64, slice(4, 5), 7).then_inc(dve_stat, 1)
            row_sum(15, 0)
            row_reciprocal(15, 0)
            lambda_scale(15, 0)
            add_tiles(6, 0, (0, 1))
            ax_lo(14, 0)
            add_tiles(6, 0, (2, 3))
            o_lo(14, 0, (0,))
            attn_lo(15, 0)
            o_lo(14, 0, (1,))
            dve.wait_ge(pe_f, 35)
            add_tile(4, 4)
            dve.wait_ge(pe_stat, 8)
            dve.wait_ge(pool_rinv, 7)
            mean_squares(P, slice(0, 2), 5).then_inc(dve_stat, 1)
            dve.wait_ge(pool_rinv, 8)
            dve.wait_ge(dve_f, 35)
            for t in range(2):
                dve.wait_ge(pe_f, 36 + t)
                add_tile(t, F_BANK[t])
            ax_lo(15, 0)
            for t in range(2):
                dve.wait_ge(dve_f, 36 + t)
                row_stats(t)
                row_mean(t)
            o_lo(15, 0)
            for t in range(2):
                normalise(t)
            dve.wait_ge(pe_stat, 9)
            mean_squares(P, slice(2, 4), 5)
            mean_squares(64, slice(4, 5), 5).then_inc(dve_stat, 1)
            dve.wait_ge(pool_rinv, 9)

            def add_last(t):
                dve.wait_ge(pe_f, 36 + t)
                add_tile(t, (6, 7, 4)[t - 2])

            add_last(2)
            dve.wait_ge(dve_f, 38)
            row_stats(2)
            row_mean(2)
            add_last(3)
            dve.wait_ge(dve_f, 39)
            row_stats(3)
            add_last(4)
            row_mean(3)
            normalise(2)
            dve.wait_ge(dve_f, 40)
            row_stats(4)
            h2_lo(0)
            row_mean(4)
            normalise(3)
            h2_lo(1)
            h2_lo(2)
            normalise(4)
            h2_lo(3)
            h2_lo(4)

            def route_top():
                dve.wait_ge(pe_route, 2)
                V.tensor_copy(logit[:, 0:4, :], ps[:, 6, 0:32].rearrange("p (t e) -> p t e", e=EXPERTS))
                V.tensor_copy(logit[0:64, 4, :], ps[0:64, 6, 32:40]).then_inc(logit_ready, 1)
                dve.wait_ge(logit_ready, 1)
                for t in range(TILES):
                    l = V.max(top[:, t, :], logit[:, t, :])
                l.then_inc(top_ready, 1)
                dve.wait_ge(top_ready, 1)
                V.tensor_tensor(prb[:, :, 0:1], top[:, :, 1:2], top[:, :, 0:1], ALU.subtract).then_inc(diff_ready, 1)
                for t in range(TILES):
                    l = V.max_index(topi[:, t, :], top[:, t, :], logit[:, t, :])
                l.then_inc(index_ready, 1)
                dve.wait_ge(index_ready, 1)
                V.tensor_copy(topf[:], topi[:, :, 0:2]).then_inc(index_ready, 1)

            def route_weights():
                dve.wait_ge(exp_ready, 1)
                V.tensor_scalar(prb[:, :, 2:3], prb[:, :, 1:2], 1.0, None, ALU.add).then_inc(weight_part, 1)
                dve.wait_ge(weight_part, 1)
                V.reciprocal(prb[:, :, 2:3], prb[:, :, 2:3]).then_inc(weight_part, 1)
                dve.wait_ge(weight_part, 2)
                V.tensor_tensor(prb[:, :, 3:4], prb[:, :, 1:2], prb[:, :, 2:3], ALU.mult).then_inc(weight_part, 1)

            def route_gates():
                dve.wait_ge(iota_ready, 1)
                dve.wait_ge(index_ready, 2)
                shape = [P, TILES, EXPERTS]
                for i in range(2):
                    l = V.tensor_tensor(gate[:, i, :, :], iota[:, :].unsqueeze(1).broadcast_to(shape),
                                        topf[:, :, i:i + 1].broadcast_to(shape), ALU.is_equal)
                l.then_inc(gate_part, 1)
                dve.wait_ge(gate_part, 1)
                dve.wait_ge(weight_part, 3)
                for i in range(2):
                    l = V.tensor_tensor(gate[:, i, :, :], gate[:, i, :, :], prb[:, :, 2 + i:3 + i].broadcast_to(shape),
                                        ALU.mult)
                l.then_inc(gate_part, 1)
                dve.wait_ge(gate_part, 2)
                V.tensor_tensor(gate[:, 0, :, :], gate[:, 0, :, :], gate[:, 1, :, :], ALU.add).then_inc(gate_ready, 1)

            def hidden(v, it=0):
                m = up_rows(v // 2)
                if v < 2 * SHARED_CHUNKS:
                    dve.wait_ge(act_sil, v + 1 + 4 * it)
                else:
                    dve.wait_ge(pool_gate, v - 2 * SHARED_CHUNKS + 1 + 4 * it)
                dve.wait_ge(pe_up, 2 * v + 2 + 8 * it)
                if v >= 2:
                    dve.wait_ge(act_h, v - 1 + 4 * it)
                    dve.wait_ge(dve_hl, v - 1 + 4 * it)
                V.tensor_tensor(hraw[0:m, v % 2, :], ps[0:m, 2 * (v % 2) + 1, 0:HALF], sil[0:m, v % 2, :],
                                ALU.mult).then_inc(dve_h, 1)

            def hidden_lo(v, it=0):
                m = up_rows(v // 2)
                dve.wait_ge(act_h, v + 1 + 4 * it)
                V.tensor_tensor(hh[1][0:m, v % 2, :], hraw[0:m, v % 2, :], hh[0][0:m, v % 2, :].bitcast(F32),
                                ALU.subtract).then_inc(dve_hl, 1)

            def ffn_step(v, it=0):
                if v % 2 == 1 and v // 2 + 2 < CHUNKS:
                    split12_hi(v // 2 + 2, it)
                hidden(v, it)
                if v % 2 == 1 and v // 2 + 1 < CHUNKS:
                    split3_hi(v // 2 + 1, it)
                hidden_lo(v, it)
                if v % 2 == 1 and v // 2 + 1 < CHUNKS:
                    split3_lo(v // 2 + 1, it)

            ffn_step(0)
            ffn_step(1)
            route_top()
            ffn_step(2)
            route_weights()
            route_gates()
            split12_hi(3)
            hidden(3)
            split3_hi(2)
            hidden_lo(3)
            hidden(4)
            split3_lo(2)
            dve.wait_ge(pe_gt, 1)
            V.tensor_copy(gateT[:, 0:384], ps[0:EXPERTS, 0, 0:384])
            V.tensor_copy(gateT[:, 384:TOK], ps[0:EXPERTS, 1, 0:192]).then_inc(gt_ready, 1)
            hidden_lo(4)
            for v in range(5, 2 * SHARED_CHUNKS):
                ffn_step(v)
            with dve.Fori(0, 10) as i:
                for r in range(4):
                    ffn_step(2 * SHARED_CHUNKS + r, i)
            for v in range(52, 56):
                ffn_step(v)
            dve.wait_ge(pe_dn, 2 * CHUNKS - 1)
            for k in range(DC):
                V.tensor_copy(yT[:, k, 0:HALF], ps[:, 4 + k, 0:HALF]).then_inc(y_first, 1)
            dve.wait_ge(pe_dn, 2 * CHUNKS)
            V.tensor_copy(yT[:, 1, HALF:TOK], ps[:, 7, 0:HALF]).then_inc(y_second, 1)

            def y_add(t):
                n = TROWS[t]
                dve.wait_ge(pe_yt, t + 1)
                V.tensor_tensor(h[0:n, t, :], ps[0:n, t % 4, 0:D], h[0:n, t, :], ALU.add).then_inc(y_tok, 1)

            def y_stats(t):
                dve.wait_ge(y_tok, t + 1)
                V.bn_stats(bns[0:TROWS[t], t, 0, :], h[0:TROWS[t], t, :]).then_inc(stat4, 1)

            def y_mean(t):
                dve.wait_ge(stat4, 2 * t + 1)
                V.bn_aggr(mv[0:TROWS[t], t, :], bns[0:TROWS[t], t, 0, :]).then_inc(stat4, 1)

            def y_norm(t):
                n = TROWS[t]
                dve.wait_ge(rstd4, t + 1)
                V.tensor_scalar(h[0:n, t, :], h[0:n, t, :], mv[0:n, t, 0:1], rstd[0:n, t:t + 1],
                                ALU.subtract, ALU.mult).then_inc(y_done, 1)

            for t in range(TILES + 3):
                if t < TILES:
                    y_add(t)
                if 0 <= t - 2 < TILES:
                    y_mean(t - 2)
                if 0 <= t - 1 < TILES:
                    y_stats(t - 1)
                if 0 <= t - 3 < TILES:
                    y_norm(t - 3)

        @block.gpsimd
        def _(pool):
            G = nc.gpsimd
            steps = [0]

            def lo(o, i, hi, done):
                return G.tensor_tensor(o, i, hi.bitcast(F32), ALU.subtract).then_inc(done, 1)

            def inv_std(t, done, start, ready):
                pool.wait_ge(done, start + 2 * t + 2)
                n = TROWS[t]
                G.tensor_scalar(mv[0:n, t, 1:2], mv[0:n, t, 1:2], EPS, 1.0, ALU.add, ALU.mult).then_inc(eps_added, 1)
                steps[0] += 1
                pool.wait_ge(eps_added, steps[0])
                G.tensor_tensor(rstd[0:n, t:t + 1], mv[0:n, t, 1:2], mhalf[0:n, 0:1], ALU.pow).then_inc(ready, 1)

            G.iota(iota[:], pattern=[[1, EXPERTS]], base=0, channel_multiplier=0,
                   allow_small_or_imprecise_dtypes=True).then_inc(iota_ready, 1)
            def neg_mean_over_std(t):
                n = TROWS[t]
                inv_std(t, stat1, 0, rstd1)
                G.tensor_scalar(nmr[0:n, t:t + 1], mv[0:n, t, 0:1], -1.0, 1.0, ALU.mult, ALU.mult).then_inc(neg_mean, 1)
                pool.wait_ge(neg_mean, t + 1)
                pool.wait_ge(rstd1, t + 1)
                G.tensor_tensor(nmr[0:n, t:t + 1], nmr[0:n, t:t + 1], rstd[0:n, t:t + 1], ALU.mult).then_inc(nmr_ready, 1)

            pool.wait_ge(mem_ready, 1)
            for t in range(4):
                neg_mean_over_std(t)
            inv_std(0, stat2, 0, rstd2)
            neg_mean_over_std(4)
            pool.wait_ge(hi_qk, 1)
            G.tensor_tensor(qks[1][:, 0, 0:2 * D], qk_raw[:, 0, 0:2 * D], qks[0][:, 0, 0:2 * D].bitcast(F32), ALU.subtract)
            inv_std(1, stat2, 0, rstd2)
            lo(qks[1][:, 0, 2 * D:4 * D], qk_raw[:, 0, 2 * D:4 * D], qks[0][:, 0, 2 * D:4 * D], lo_qk)
            for t in range(2, TILES):
                inv_std(t, stat2, 0, rstd2)

            def weigh(u, it):
                pool.wait_ge(dve_r, u + 1 + 4 * it)
                G.tensor_tensor(prob[:], prob[:], rsum[:, :].unsqueeze(2).broadcast_to([GRP, 2 * GRPS, GRP]),
                                ALU.mult).then_inc(weighed, 1)
                pool.wait_ge(weighed, u + 1 + 4 * it)
                pool.wait_ge(pe_pt, u + 4 * it)
                G.tensor_tensor(attn[:], prob[:, 0:GRPS, :], prob[:, GRPS:2 * GRPS, :], ALU.add).then_inc(attn_ready, 1)

            def add_squares(u, it):
                pool.wait_ge(act_o, 2 * u + 2 + 8 * it)
                G.tensor_tensor(sqs[:, (u // 2) % 2, HALF * (u % 2):HALF * (u % 2) + HALF], sq[:, 0, :], sq[:, 1, :],
                                ALU.add).then_inc(pool_sq, 1)

            def step(s, it=0):
                if s % 2 == 0 and (s + 2) // 2 < HEADS:
                    hd = (s + 2) // 2
                    pool.wait_ge(hi_qk, hd + 1 + 2 * it)
                    lo(qks[1][:, hd % 2, :], qk_raw[:, hd % 2, :], qks[0][:, hd % 2, :], lo_qk)
                if s % 2 == 1 and 0 <= s - 1 < UNITS:
                    hd = (s - 1) // 2
                    pool.wait_ge(hi_v, hd + 1 + 2 * it)
                    lo(vs[1][:, hd % 2, :], v_raw[:, hd % 2, :], vs[0][:, hd % 2, :], lo_v)
                    pool.wait_ge(hi_o, hd + 1 + 2 * it)
                    lo(os_[1][:, hd % 2, :], o_raw[:, hd % 2, :], os_[0][:, hd % 2, :], lo_o)
                if s % 2 == 1 and s >= 3:
                    hd = (s - 3) // 2
                    pool.wait_ge(dve_stat, hd + 1 + 2 * it)
                    if hd >= 1:
                        pool.wait_ge(dve_f, 5 * hd + 10 * it)
                    G.tensor_tensor(rinv[:], ms[:], mhalf[:], ALU.pow).then_inc(pool_rinv, 1)
                if 0 <= s < UNITS:
                    if s >= 1:
                        weigh(s, it)
                if 1 <= s <= UNITS:
                    add_squares(s - 1, it)

            for s in range(0, 4):
                step(s)
            with pool.Fori(0, 2) as i:
                for r in range(4):
                    step(4 + r, i)
            def split12_lo(c, it=0):
                m = up_rows(c)
                pool.wait_ge(hi_12, c + 1 + 2 * it)
                lo(w12s[1][:, c % 2, :, :, 0:m], r12[:, c % 2, :, :, 0:m], w12s[0][:, c % 2, :, :, 0:m], lo_12)

            step(12)
            step(13)
            split12_lo(0)
            step(14)
            pool.wait_ge(hi_v, HEADS)
            lo(vs[1][:, 1, :], v_raw[:, 1, :], vs[0][:, 1, :], lo_v)
            pool.wait_ge(dve_stat, 7)
            pool.wait_ge(dve_f, 30)
            G.tensor_tensor(rinv[:], ms[:], mhalf[:], ALU.pow).then_inc(pool_rinv, 1)
            weigh(15, 0)
            pool.wait_ge(hi_o, HEADS)
            lo(os_[1][:, 1, :], o_raw[:, 1, :], os_[0][:, 1, :], lo_o)
            add_squares(14, 0)
            pool.wait_ge(dve_stat, 8)
            pool.wait_ge(dve_f, 32)
            G.tensor_tensor(rinv[:, 0:2], ms[:, 0:2], mhalf[:, 0:2], ALU.pow).then_inc(pool_rinv, 1)
            inv_std(0, stat3, 0, rstd3)
            inv_std(1, stat3, 0, rstd3)
            add_squares(15, 0)
            pool.wait_ge(dve_stat, 9)
            pool.wait_ge(dve_f, 35)
            G.tensor_tensor(rinv[:, 2:5], ms[:, 2:5], mhalf[:, 2:5], ALU.pow).then_inc(pool_rinv, 1)
            for t in range(2, TILES):
                inv_std(t, stat3, 0, rstd3)
            split12_lo(1)

            def ffn_step(v, it=0):
                if v >= 2 * SHARED_CHUNKS:
                    c = v // 2
                    pool.wait_ge(act_sil, v + 1 + 4 * it)
                    if v % 2 == 0:
                        g = c - SHARED_CHUNKS
                        gate_loads(g, it)
                    cols = slice(HALF * (v % 2), HALF * (v % 2) + HALF)
                    G.tensor_tensor(sil[:, v % 2, :], sil[:, v % 2, :], gates[:, (c - SHARED_CHUNKS) % 4, cols],
                                    ALU.mult).then_inc(pool_gate, 1)
                if v % 2 == 1 and v // 2 + 2 < CHUNKS:
                    split12_lo(v // 2 + 2, it)

            def gate_loads(g, it):
                pool.wait_ge(ld_g[g % 4], 16 * (g // 4 + 1 + it))

            ffn_step(0)
            ffn_step(1)
            pool.wait_ge(diff_ready, 1)
            G.tensor_tensor(prb[:, :, 1:2].rearrange("p t a -> p (t a)"), euler[:], prb[:, :, 0:1].rearrange("p t a -> p (t a)"), ALU.pow).then_inc(exp_ready, 1)
            for v in range(2, 2 * SHARED_CHUNKS):
                ffn_step(v)

            def ffn_step8(v, i):
                c = v // 2
                cols = slice(HALF * (v % 2), HALF * (v % 2) + HALF)
                pool.wait_ge(act_sil, v + 1 + 8 * i)
                if v % 2 == 0:
                    gate_loads(c - SHARED_CHUNKS, i)
                G.tensor_tensor(sil[:, v % 2, :], sil[:, v % 2, :], gates[:, (c - SHARED_CHUNKS) % 4, cols],
                                ALU.mult).then_inc(pool_gate, 1)
                if v % 2 == 1:
                    split12_lo(c + 2, 2 * i)

            with pool.Fori(0, 5) as i:
                for r in range(8):
                    ffn_step8(2 * SHARED_CHUNKS + r, i)
            for v in range(52, 56):
                ffn_step(v)
            for t in range(TILES):
                inv_std(t, stat4, 0, rstd4)


def kernel(**inputs):
    import numpy as np
    import concourse.bacc as bacc
    from concourse.bass_utils import run_bass_kernel_spmd as run

    f = {k: np.asarray(v) for k, v in inputs.items()}
    c = np.ascontiguousarray
    a = {}
    a["x"] = c(f["x"].reshape(16, 3, 6, 16, 6, 16).transpose(0, 2, 4, 1, 3, 5).reshape(TOK, PATCH))
    a["tokw"] = c(f["L0_tok_W"].T.reshape(KC, P, D).transpose(1, 0, 2))
    a["consts"] = c(np.concatenate([
        f["L0_tok_ln1_w"].reshape(KC, P).T, f["L0_attn_rms_scale"].reshape(2, P).T,
        f["L0_attn_lambda_q1"].T, f["L0_attn_lambda_k1"].T, f["L0_attn_lambda_q2"].T, f["L0_attn_lambda_k2"].T], axis=1))
    omega = np.arange(D // 4, dtype=np.float32) / np.float32(D // 4 - 1)
    omega = (np.float32(1.0) / np.float32(10000.0) ** omega).astype(np.float32)
    yy, xx = np.meshgrid(np.arange(6, dtype=np.float32), np.arange(6, dtype=np.float32), indexing="ij")
    yo, xo = yy.reshape(-1)[:, None] * omega[None, :], xx.reshape(-1)[:, None] * omega[None, :]
    a["pe_tab"] = c(np.tile(np.concatenate([np.sin(xo), np.cos(xo), np.sin(yo), np.cos(yo)], axis=1), (IMAGES, 1)).astype(np.float32))
    a["g2"] = c(f["L0_tok_ln2_w"].reshape(1, D))

    def head_in(w):
        return w.reshape(HEADS, D, DC, P).transpose(0, 3, 2, 1).reshape(HEADS, P, DC * D)

    a["wqk"] = c(np.concatenate([head_in(f["L0_attn_Wq"]), head_in(f["L0_attn_Wk"])], axis=2))
    a["wv"] = c(head_in(f["L0_attn_Wv"]))
    a["wo"] = c(f["L0_attn_Wo"].T.reshape(HEADS, DC, P, D).transpose(0, 2, 1, 3).reshape(HEADS, P, DC * D))
    a["ident"] = np.eye(P, dtype=np.float32)
    image = np.arange(GRP) // IMG_TOK
    masks = np.where(image[:, None] == image[None, :], 0.0, -1e30).astype(np.float32)
    a["masks"] = masks
    a["wg"] = c(f["L0_ffn_Wg"].reshape(DC, P, EXPERTS).transpose(1, 0, 2))
    r1 = np.concatenate([f["L0_ffn_Ws1"].T, f["L0_ffn_W1"].transpose(0, 2, 1).reshape(-1, D)])
    r2 = np.concatenate([f["L0_ffn_Ws2"].T, f["L0_ffn_W2"].transpose(0, 2, 1).reshape(-1, D)])
    r3 = np.concatenate([f["L0_ffn_Ws3"], f["L0_ffn_W3"].reshape(-1, D)])

    def chunked(r, m):
        return r.reshape(-1, m, DC, P).transpose(0, 3, 2, 1)

    a["s12"] = c(np.stack([chunked(r1[:SHARED0], SHARED0)[0], chunked(r2[:SHARED0], SHARED0)[0]], axis=1))
    a["s3"] = c(r3[:SHARED0])
    a["w12"] = c(np.stack([chunked(r1[SHARED0:], P), chunked(r2[SHARED0:], P)], axis=2).reshape(CHUNKS - 1, P, 4 * P))
    a["w3"] = c(r3[SHARED0:].reshape(CHUNKS - 1, P, D))

    nc = bacc.Bacc("TRN2", target_bir_lowering=False, num_devices=1)
    order = ["x", "tokw", "consts", "pe_tab", "g2", "wqk", "wv", "wo", "ident", "masks", "wg", "s12", "s3", "w12", "w3"]
    args = [nc.dram_tensor(f"in_{n}", a[n].shape, F32, kind="ExternalInput").ap() for n in order]
    out = nc.dram_tensor("out", (TOK, D), F32, kind="ExternalOutput").ap()
    build(nc, *args, out)
    r = run(nc, [{f"in_{n}": a[n] for n in order}], core_ids=[0])
    return r.results[0]["out"].reshape(IMAGES, IMG_TOK, D)
```
